# Optimizing a Trainium2 kernel written in Bass

```python
import numpy as np
import jax
import jax.numpy as jnp

def _softmax(x, axis=-1):
    return jax.nn.softmax(x, axis=axis)

def _gelu(x):
    return jax.nn.gelu(x, approximate=True)

def _silu(x):
    return jax.nn.silu(x)

def _sigmoid(x):
    return jax.nn.sigmoid(x)

def _layernorm(x, axis=-1, eps=1e-05):
    m = jnp.mean(x, axis=axis, keepdims=True)
    v = jnp.var(x, axis=axis, keepdims=True)
    return (x - m) / jnp.sqrt(v + eps)

def _scatter_add(tgt, idx, src, axis=0):
    return tgt.at[idx].add(src)

def _segment_sum(src, seg, n):
    return jax.ops.segment_sum(src, seg, n)
kernel_name = 'mk_gnn_resnorm_d2_gnn_r32_96ece6'

def setup_inputs(seed: int=0):
    np.random.seed(seed)
    _w = jnp.asarray

    def _rec_inputs():
        import jax
        import jax.numpy as jnp
        _gk = jax.random.key(seed)
        x = -0.0003713 + 1 * jax.random.normal(jax.random.fold_in(_gk, 1), (3125, 256), jnp.float32)
        src = jax.random.randint(jax.random.fold_in(_gk, 2), (50000,), 0, 3125, jnp.int32)
        dst = jnp.minimum((3125 * jax.random.uniform(jax.random.fold_in(_gk, 3), (50000,)) ** 2.0).astype(jnp.int32), 99999)
        _o = jnp.argsort(dst, stable=True)
        src = src[_o]
        dst = dst[_o]
        edge_type_64 = jax.random.randint(jax.random.fold_in(_gk, 12), (50000,), 0, 64, jnp.int32)
        edge_weight = jax.random.uniform(jax.random.fold_in(_gk, 13), (50000,), jnp.float32, 0.0, 0.999998)
        return (x, src, dst, edge_type_64, edge_weight)
    x, src, dst, edge_type_64, edge_weight = _rec_inputs()

    def _L0_gnn_setup():
        import jax, jax.numpy as jnp
        import numpy as np
        N_NODES = 50000
        N_EDGES = 25000
        IN_DIM, HID_DIM, OUT_DIM, N_HEADS = (256, 256, 64, 4)
        key = jax.random.key(seed)
        ks = jax.random.split(key, 8)
        x = jax.random.normal(ks[0], (N_NODES, IN_DIM), dtype=jnp.float32)
        idx = jax.random.randint(ks[1], (2, N_EDGES), 0, N_NODES, dtype=jnp.int64)
        elem = jax.random.uniform(ks[2], (N_EDGES,), dtype=jnp.float32)
        W1 = jax.random.normal(ks[3], (N_HEADS, IN_DIM, HID_DIM), dtype=jnp.float32) * 0.05
        b1 = jnp.zeros((N_HEADS, HID_DIM), dtype=jnp.float32)
        W2 = jax.random.normal(ks[4], (N_HEADS, HID_DIM, OUT_DIM), dtype=jnp.float32) * 0.05
        b2 = jnp.zeros((N_HEADS, OUT_DIM), dtype=jnp.float32)
        attn_w = jax.random.normal(ks[5], (N_HEADS, 2 * OUT_DIM + 1, 1), dtype=jnp.float32) * 0.05
        attn_b = jnp.zeros((N_HEADS, 1), dtype=jnp.float32)
        return {'x': x, 'idx': idx, 'elem': elem, 'W1': W1, 'b1': b1, 'W2': W2, 'b2': b2, 'attn_w': attn_w, 'attn_b': attn_b}
    _L0_gnn_all = _L0_gnn_setup()
    _L0_gnn_in = {k: v for k, v in _L0_gnn_all.items() if k in ('W1', 'b1', 'W2', 'b2', 'attn_w', 'attn_b')}
    del _L0_gnn_all

    def _L1_gnn_setup():
        import jax, jax.numpy as jnp
        import numpy as np
        N_NODES = 50000
        N_EDGES = 15625
        IN_DIM = 256
        HID = 64
        HEADS = 4
        N_REL = 64
        key = jax.random.key(seed)
        ks = jax.random.split(key, 16)
        s = 0.02
        return {'node_features': jax.random.normal(ks[0], (N_NODES, IN_DIM), jnp.float32), 'edge_index': jax.random.randint(ks[1], (2, N_EDGES), 0, N_NODES, jnp.int32), 'edge_relations': jax.random.randint(ks[2], (N_EDGES,), 0, N_REL, jnp.int32), 'query_emb': jax.random.normal(ks[3], (IN_DIM,), jnp.float32), 'Wq': jax.random.normal(ks[4], (IN_DIM, HID * HEADS), jnp.float32) * s, 'bq': jnp.zeros((HID * HEADS,), jnp.float32), 'Wk': jax.random.normal(ks[5], (IN_DIM, HID * HEADS), jnp.float32) * s, 'bk': jnp.zeros((HID * HEADS,), jnp.float32), 'Wv': jax.random.normal(ks[6], (IN_DIM, HID * HEADS), jnp.float32) * s, 'bv': jnp.zeros((HID * HEADS,), jnp.float32), 'rel_w': jax.random.normal(ks[7], (N_REL, HID), jnp.float32) * s, 'Wo': jax.random.normal(ks[8], (HID * HEADS, IN_DIM), jnp.float32) * s, 'bo': jnp.zeros((IN_DIM,), jnp.float32), 'gamma': jnp.ones((IN_DIM,), jnp.float32), 'beta': jnp.zeros((IN_DIM,), jnp.float32)}
    _L1_gnn_all = _L1_gnn_setup()
    _L1_gnn_in = {k: v for k, v in _L1_gnn_all.items() if k in ('query_emb', 'Wq', 'bq', 'Wk', 'bk', 'Wv', 'bv', 'rel_w', 'Wo', 'bo', 'gamma', 'beta')}
    del _L1_gnn_all
    return {'x': x, 'src': src, 'dst': dst, 'edge_type_64': edge_type_64, 'edge_weight': edge_weight, 'L0_gnn_W1': _L0_gnn_in['W1'], 'L0_gnn_b1': _L0_gnn_in['b1'], 'L0_gnn_W2': _L0_gnn_in['W2'], 'L0_gnn_b2': _L0_gnn_in['b2'], 'L0_gnn_attn_w': _L0_gnn_in['attn_w'], 'L0_gnn_attn_b': _L0_gnn_in['attn_b'], 'L1_gnn_query_emb': _L1_gnn_in['query_emb'], 'L1_gnn_Wq': _L1_gnn_in['Wq'], 'L1_gnn_bq': _L1_gnn_in['bq'], 'L1_gnn_Wk': _L1_gnn_in['Wk'], 'L1_gnn_bk': _L1_gnn_in['bk'], 'L1_gnn_Wv': _L1_gnn_in['Wv'], 'L1_gnn_bv': _L1_gnn_in['bv'], 'L1_gnn_rel_w': _L1_gnn_in['rel_w'], 'L1_gnn_Wo': _L1_gnn_in['Wo'], 'L1_gnn_bo': _L1_gnn_in['bo'], 'L1_gnn_gamma': _L1_gnn_in['gamma'], 'L1_gnn_beta': _L1_gnn_in['beta']}

def reference(x, src, dst, edge_type_64, edge_weight, L0_gnn_W1, L0_gnn_b1, L0_gnn_W2, L0_gnn_b2, L0_gnn_attn_w, L0_gnn_attn_b, L1_gnn_query_emb, L1_gnn_Wq, L1_gnn_bq, L1_gnn_Wk, L1_gnn_bk, L1_gnn_Wv, L1_gnn_bv, L1_gnn_rel_w, L1_gnn_Wo, L1_gnn_bo, L1_gnn_gamma, L1_gnn_beta):
    import jax
    import jax.numpy as jnp

    def _L0_gnn_ref(x, idx, elem, W1, b1, W2, b2, attn_w, attn_b):
        import jax, jax.numpy as jnp
        import numpy as np
        N_NODES = 50000
        N_EDGES = 25000
        IN_DIM, HID_DIM, OUT_DIM, N_HEADS = (256, 256, 64, 4)
        n = x.shape[0]
        src, dst = (idx[0], idx[1])

        def head(W1h, b1h, W2h, b2h, awh, abh):
            feats = jnp.maximum(x @ W1h + b1h, 0.0) @ W2h + b2h
            f_src = feats[src]
            f_dst = feats[dst]
            x_cat = jnp.concatenate([f_src, f_dst, elem[:, None]], axis=1)
            score = (x_cat @ awh + abh)[:, 0]
            w = jnp.exp(score - jnp.max(score))
            pooled = jax.ops.segment_sum(w[:, None] * f_dst, src, num_segments=n)
            row_sum = jax.ops.segment_sum(w, src, num_segments=n)
            return pooled / row_sum[:, None]
        h = jax.vmap(head)(W1, b1, W2, b2, attn_w, attn_b)
        return jnp.transpose(h, (1, 0, 2)).reshape(n, -1)

    def _L1_gnn_ref(node_features, edge_index, edge_relations, query_emb, Wq, bq, Wk, bk, Wv, bv, rel_w, Wo, bo, gamma, beta):
        import jax, jax.numpy as jnp
        import numpy as np
        N_NODES = 50000
        N_EDGES = 15625
        IN_DIM = 256
        HID = 64
        HEADS = 4
        N_REL = 64
        N = node_features.shape[0]
        D = rel_w.shape[1]
        H = Wq.shape[1] // D
        enh = node_features + 0.1 * query_emb[None, :]
        Q = (enh @ Wq + bq).reshape(N, H, D)
        K = (enh @ Wk + bk).reshape(N, H, D)
        V = (enh @ Wv + bv).reshape(N, H, D)
        src, dst = (edge_index[0], edge_index[1])
        rel = rel_w[edge_relations]
        mod_k = K[src] + 0.2 * rel[:, None, :]
        scores = jnp.einsum('ehd,ehd->eh', Q[dst], mod_k) / D ** 0.5
        seg_max = jax.ops.segment_max(scores, dst, num_segments=N)
        ex = jnp.exp(scores - seg_max[dst])
        denom = jax.ops.segment_sum(ex, dst, num_segments=N)
        w = ex / denom[dst]
        agg = jax.ops.segment_sum(w[:, :, None] * V[src], dst, num_segments=N)
        deg = jax.ops.segment_sum(jnp.ones((src.shape[0],), jnp.float32), dst, num_segments=N)
        msgs = jnp.where(deg[:, None, None] > 0, agg, V)
        out = msgs.reshape(N, H * D) @ Wo + bo
        x = out + node_features
        mu = jnp.mean(x, axis=-1, keepdims=True)
        var = jnp.var(x, axis=-1, keepdims=True)
        return (x - mu) / jnp.sqrt(var + 1e-05) * gamma + beta
    edge_index = jnp.stack([src, dst])
    x = _layernorm(x + _L0_gnn_ref(x, edge_index, edge_weight, L0_gnn_W1, L0_gnn_b1, L0_gnn_W2, L0_gnn_b2, L0_gnn_attn_w, L0_gnn_attn_b), axis=-1)
    x = _layernorm(x + _L1_gnn_ref(x, edge_index, edge_type_64, L1_gnn_query_emb, L1_gnn_Wq, L1_gnn_bq, L1_gnn_Wk, L1_gnn_bk, L1_gnn_Wv, L1_gnn_bv, L1_gnn_rel_w, L1_gnn_Wo, L1_gnn_bo, L1_gnn_gamma, L1_gnn_beta), axis=-1)
    return x

_drawn_inputs = setup_inputs


def setup_inputs(seed=0):
    import zlib

    import numpy as np

    out = dict(_drawn_inputs(seed))
    spreads = {'L0_gnn_b1': (0.0, 0.1),
     'L0_gnn_b2': (0.0, 0.1),
     'L0_gnn_attn_b': (0.0, 2.0),
     'L1_gnn_bq': (0.0, 0.8),
     'L1_gnn_bk': (0.0, 2.0),
     'L1_gnn_bv': (0.0, 0.509),
     'L1_gnn_bo': (0.0, 0.1),
     'L1_gnn_gamma': (1.0, 0.2),
     'L1_gnn_beta': (0.0, 0.1)}
    factors = {'edge_weight': 8.0,
     'L0_gnn_attn_w': 3.65,
     'L1_gnn_query_emb': 8.0,
     'L1_gnn_Wq': 8.0,
     'L1_gnn_Wk': 8.0,
     'L1_gnn_Wv': 2.793,
     'L1_gnn_rel_w': 64.0}
    for name, (base, spread) in spreads.items():
        noise = np.random.default_rng([zlib.crc32(name.encode()), seed]).standard_normal(out[name].shape)
        drawn = base * np.exp(spread * noise) if base else spread * noise
        out[name] = jnp.asarray(drawn.astype(out[name].dtype))
    for name, factor in factors.items():
        out[name] = (out[name] * factor).astype(out[name].dtype)
    return out
```

```python
from contextlib import ExitStack

import concourse.bass as bass
from concourse import mybir

ALU = mybir.AluOpType
ACT = mybir.ActivationFunctionType
AX = mybir.AxisListType
F32 = mybir.dt.float32
BF16 = mybir.dt.bfloat16
I32 = mybir.dt.int32
U32 = mybir.dt.uint32
I16 = mybir.dt.int16

P = 128
N, E = 3125, 50000
D, HEADS, HD, RELS = 256, 4, 64, 64
HID = 256
NW = -(-N // P)
NPAD = NW * P
TAIL_NODES = N - (NW - 1) * P
EPP = -(-E // P)
EPAD = EPP * P
TAIL_EDGES = E - (P - 1) * EPP
TPG = 2
GE = TPG * P
NG = (E + NW * (GE - 1)) // GE
NT = NG * TPG
SL = 4
assert NG % SL == 0 and GE == 256
NROWS = NG * GE
TRASH = NROWS
SCRAP = TRASH + P
ROWW = 264
VROW = 260
FH = HD + 2
NO_NODE = 8000
BIG = 1.0e30
EPS = 1.0e-5
CH = 5
CW = NW // CH
LAYER0, LAYER1 = "layer 0", "layer 1"


def named(**things):
    return type("Named", (), things)


def rounds(eng, count, turn):
    turn(0)
    with eng.Fori(1, count) as r:
        turn(r)


def allocators(nc, ctx, stage):
    numbers = []

    def sb(name, shape, dt):
        return ctx.enter_context(nc.sbuf_tensor(f"{stage}_{name}", shape, dt))

    def psum(name, shape):
        return ctx.enter_context(nc.psum_tensor(f"{stage}_{name}", shape, F32))

    def sem(name):
        handle = ctx.enter_context(nc.semaphore(f"{stage}_{name}"))
        numbers.append(handle.num)
        return handle

    def sems(names):
        return named(**{n: sem(n) for n in names.split()})

    def slot_sems(names):
        return [[sem(f"{n}_{b}") for b in range(SL)] for n in names.split()]

    def clear():
        if numbers:
            nc.all_engine_barrier(sems_to_clear=range(min(numbers), max(numbers) + 1))

    ctx.callback(clear)
    return sb, psum, sems, slot_sems


def prepare(nc, i, t):
    with ExitStack() as ctx:
        sb, psum, sems, slot_sems = allocators(nc, ctx, "prepare")
        w1 = sb("w1", [P, 2, HEADS * HID], F32)
        w2 = sb("w2", [P, HEADS, 2, HD], F32)
        w2x = sb("w2x", [P, HEADS, 2, FH], F32)
        aw = sb("aw", [P, HEADS, 2 * HD + 1], F32)
        ab = sb("ab", [P, HEADS], F32)
        b1 = sb("b1", [P, HEADS * 2], F32)
        b2 = sb("b2", [P, HEADS, HD], F32)
        b2x = sb("b2x", [P, HEADS, FH], F32)
        junk = sb("junk", [P, HD], F32)
        dots = sb("dots", [P, HEADS, 3, 2], F32)
        x_now = sb("x_now", [P, CW, D], F32)
        x_t = sb("x_t", [P, 2, CW * P], F32)
        hid = sb("hid", [P, HEADS * 2, CW * P], F32)
        ftmp = sb("ftmp", [P, 2, HEADS * FH], F32)
        fres = sb("fres", [P, 2, HEADS * FH], F32)
        src_i = sb("src_i", [P, EPP], I32)
        dst_i = sb("dst_i", [P, EPP], I32)
        typ_i = sb("typ_i", [P, EPP], I32)
        wgt = sb("wgt", [P, EPP], F32)
        win_i = sb("win_i", [P, EPP], I32)
        low_i = sb("low_i", [P, EPP], I32)
        ones_e = sb("ones_e", [P, EPP], BF16)
        mask = sb("mask", [P, NW, EPP], BF16)
        rank = sb("rank", [P, NW, EPP], F32)
        win_no = sb("win_no", [P, NW], F32)
        win_end = sb("win_end", [P, NW], F32)
        cnt = sb("cnt", [P, 2 * NW], F32)
        tot = sb("tot", [P, 2 * NW], F32)
        below = sb("below", [P, P], F32)
        base = sb("base", [P, NW], F32)
        gi = sb("gi", [P, 2, NW], I32)
        grp = sb("grp", [P, 2, NW], F32)
        cum = sb("cum", [P, 2, NW], F32)
        fst = sb("fst", [P, 2, NW], F32)
        fill = sb("fill", [P, 2, NW], F32)
        no_fill = sb("no_fill", [P, 2, NW], F32)
        scrap = sb("scrap", [P, 2, NW], F32)
        off = sb("off", [P, NW + 1], F32)
        step = sb("step", [P, NW], F32)
        g_no = sb("g_no", [P, NG], F32)
        reach = mask[:, :, :].rearrange("p k j -> p (k j)")[:, 0:NG * NW].rearrange("p (g k) -> p g k", k=NW)
        reach_o = rank[:, :, :].rearrange("p k j -> p (k j)")[:, 0:NG * NW].rearrange("p (g k) -> p g k", k=NW)
        acc_f = rank[:, :, :].rearrange("p k j -> p (k j)")[:, NG * NW:NG * (NW + 4)].rearrange("p (a g) -> p a g", a=4)
        ones_w = sb("ones_w", [P, NW], F32)
        ps_x = [psum(f"ps_x{b}", [P, 512]) for b in range(2)]
        ps_h = [psum(f"ps_h{b}", [P, 512]) for b in range(2)]
        ps_f = [psum(f"ps_f{b}", [P, 512]) for b in range(2)]
        ps_c = psum("ps_c", [P, 512])
        s = sems("pad_set const_set ident_set tri_set x_in w_in e_in prep w2x_set x_turned xt_copied hid_made "
                       "hid_kept f_made f_copied f_hi f_res f_mid f_lo x_staged d counted totals")

        with nc.Block() as block:
            @block.sync
            def _(sp):
                sp.dma_start(t.x[:, 0:NW - 1, :], i.x[0:(NW - 1) * P, :].rearrange("(w p) c -> p w c", p=P)).then_inc(s.x_in, 16)
                sp.dma_start(w1[:, :, :].rearrange("p k (h m) -> p k h m", h=HEADS)[:, 0, :, :],
                             i.L0_gnn_W1[:, 0:P, :].rearrange("h p m -> p h m")).then_inc(s.w_in, 16)
                sp.dma_start(w1[:, :, :].rearrange("p k (h m) -> p k h m", h=HEADS)[:, 1, :, :],
                             i.L0_gnn_W1[:, P:2 * P, :].rearrange("h p m -> p h m")).then_inc(s.w_in, 16)
                sp.dma_start(w2[:, :, :, :], i.L0_gnn_W2.rearrange("h (k p) m -> p h k m", p=P)).then_inc(s.w_in, 16)
                sp.dma_start(aw[:, :, :], i.L0_gnn_attn_w.rearrange("h m o -> (h m o)").partition_broadcast(P)
                             .rearrange("p (h m) -> p h m", h=HEADS)).then_inc(s.w_in, 16)
                sp.dma_start(ab[:, :], i.L0_gnn_attn_b.rearrange("h o -> (h o)").partition_broadcast(P)).then_inc(s.w_in, 16)
                sp.dma_start(b1[:, :].rearrange("p (h k) -> p h k", k=2), i.L0_gnn_b1.rearrange("h (k p) -> p h k", p=P),
                             allow_slow_non_contiguous=True).then_inc(s.w_in, 16)
                sp.dma_start(b2[:, :, :], i.L0_gnn_b2.rearrange("h m -> (h m)").partition_broadcast(P)
                             .rearrange("p (h m) -> p h m", h=HEADS)).then_inc(s.w_in, 16)
                sp.wait_ge(s.pad_set, 5)
                sp.dma_start(t.x[0:TAIL_NODES, NW - 1, :], i.x[(NW - 1) * P:N, :]).then_inc(s.x_in, 16)
                for dst_tile, src in ((src_i, i.src), (dst_i, i.dst), (typ_i, i.edge_type_64), (wgt, i.edge_weight)):
                    sp.dma_start(dst_tile[0:P - 1, :], src[0:(P - 1) * EPP].rearrange("(p j) -> p j", p=P - 1)).then_inc(s.e_in, 16)
                    sp.dma_start(dst_tile[P - 1:P, 0:TAIL_EDGES], src[(P - 1) * EPP:E].rearrange("(a j) -> a j", a=1)).then_inc(s.e_in, 16)

            @block.gpsimd
            def _(pool):
                pool.memset(t.x[:, NW - 1, :], 0.0).then_inc(s.pad_set, 1)
                pool.memset(src_i[:, TAIL_EDGES:EPP], NO_NODE).then_inc(s.pad_set, 1)
                pool.memset(dst_i[:, TAIL_EDGES:EPP], NO_NODE).then_inc(s.pad_set, 1)
                pool.memset(typ_i[:, TAIL_EDGES:EPP], 0).then_inc(s.pad_set, 1)
                pool.memset(wgt[:, TAIL_EDGES:EPP], 0.0).then_inc(s.pad_set, 1)
                pool.memset(t.ident[:, :], 0.0).then_inc(s.ident_set, 1)
                pool.memset(below[:, :], 1.0).then_inc(s.tri_set, 1)
                pool.wait_ge(s.ident_set, 1)
                pool.affine_select(out=t.ident[:, :], in_=t.ident[:, :], compare_op=ALU.not_equal, fill=1.0,
                                   base=0, pattern=[[-1, P]], channel_multiplier=1).then_inc(s.ident_set, 1)
                pool.wait_ge(s.tri_set, 1)
                pool.affine_select(out=below[:, :], in_=below[:, :], compare_op=ALU.is_gt, fill=0.0,
                                   base=0, pattern=[[1, P]], channel_multiplier=-1).then_inc(s.tri_set, 1)
                pool.iota(t.lane[:, :], pattern=[[0, 1]], base=0, channel_multiplier=1,
                          allow_small_or_imprecise_dtypes=True).then_inc(s.const_set, 1)
                pool.iota(t.trash[:, :], pattern=[[0, 1]], base=TRASH, channel_multiplier=1,
                          allow_small_or_imprecise_dtypes=True).then_inc(s.const_set, 1)
                pool.iota(win_no[:, :], pattern=[[1, NW]], base=0, channel_multiplier=0,
                          allow_small_or_imprecise_dtypes=True).then_inc(s.const_set, 1)
                pool.iota(win_end[:, :], pattern=[[P, NW]], base=P, channel_multiplier=0,
                          allow_small_or_imprecise_dtypes=True).then_inc(s.const_set, 1)
                pool.iota(scrap[:, :, :], pattern=[[GE, 2 * NW]], base=SCRAP, channel_multiplier=0,
                          allow_small_or_imprecise_dtypes=True).then_inc(s.const_set, 1)
                pool.iota(g_no[:, :], pattern=[[1, NG]], base=0, channel_multiplier=0,
                          allow_small_or_imprecise_dtypes=True).then_inc(s.const_set, 1)
                pool.iota(t.cols[:, :], pattern=[[1, P]], base=0, channel_multiplier=0,
                          allow_small_or_imprecise_dtypes=True).then_inc(s.const_set, 1)
                pool.iota(t.win_of_col[:, :], pattern=[[1, NW], [0, HEADS]], base=0, channel_multiplier=0,
                          allow_small_or_imprecise_dtypes=True).then_inc(s.const_set, 1)
                pool.memset(t.ones[:, :], 1.0).then_inc(s.const_set, 1)
                pool.memset(ones_e[:, :], 1.0).then_inc(s.const_set, 1)
                pool.memset(ones_w[:, :], 1.0).then_inc(s.const_set, 1)
                pool.wait_ge(s.x_in, 32)
                pool.tensor_copy(x_now[:, :, :], t.x[:, 0:CW, :]).then_inc(s.x_staged, 1)

                def split_rest(c):
                    for w in range(CW):
                        n = c * CW + w
                        b = w % 2
                        hi, mid, lo = (t.table3[:, bass.ds(n, 1), k * ROWW:k * ROWW + HEADS * FH].rearrange("p a f -> p (a f)") for k in range(3))
                        pool.wait_ge(s.f_hi, n + 1)
                        nc.gpsimd.tensor_tensor(fres[:, b, :], ftmp[:, b, :], hi, ALU.subtract).then_inc(s.f_res, 1)
                        pool.wait_ge(s.f_mid, n + 1)
                        nc.gpsimd.tensor_tensor(lo, fres[:, b, :], mid, ALU.subtract).then_inc(s.f_lo, 1)

                def turn(c):
                    pool.wait_ge(s.x_turned, (c + 1) * CW)
                    pool.tensor_copy(x_now[:, :, :], t.x[:, bass.ds(c * CW + CW, CW), :]).then_inc(s.x_staged, 1)
                    split_rest(c)
                rounds(pool, CH - 1, turn)
                split_rest(CH - 1)

            @block.tensor
            def _(pe):
                pe.wait_ge(s.ident_set, 2)
                pe.wait_ge(s.w_in, 16 * 7)
                pe.wait_ge(s.w2x_set, 1)
                pe.wait_ge(s.const_set, 11)
                def turn(c):
                    pe.wait_ge(s.x_staged, c + 1)
                    for w in range(CW):
                        k = c * CW + w
                        xw = x_now[:, w, :]
                        if w < 2:
                            pe.wait_ge(s.xt_copied, c * CW)
                        else:
                            pe.wait_ge(s.xt_copied, k - 1)
                        for half in range(2):
                            last = nc.tensor.transpose(ps_x[w % 2][:, half * P:(half + 1) * P], xw[:, half * P:(half + 1) * P], t.ident[:, :])
                        last.then_inc(s.x_turned, 1)
                    pe.wait_ge(s.xt_copied, (c + 1) * CW)
                    for m in range(HEADS * 2):
                        for nh in range(2):
                            k = m * 2 + nh
                            b = k % 2
                            if k < 2:
                                pe.wait_ge(s.hid_kept, c * HEADS * 4)
                            else:
                                pe.wait_ge(s.hid_kept, c * HEADS * 4 + k - 1)
                            half = CW * P // 2
                            for kk in range(2):
                                last = nc.tensor.matmul(ps_h[b][:, 0:half], w1[:, kk, m * P:(m + 1) * P],
                                                        x_t[:, kk, nh * half:(nh + 1) * half], start=kk == 0, stop=kk == 1)
                            last.then_inc(s.hid_made, 1)
                    pe.wait_ge(s.hid_kept, (c + 1) * HEADS * 4)
                    for w in range(CW):
                        if w < 2:
                            pe.wait_ge(s.f_hi, c * CW)
                        else:
                            pe.wait_ge(s.f_hi, c * CW + w - 1)
                        for h in range(HEADS):
                            out = ps_f[w % 2][:, h * FH:(h + 1) * FH]
                            for kk in range(2):
                                nc.tensor.matmul(out, hid[:, 2 * h + kk, w * P:(w + 1) * P], w2x[:, h, kk, :], start=kk == 0, stop=False)
                            last = nc.tensor.matmul(out, t.ones[0:1, 0:P], b2x[0:1, h, :], start=False, stop=True)
                        last.then_inc(s.f_made, 1)
                rounds(pe, CH, turn)
                pe.wait_ge(s.counted, 1)
                pe.wait_ge(s.tri_set, 2)
                nc.tensor.matmul(ps_c[:, 0:NW], below[:, :], cnt[:, 0:NW], start=True, stop=True)
                nc.tensor.matmul(ps_c[:, 64:64 + 2 * NW], t.ones[:, 0:P], cnt[:, :], start=True, stop=True).then_inc(s.totals, 1)

            @block.scalar
            def _(act):
                act.wait_ge(s.w_in, 16 * 7)
                def turn(c):
                    for w in range(CW):
                        act.wait_ge(s.x_turned, c * CW + w + 1)
                        nc.scalar.activation(x_t[:, :, w * P:(w + 1) * P], ps_x[w % 2][:, 0:2 * P].rearrange("p (k n) -> p k n", k=2),
                                             ACT.Copy).then_inc(s.xt_copied, 1)
                    for m in range(HEADS * 2):
                        for nh in range(2):
                            k = m * 2 + nh
                            half = CW * P // 2
                            act.wait_ge(s.hid_made, c * HEADS * 4 + k + 1)
                            nc.scalar.activation(hid[:, m, nh * half:(nh + 1) * half], ps_h[k % 2][:, 0:half], ACT.Relu,
                                                 bias=b1[:, m:m + 1]).then_inc(s.hid_kept, 1)
                    for w in range(CW):
                        n = c * CW + w
                        b = w % 2
                        hi = t.table3[:, bass.ds(n, 1), 0:HEADS * FH].rearrange("p a f -> p (a f)")
                        mid = t.table3[:, bass.ds(n, 1), ROWW:ROWW + HEADS * FH].rearrange("p a f -> p (a f)")
                        act.wait_ge(s.f_made, n + 1)
                        if w < 2:
                            act.wait_ge(s.f_lo, c * CW)
                        else:
                            act.wait_ge(s.f_lo, n - 1)
                        nc.scalar.activation(ftmp[:, b, :], ps_f[b][:, 0:HEADS * FH], ACT.Copy).then_inc(s.f_copied, 1)
                        nc.scalar.activation(hi, ps_f[b][:, 0:HEADS * FH], ACT.Copy).then_inc(s.f_hi, 1)
                        act.wait_ge(s.f_res, n + 1)
                        nc.scalar.activation(mid, fres[:, b, :], ACT.Copy).then_inc(s.f_mid, 1)
                rounds(act, CH, turn)

            @block.vector
            def _(dve):
                done = [0]

                def step_done(ins):
                    done[0] += 1
                    ins.then_inc(s.d, 1)
                    dve.wait_ge(s.d, done[0])

                dve.wait_ge(s.w_in, 16 * 7)
                for h in range(HEADS):
                    for part in range(2):
                        a = aw[:, h, part * HD:(part + 1) * HD]
                        for q in range(3):
                            m = w2[:, h, q, :] if q < 2 else b2[:, h, :]
                            step_done(nc.vector.tensor_tensor_reduce(junk[:, :], m, a, 1.0, 0.0, ALU.mult, ALU.add,
                                                                     dots[:, h, q, part:part + 1]))
                nc.vector.tensor_copy(w2x[:, :, :, 0:HD], w2[:, :, :, :]).then_inc(s.prep, 1)
                nc.vector.tensor_copy(w2x[:, :, :, HD:FH], dots[:, :, 0:2, :]).then_inc(s.prep, 1)
                nc.vector.tensor_copy(b2x[:, :, 0:HD], b2[:, :, :]).then_inc(s.prep, 1)
                step_done(nc.vector.tensor_copy(b2x[:, :, HD:HD + 1], dots[:, :, 2, 0:1]))
                nc.vector.tensor_copy(t.elem_w[:, :], aw[:, :, 2 * HD]).then_inc(s.prep, 1)
                nc.vector.tensor_tensor(b2x[:, :, HD + 1], dots[:, :, 2, 1], ab[:, :], ALU.add).then_inc(s.prep, 1)
                dve.wait_ge(s.prep, 5)
                dve.sem_inc(s.w2x_set, 1)

                dve.wait_ge(s.e_in, 16 * 8)
                dve.wait_ge(s.const_set, 11)
                nc.vector.tensor_scalar(win_i[:, :], src_i[:, :], 7, None, ALU.arith_shift_right).then_inc(s.prep, 1)
                step_done(nc.vector.tensor_scalar(low_i[:, :], src_i[:, :], P - 1, None, ALU.bitwise_and))
                dve.wait_ge(s.prep, 6)
                for c, v in enumerate((dst_i, src_i, low_i, win_i, wgt)):
                    step_done(nc.vector.tensor_copy(t.rec[:, :, c], v[:, :]))
                step_done(nc.vector.memset(t.rec[:, :, 6:8], 0.0))
                for c, v in enumerate((low_i, dst_i, typ_i)):
                    step_done(nc.vector.tensor_copy(t.row16[:, c, :], v[:, :]))

                with dve.Fori(0, NW) as k:
                    row = mask[:, bass.ds(k, 1), :].rearrange("p a j -> p (a j)")
                    nc.vector.tensor_scalar(row, t.rec[:, :, 0], win_end[:, bass.ds(k, 1)], None, ALU.is_lt).then_inc(s.d, 1)
                done[0] += NW
                dve.wait_ge(s.d, done[0])
                step_done(nc.vector.tensor_reduce(cnt[:, NW:2 * NW], mask[:, :, :], AX.X, ALU.add))
                before = done[0]
                with dve.Fori(0, NW) as k:
                    row = mask[:, bass.ds(k, 1), :].rearrange("p a j -> p (a j)")
                    rnk = rank[:, bass.ds(k, 1), :].rearrange("p a j -> p (a j)")
                    nc.vector.tensor_scalar(row, t.rec[:, :, 3], win_no[:, bass.ds(k, 1)], None, ALU.is_equal).then_inc(s.d, 1)
                    dve.wait_ge(s.d, 2 * k + before + 1)
                    nc.vector.tensor_tensor_scan(rnk, ones_e[:, :], row, 0.0, ALU.mult, ALU.add).then_inc(s.d, 1)
                done[0] += 2 * NW
                dve.wait_ge(s.d, done[0])
                nc.vector.tensor_copy(cnt[:, 0:NW], rank[:, :, EPP - 1]).then_inc(s.counted, 1)
                dve.wait_ge(s.totals, 1)
                step_done(nc.vector.tensor_copy(tot[:, 0:NW], ps_c[:, 64:64 + NW]))
                step_done(nc.vector.tensor_copy(tot[:, NW:2 * NW], ps_c[:, 64 + NW:64 + 2 * NW]))
                step_done(nc.vector.tensor_copy(off[:, 1:NW + 1], tot[:, NW:2 * NW]))
                step_done(nc.vector.memset(off[:, 0:1], 0.0))
                step_done(nc.vector.tensor_tensor(tot[:, NW:2 * NW], off[:, 1:NW + 1], off[:, 0:NW], ALU.subtract))
                step_done(nc.vector.tensor_scalar(gi[:, :, :].rearrange("p a k -> p (a k)"), tot[:, :], float(GE - 1), None, ALU.add))
                step_done(nc.vector.tensor_scalar(gi[:, :, :], gi[:, :, :], 8, None, ALU.arith_shift_right))
                step_done(nc.vector.tensor_copy(grp[:, :, :], gi[:, :, :]))
                for a in range(2):
                    step_done(nc.vector.tensor_tensor_scan(cum[:, a, :], ones_w[:, :], grp[:, a, :], 0.0, ALU.mult, ALU.add))
                step_done(nc.vector.tensor_tensor(fst[:, :, :], cum[:, :, :], grp[:, :, :], ALU.subtract))
                step_done(nc.vector.tensor_scalar(base[:, :], fst[:, 0, :], float(GE), -1.0, ALU.mult, ALU.add))
                step_done(nc.vector.tensor_tensor(base[:, :], base[:, :], ps_c[:, 0:NW], ALU.add))
                step_done(nc.vector.tensor_scalar(fill[:, 0, :], cum[:, 0, :], -1.0, None, ALU.add))
                step_done(nc.vector.tensor_scalar(fill[:, 1, :], win_no[:, :], cum[:, 0, NW - 1:NW], None, ALU.add))
                step_done(nc.vector.tensor_scalar(no_fill[:, 0, :], grp[:, 0, :], 0.0, None, ALU.is_equal))
                step_done(nc.vector.tensor_scalar(no_fill[:, 1, :], fill[:, 1, :], float(NG), None, ALU.is_ge))
                step_done(nc.vector.tensor_scalar(fill[:, :, :], fill[:, :, :], float(GE), None, ALU.mult))
                step_done(nc.vector.tensor_tensor(scrap[:, :, :], scrap[:, :, :], fill[:, :, :], ALU.subtract))
                step_done(nc.vector.tensor_tensor(scrap[:, :, :], scrap[:, :, :], no_fill[:, :, :], ALU.mult))
                step_done(nc.vector.tensor_tensor(t.fill_at[:, :], fill[:, :, :].rearrange("p a k -> p (a k)"),
                                                  scrap[:, :, :].rearrange("p a k -> p (a k)"), ALU.add))
                before = done[0]
                with dve.Fori(0, NW) as k:
                    row = mask[:, bass.ds(k, 1), :].rearrange("p a j -> p (a j)")
                    rnk = rank[:, bass.ds(k, 1), :].rearrange("p a j -> p (a j)")
                    nc.vector.scalar_tensor_tensor(rnk, rnk, base[:, bass.ds(k, 1)], row, ALU.add, ALU.mult).then_inc(s.d, 1)
                done[0] += NW
                dve.wait_ge(s.d, done[0])
                step_done(nc.vector.tensor_reduce(t.rec[:, :, 5], rank[:, :, :].rearrange("p k j -> p j k"), AX.X, ALU.add))

                def windows_passed(a):
                    step_done(nc.vector.tensor_tensor(reach[:, :, :], g_no[:, :].unsqueeze(2).broadcast_to([P, NG, NW]),
                                                      cum[:, a, :].unsqueeze(1).broadcast_to([P, NG, NW]), ALU.is_ge))
                    step_done(nc.vector.tensor_reduce(acc_f[:, a, :], reach[:, :, :], AX.X, ALU.add))
                    step_done(nc.vector.tensor_scalar(acc_f[:, a, :], acc_f[:, a, :], float(NW - 1), None, ALU.min))

                windows_passed(0)
                step_done(nc.vector.tensor_copy(t.src_win[:, :], acc_f[:, 0, :]))
                windows_passed(1)
                step_done(nc.vector.tensor_copy(t.dst_win[:, :], acc_f[:, 1, :]))
                step_done(nc.vector.tensor_scalar(t.win_base[:, :], acc_f[:, 1, :], float(P), None, ALU.mult))
                step_done(nc.vector.tensor_scalar(t.win_lane[:, :], t.win_base[:, :], t.lane[:, 0:1], None, ALU.add))
                step_done(nc.vector.scalar_tensor_tensor(off[:, 0:NW], fst[:, 1, :], -float(GE), off[:, 0:NW], ALU.mult, ALU.add))
                step_done(nc.vector.tensor_tensor(step[:, 0:NW - 1], off[:, 1:NW], off[:, 0:NW - 1], ALU.subtract))
                step_done(nc.vector.memset(step[:, NW - 1:NW], float(2 * E)))
                step_done(nc.vector.tensor_tensor(reach_o[:, :, :], reach[:, :, :], step[:, :].unsqueeze(1).broadcast_to([P, NG, NW]), ALU.mult))
                step_done(nc.vector.tensor_reduce(acc_f[:, 2, :], reach_o[:, :, :], AX.X, ALU.add))
                step_done(nc.vector.scalar_tensor_tensor(acc_f[:, 3, :], g_no[:, :], float(GE), acc_f[:, 2, :], ALU.mult, ALU.add))
                step_done(nc.vector.tensor_scalar(t.first_edge[:, :], acc_f[:, 3, :], float(E), None, ALU.min))


def edge_tables(nc, i, t):
    with ExitStack() as ctx:
        sb, psum, sems, slot_sems = allocators(nc, ctx, "edge_tables")
        neutral = sb("neutral", [P, TPG, ROWW], F32)
        pad_rec = sb("pad_rec", [P, TPG, 8], F32)
        pad_row = sb("pad_row", [3, GE], I16)
        s = sems("neutral_set written")
        with nc.Block() as block:
            @block.gpsimd
            def _(pool):
                pool.memset(neutral[:, :, 0:D], 0.0).then_inc(s.neutral_set, 1)
                pool.memset(neutral[:, :, D:D + HEADS], -BIG).then_inc(s.neutral_set, 1)
                pool.memset(neutral[:, :, D + HEADS:ROWW], -1.0).then_inc(s.neutral_set, 1)
                pool.memset(pad_rec[:, :, :], float(NO_NODE)).then_inc(s.neutral_set, 1)
                pool.memset(pad_row[:, :], NO_NODE).then_inc(s.neutral_set, 1)

            @block.sync
            def _(sp):
                sp.dma_start(t.rec_dram[0:EPAD, :].rearrange("(p j) c -> p (j c)", p=P),
                             t.rec[:, :, :].rearrange("p j c -> p (j c)")).then_inc(s.written, 16)
                for r in range(3):
                    sp.dma_start(t.row_dram[r, 0:EPAD].rearrange("(p j) -> p j", p=P), t.row16[:, r, :]).then_inc(s.written, 16)
                sp.wait_ge(s.neutral_set, 5)
                sp.dma_start(t.rec_dram[EPAD:EPAD + GE, :].rearrange("(q p) c -> p q c", p=P), pad_rec[:, :, :]).then_inc(s.written, 16)
                sp.dma_start(t.row_dram[:, EPAD:EPAD + GE], pad_row[:, :]).then_inc(s.written, 16)
                with sp.Fori(0, 2 * NW) as k:
                    at = sp.value_load(t.fill_at[0:1, bass.ds(k, 1)], min_val=0, max_val=SCRAP + (2 * NW - 1) * GE)
                    sp.dma_start(t.rows_dram[bass.ds(at, GE), :].rearrange("(q p) c -> p q c", p=P), neutral[:, :, :]).then_inc(s.written, 16)
                sp.wait_ge(s.written, 16 * (6 + 2 * NW))


def layer0_edges(nc, i, t):
    with ExitStack() as ctx:
        sb, psum, sems, slot_sems = allocators(nc, ctx, "layer0_edges")
        wide = sb("wide", [P, SL, 2, GE], I16)
        hot = sb("hot", [P, SL, 2, GE], BF16)
        picked = sb("picked", [P, SL, TPG, NW * HEADS], F32)
        part = sb("part", [P, SL, TPG, HEADS], F32)
        dst_part = sb("dst_part", [P, SL, TPG, HEADS], F32)
        row = sb("row", [P, SL, TPG, ROWW], F32)
        at = sb("at", [P, SL, TPG], U32)
        at_f = sb("at_f", [P, SL, TPG], F32)
        ps_f = [psum(f"ps_f{b}", [P, TPG, 512]) for b in range(2)]
        ps_a = [psum(f"ps_a{b}", [P, TPG, 256]) for b in range(2)]
        s = sems("d turn load_turn row_zero")
        wide_in, rec_in, hot_made, f_ready = slot_sems("wide_in rec_in hot_made f_ready")
        scored, f_copied = slot_sems("scored f_copied")
        row_out = t.row_out
        dst_part_copied, = slot_sems("dst_part_copied")
        with nc.Block() as block:
            @block.sync
            def _(sp):
                def turn(r):
                    for b in range(SL):
                        g = SL * r + b
                        e0 = sp.value_load(t.first_edge[0:1, bass.ds(g, 1)], min_val=0, max_val=E)
                        sp.dma_start(t.edge[:, bass.ds(g * TPG, TPG), :],
                                     t.rec_dram[bass.ds(e0, GE), :].rearrange("(q p) c -> p q c", p=P)).then_inc(rec_in[b], 16)
                        sp.wait_ge(hot_made[b], r)
                        sp.sem_inc(s.load_turn, 1)
                        sp.dma_start(wide[:, b, :, :], t.row_dram[0:2, bass.ds(e0, GE)].partition_broadcast(P)).then_inc(wide_in[b], 16)
                rounds(sp, NG // SL, turn)

            @block.vector
            def _(dve):
                nc.vector.memset(row[:, :, :, D + HEADS:ROWW], 0.0).then_inc(s.row_zero, 1)
                dve.wait_ge(s.row_zero, 1)

                def one_hots(r, b, g):
                    dve.wait_ge(wide_in[b], 16 * (r + 1))
                    dve.wait_ge(f_ready[b], r)
                    nc.vector.tensor_scalar(hot[:, b, 0, :], wide[:, b, 0, :], t.lane[:, 0:1], None, ALU.is_equal)
                    nc.vector.tensor_scalar(hot[:, b, 1, :], wide[:, b, 1, :], t.win_lane[:, bass.ds(g, 1)], None,
                                            ALU.is_equal).then_inc(hot_made[b], 1)

                STEPS = 12

                def scores(r, b, g):
                    e = t.edge[:, bass.ds(g * TPG, TPG), :]
                    n = g * STEPS
                    dve.wait_ge(rec_in[b], 16 * (r + 1))
                    nc.vector.tensor_scalar(t.local[:, bass.ds(g * TPG, TPG)], e[:, :, 0], t.win_base[:, bass.ds(g, 1)], None,
                                            ALU.subtract).then_inc(s.d, 1)
                    nc.vector.tensor_scalar(t.valid[:, bass.ds(g * TPG, TPG)], e[:, :, 0], t.win_base[:, bass.ds(g, 1)], float(P),
                                            ALU.subtract, ALU.is_lt).then_inc(s.d, 1)
                    dve.wait_ge(f_ready[b], r + 1)
                    for q in range(TPG):
                        nc.vector.scalar_tensor_tensor(picked[:, b, q, :], t.win_of_col[:, :], e[:, q, 3:4],
                                                       ps_a[b % 2][:, q, 0:NW * HEADS], ALU.is_equal, ALU.mult).then_inc(s.d, 1)
                    dve.wait_ge(s.d, n + 2)
                    nc.vector.scalar_tensor_tensor(at_f[:, b, :], e[:, :, 5], t.trash[:, 0:1], t.valid[:, bass.ds(g * TPG, TPG)],
                                                   ALU.subtract, ALU.mult).then_inc(s.d, 1)
                    dve.wait_ge(s.d, n + 4)
                    nc.vector.tensor_reduce(part[:, b, :, :], picked[:, b, :, :].rearrange("p q (w h) -> p q h w", h=HEADS),
                                            AX.X, ALU.add).then_inc(s.d, 1)
                    dve.wait_ge(row_out[b], 16 * TPG * r)
                    dve.wait_ge(s.d, n + 5)
                    nc.vector.tensor_scalar(at[:, b, :], at_f[:, b, :], t.trash[:, 0:1], None, ALU.add).then_inc(s.d, 1)
                    nc.vector.tensor_copy(row[:, b, :, D + HEADS:D + HEADS + 1], e[:, :, 2:3]).then_inc(s.d, 1)
                    dve.wait_ge(s.d, n + 6)
                    for q in range(TPG):
                        nc.vector.scalar_tensor_tensor(part[:, b, q, :], t.elem_w[:, :], e[:, q, 4:5],
                                                       part[:, b, q, :], ALU.mult, ALU.add).then_inc(s.d, 1)
                    dve.wait_ge(dst_part_copied[b], r + 1)
                    dve.wait_ge(s.d, n + 10)
                    nc.vector.tensor_tensor(t.score[:, bass.ds(g * TPG, TPG), :], part[:, b, :, :],
                                            dst_part[:, b, :, :], ALU.add).then_inc(s.d, 1)
                    nc.vector.tensor_tensor(row[:, b, :, D:D + HEADS], part[:, b, :, :], dst_part[:, b, :, :], ALU.add).then_inc(s.d, 1)
                    dve.wait_ge(s.d, n + 12)
                    dve.sem_inc(scored[b], 1)

                def body(r, last):
                    for b in range(SL):
                        if b < SL - 1:
                            one_hots(r, b + 1, SL * r + b + 1)
                        elif not last:
                            one_hots(r + 1, 0, SL * r + SL)
                        scores(r, b, SL * r + b)

                one_hots(0, 0, 0)
                body(0, False)
                with dve.Fori(1, NG // SL - 1) as r:
                    body(r, False)
                body(NG // SL - 1, True)

            @block.tensor
            def _(pe):
                def turn(r):
                    for b in range(SL):
                        win = pe.value_load(t.dst_win[0:1, bass.ds(SL * r + b, 1)], min_val=0, max_val=NW - 1)
                        pe.wait_ge(hot_made[b], r + 1)
                        pe.wait_ge(f_copied[(b + 2) % SL], r + b // 2)
                        pe.wait_ge(scored[(b + 2) % SL], r + b // 2)
                        for q in range(TPG):
                            for k in range(3):
                                feats = t.table3[:, bass.ds(win, 1), k * ROWW:k * ROWW + HEADS * FH].rearrange("p a f -> p (a f)")
                                nc.tensor.matmul(ps_f[b % 2][:, q, 0:HEADS * FH], hot[:, b, 1, q * P:(q + 1) * P], feats,
                                                 start=k == 0, stop=k == 2)
                        for q in range(TPG):
                            for k in range(3):
                                last = nc.tensor.matmul(ps_a[b % 2][:, q, 0:NW * HEADS], hot[:, b, 0, q * P:(q + 1) * P],
                                                        t.table3[:, :, k * ROWW + HD:k * ROWW + HEADS * FH:FH],
                                                        start=k == 0, stop=k == 2)
                        last.then_inc(f_ready[b], 1)
                rounds(pe, NG // SL, turn)

            @block.scalar
            def _(act):
                def turn(r):
                    for b in range(SL):
                        act.wait_ge(f_ready[b], r + 1)
                        act.wait_ge(scored[b], r)
                        nc.scalar.activation(dst_part[:, b, :, :], ps_f[b % 2][:, :, HD + 1:HEADS * FH:FH], ACT.Copy).then_inc(dst_part_copied[b], 1)
                        act.wait_ge(row_out[b], 16 * TPG * r)
                        for q in range(TPG):
                            last = nc.scalar.activation(row[:, b, q, 0:D].rearrange("p (h f) -> p h f", h=HEADS),
                                                        ps_f[b % 2][:, q, 0:HEADS * FH].rearrange("p (h f) -> p h f", h=HEADS)[:, :, 0:HD],
                                                        ACT.Copy)
                        last.then_inc(f_copied[b], 1)
                rounds(act, NG // SL, turn)

            @block.gpsimd
            def _(pool):
                def turn(r):
                    for b in range(SL):
                        pool.wait_ge(f_copied[b], r + 1)
                        pool.wait_ge(scored[b], r + 1)
                        pool.sem_inc(s.turn, 1)
                        for q in range(TPG):
                            pool.indirect_dma_start(t.rows_dram, bass.IndirectOffsetOnAxis(ap=at[:, b, q:q + 1], axis=0),
                                                    row[:, b, q, :], None, bounds_check=NROWS - 1,
                                                    oob_is_err=False).then_inc(row_out[b], 16)
                rounds(pool, NG // SL, turn)
                for b in range(SL):
                    pool.wait_ge(row_out[b], 16 * TPG * (NG // SL))


def layer0_sum(nc, i, t):
    with ExitStack() as ctx:
        sb, psum, sems, slot_sems = allocators(nc, ctx, "layer0_sum")
        hide = sb("hide", [P, NT], F32)
        masked = sb("masked", [P, NT, HEADS], F32)
        top_lane = sb("top_lane", [P, HEADS], F32)
        top = sb("top", [P, HEADS], F32)
        rin = sb("rin", [P, SL, TPG, ROWW], F32)
        rel = sb("rel", [P, SL, TPG, HEADS], F32)
        hot = sb("hot", [P, SL, TPG, P], F32)
        rhs = sb("rhs", [P, SL, TPG, D + HEADS], F32)
        ps = [psum(f"ps{b}", [P, 512]) for b in range(SL)]
        s = sems("d lane_top top_set acc_zero")
        rows_in, hot_made, weighed, summed, kept = slot_sems("rows_in hot_made weighed summed kept")
        scaled_dve, scaled_pool = slot_sems("scaled_dve scaled_pool")

        def scale(eng, b, q, sem):
            return eng.tensor_tensor(rhs[:, b, q, 0:D].rearrange("p (h f) -> p h f", h=HEADS),
                                     rin[:, b, q, 0:D].rearrange("p (h f) -> p h f", h=HEADS),
                                     rhs[:, b, q, D:D + HEADS].unsqueeze(2).broadcast_to([P, HEADS, HD]), ALU.mult).then_inc(sem, 1)

        with nc.Block() as block:
            @block.sync
            def _(sp):
                def turn(r):
                    for b in range(SL):
                        sp.wait_ge(hot_made[b], r)
                        sp.wait_ge(scaled_dve[b], r)
                        sp.wait_ge(scaled_pool[b], r)
                        sp.dma_start(rin[:, b, :, :], t.rows_dram[bass.ds((SL * r + b) * GE, GE), :]
                                     .rearrange("(q p) c -> p q c", p=P)).then_inc(rows_in[b], 16)
                rounds(sp, NG // SL, turn)

            @block.gpsimd
            def _(pool):
                pool.memset(t.acc[:, :, :], 0.0).then_inc(s.acc_zero, 1)
                pool.wait_ge(s.lane_top, 1)
                pool.partition_all_reduce(top[:, :], top_lane[:, :], P, bass.bass_isa.ReduceOp.max).then_inc(s.top_set, 1)
                def turn(r):
                    for b in range(SL):
                        pool.wait_ge(weighed[b], r + 1)
                        pool.wait_ge(summed[b], r)
                        scale(nc.gpsimd, b, 1, scaled_pool[b])
                rounds(pool, NG // SL, turn)

            @block.scalar
            def _(act):
                def turn(r):
                    for b in range(SL):
                        act.wait_ge(hot_made[b], r + 1)
                        act.wait_ge(summed[b], r)
                        nc.scalar.activation(rhs[:, b, :, D:D + HEADS], rel[:, b, :, :], ACT.Exp).then_inc(weighed[b], 1)
                rounds(act, NG // SL, turn)

            @block.tensor
            def _(pe):
                def turn(r):
                    for b in range(SL):
                        pe.wait_ge(scaled_dve[b], r + 1)
                        pe.wait_ge(scaled_pool[b], r + 1)
                        pe.wait_ge(kept[b], r)
                        for q in range(TPG):
                            last = nc.tensor.matmul(ps[b][:, 0:D + HEADS], hot[:, b, q, :], rhs[:, b, q, :],
                                                    start=q == 0, stop=q == TPG - 1)
                        last.then_inc(summed[b], 1)
                rounds(pe, NG // SL, turn)

            @block.vector
            def _(dve):
                nc.vector.tensor_scalar(hide[:, :], t.valid[:, :], 1.0, BIG, ALU.subtract, ALU.mult).then_inc(s.d, 1)
                dve.wait_ge(s.d, 1)
                nc.vector.tensor_tensor(masked[:, :, :], t.score[:, :, :], hide[:, :].unsqueeze(2).broadcast_to([P, NT, HEADS]),
                                        ALU.add).then_inc(s.d, 1)
                dve.wait_ge(s.d, 2)
                nc.vector.tensor_reduce(top_lane[:, :], masked[:, :, :].rearrange("p n h -> p h n"), AX.X, ALU.max).then_inc(s.lane_top, 1)
                dve.wait_ge(s.top_set, 1)
                dve.wait_ge(s.acc_zero, 1)

                def prepare_group(r, b):
                    dve.wait_ge(rows_in[b], 16 * (r + 1))
                    dve.wait_ge(summed[b], r)
                    dve.wait_ge(weighed[b], r)
                    for q in range(TPG):
                        nc.vector.tensor_scalar(hot[:, b, q, :], t.cols[:, :], rin[:, b, q, D + HEADS:D + HEADS + 1], None, ALU.is_equal)
                    nc.vector.tensor_tensor(rel[:, b, :, :], rin[:, b, :, D:D + HEADS],
                                            top[:, :].unsqueeze(1).broadcast_to([P, TPG, HEADS]), ALU.subtract).then_inc(hot_made[b], 1)

                def scale_group(r, b):
                    dve.wait_ge(weighed[b], r + 1)
                    scale(nc.vector, b, 0, scaled_dve[b])

                def add_group(r, b, g):
                    win = dve.value_load(t.src_win[0:1, bass.ds(g, 1)], min_val=0, max_val=NW - 1)
                    sums = t.acc[:, bass.ds(win, 1), 0:D + HEADS].rearrange("p a f -> p (a f)")
                    dve.wait_ge(summed[b], r + 1)
                    dve.wait_ge(kept[(b - 1) % SL], r + (b > 0))
                    nc.vector.tensor_tensor(sums, sums, ps[b][:, 0:D + HEADS], ALU.add).then_inc(kept[b], 1)

                def ahead(r, b, last):
                    if b < SL - 2:
                        prepare_group(r, b + 2)
                    elif not last:
                        prepare_group(r + 1, b + 2 - SL)
                    if b < SL - 1:
                        scale_group(r, b + 1)
                    elif not last:
                        scale_group(r + 1, 0)

                def body(r, last):
                    for b in range(SL):
                        ahead(r, b, last)
                        add_group(r, b, SL * r + b)

                prepare_group(0, 0)
                prepare_group(0, 1)
                scale_group(0, 0)
                body(0, False)
                with dve.Fori(1, NG // SL - 1) as r:
                    body(r, False)
                body(NG // SL - 1, True)


def layer_norm_chunk(nc, dve, act_sem, d, n, v, mean, ssq, rstd):
    nc.vector.tensor_reduce(mean, v, AX.X, ALU.add).then_inc(d, 1)
    dve.wait_ge(d, n + 1)
    nc.vector.tensor_scalar(mean, mean, 1.0 / D, None, ALU.mult).then_inc(d, 1)
    dve.wait_ge(d, n + 2)
    nc.vector.tensor_tensor(v, v, mean.unsqueeze(2).broadcast_to([P, CW, D]), ALU.subtract).then_inc(act_sem, 1)


def layer0_nodes(nc, i, t):
    with ExitStack() as ctx:
        sb, psum, sems, slot_sems = allocators(nc, ctx, "layer0_nodes")
        wqkv = sb("wqkv", [P, 2, 3 * D], F32)
        bqkv = sb("bqkv", [1, 3 * D], F32)
        query = sb("query", [P, D], F32)
        node_no = sb("node_no", [P, NW], F32)
        zero_w = sb("zero_w", [P, CW, HEADS], F32)
        den = sb("den", [P, CW, HEADS], F32)
        v = sb("v", [P, CW, D], F32)
        sq = sb("sq", [P, D], F32)
        mean = sb("mean", [P, CW], F32)
        ssq = sb("ssq", [P, CW], F32)
        rstd = sb("rstd", [P, CW], F32)
        enh = sb("enh", [P, CW, D], F32)
        enh_t = sb("enh_t", [P, 2, CW * P], F32)
        qtmp = sb("qtmp", [P, 2, D], F32)
        qres = sb("qres", [P, 2, D], F32)
        keys = sb("keys", [P, CW, D], F32)
        ps_x = [psum(f"ps_x{b}", [P, 512]) for b in range(2)]
        ps_qk = [psum(f"ps_qk{b}", [P, 512]) for b in range(2)]
        ps_v = [psum(f"ps_v{b}", [P, 512]) for b in range(2)]
        s = sems("w_in q_in pad_zero scaled d centred squared rooted normed enh_made turned enh_t_made projected "
                       "q_hi q_rest q_mid q_lo kv_kept k_out v_out")
        DSTEPS = 15
        with nc.Block() as block:
            @block.sync
            def _(sp):
                for c, w in enumerate((i.L1_gnn_Wq, i.L1_gnn_Wk, i.L1_gnn_Wv)):
                    sp.dma_start(wqkv[:, :, c * D:(c + 1) * D], w.rearrange("(k p) m -> p k m", p=P)).then_inc(s.w_in, 16)
                for c, w in enumerate((i.L1_gnn_bq, i.L1_gnn_bk, i.L1_gnn_bv)):
                    sp.dma_start(bqkv[:, c * D:(c + 1) * D], w.rearrange("(a m) -> a m", a=1)).then_inc(s.w_in, 16)
                sp.dma_start(query[:, :], i.L1_gnn_query_emb.partition_broadcast(P)).then_inc(s.q_in, 16)
                def turn(c):
                    sp.wait_ge(s.kv_kept, (c + 1) * CW)
                    sp.dma_start(t.key_dram[bass.ds(c * CW * P, CW * P), :].rearrange("(w p) m -> p w m", p=P), keys[:, :, :]).then_inc(s.k_out, 16)
                    sp.dma_start(t.val_dram[bass.ds(c * CW * P, CW * P), :].rearrange("(w p) m -> p w m", p=P),
                                 t.val[:, bass.ds(c * CW, CW), :]).then_inc(s.v_out, 16)
                rounds(sp, CH, turn)
                sp.wait_ge(s.k_out, 16 * CH)
                sp.wait_ge(s.v_out, 16 * CH)

            @block.gpsimd
            def _(pool):
                pool.memset(t.val[:, :, D:VROW], 0.0).then_inc(s.pad_zero, 1)
                pool.iota(node_no[:, :], pattern=[[P, NW]], base=0, channel_multiplier=1,
                          allow_small_or_imprecise_dtypes=True).then_inc(s.pad_zero, 1)
                pool.wait_ge(s.q_in, 16)
                pool.tensor_scalar(query[:, :], query[:, :], 0.1, None, ALU.mult).then_inc(s.scaled, 1)

            @block.vector
            def _(dve):
                dve.wait_ge(s.pad_zero, 2)
                dve.wait_ge(s.scaled, 1)

                def project_rest(k, b):
                    dve.wait_ge(s.q_hi, k + 1)
                    nc.vector.tensor_tensor(qres[:, b, :], qtmp[:, b, :], t.table3[:, bass.ds(k, 1), 0:D].rearrange("p a m -> p (a m)"),
                                            ALU.subtract).then_inc(s.q_rest, 1)
                    dve.wait_ge(s.q_mid, k + 1)
                    nc.vector.tensor_tensor(t.table3[:, bass.ds(k, 1), 2 * ROWW:2 * ROWW + D].rearrange("p a m -> p (a m)"), qres[:, b, :],
                                            t.table3[:, bass.ds(k, 1), ROWW:ROWW + D].rearrange("p a m -> p (a m)"), ALU.subtract).then_inc(s.q_lo, 1)

                def turn(c):
                    n = c * DSTEPS
                    weights = t.acc[:, bass.ds(c * CW, CW), D:D + HEADS]
                    x = t.x[:, bass.ds(c * CW, CW), :]
                    nc.vector.tensor_scalar(zero_w[:, :, :], weights, 0.0, None, ALU.is_equal).then_inc(s.d, 1)
                    dve.wait_ge(s.d, n + 1)
                    nc.vector.tensor_tensor(den[:, :, :], weights, zero_w[:, :, :], ALU.add).then_inc(s.d, 1)
                    nc.vector.tensor_reduce(mean[:, :], zero_w[:, :, :], AX.X, ALU.max).then_inc(s.d, 1)
                    dve.wait_ge(s.d, n + 2)
                    nc.vector.reciprocal(den[:, :, :], den[:, :, :]).then_inc(s.d, 1)
                    dve.wait_ge(s.d, n + 3)
                    nc.vector.scalar_tensor_tensor(t.val[:, bass.ds(c * CW, CW), D], node_no[:, bass.ds(c * CW, CW)], float(N), mean[:, :],
                                                   ALU.is_lt, ALU.mult).then_inc(s.d, 1)
                    dve.wait_ge(s.d, n + 5)
                    for w in range(CW):
                        nc.vector.tensor_tensor(v[:, w, :].rearrange("p (h f) -> p h f", h=HEADS),
                                                t.acc[:, bass.ds(c * CW + w, 1), 0:D].rearrange("p a (h f) -> p (a h) f", h=HEADS),
                                                den[:, w, :].unsqueeze(2).broadcast_to([P, HEADS, HD]), ALU.mult).then_inc(s.d, 1)
                    dve.wait_ge(s.d, n + 10)
                    nc.vector.tensor_tensor(v[:, :, :], v[:, :, :], x, ALU.add).then_inc(s.d, 1)
                    dve.wait_ge(s.d, n + 11)
                    layer_norm_chunk(nc, dve, s.centred, s.d, n + 11, v[:, :, :], mean[:, :], ssq, rstd)
                    dve.wait_ge(s.squared, (c + 1) * CW)
                    nc.vector.tensor_scalar(ssq[:, :], ssq[:, :], 1.0 / D, EPS, ALU.mult, ALU.add).then_inc(s.d, 1)
                    dve.wait_ge(s.rooted, c + 1)
                    nc.vector.reciprocal(rstd[:, :], rstd[:, :]).then_inc(s.d, 1)
                    dve.wait_ge(s.d, n + 15)
                    nc.vector.tensor_tensor(x, v[:, :, :], rstd[:, :].unsqueeze(2).broadcast_to([P, CW, D]), ALU.mult).then_inc(s.normed, 1)
                    dve.wait_ge(s.normed, c + 1)
                    dve.wait_ge(s.turned, c * CW)
                    nc.vector.tensor_tensor(enh[:, :, :], x, query[:, :].unsqueeze(1).broadcast_to([P, CW, D]), ALU.add).then_inc(s.enh_made, 1)
                    for w in range(CW):
                        project_rest(c * CW + w, w % 2)
                rounds(dve, CH, turn)

            @block.scalar
            def _(act):
                def turn(c):
                    act.wait_ge(s.centred, c + 1)
                    for w in range(CW):
                        nc.scalar.activation(sq[:, :], v[:, w, :], ACT.Square, accum_out=ssq[:, w:w + 1]).then_inc(s.squared, 1)
                        act.wait_ge(s.squared, c * CW + w + 1)
                    act.wait_ge(s.d, c * DSTEPS + 14)
                    nc.scalar.activation(rstd[:, :], ssq[:, :], ACT.Sqrt).then_inc(s.rooted, 1)
                    for w in range(CW):
                        act.wait_ge(s.turned, c * CW + w + 1)
                        nc.scalar.activation(enh_t[:, :, w * P:(w + 1) * P], ps_x[w % 2][:, 0:2 * P].rearrange("p (k n) -> p k n", k=2),
                                             ACT.Copy).then_inc(s.enh_t_made, 1)
                    act.wait_ge(s.k_out, 16 * c)
                    for w in range(CW):
                        k, b = c * CW + w, w % 2
                        act.wait_ge(s.projected, k + 1)
                        if w < 2:
                            act.wait_ge(s.q_lo, c * CW)
                        else:
                            act.wait_ge(s.q_lo, k - 1)
                        nc.scalar.activation(qtmp[:, b, :], ps_qk[b][:, 0:D], ACT.Copy)
                        nc.scalar.activation(t.table3[:, bass.ds(k, 1), 0:D].rearrange("p a m -> p (a m)"), ps_qk[b][:, 0:D], ACT.Copy).then_inc(s.q_hi, 1)
                        nc.scalar.activation(keys[:, w, :], ps_qk[b][:, D:2 * D], ACT.Copy)
                        nc.scalar.activation(t.val[:, bass.ds(k, 1), 0:D].rearrange("p a m -> p (a m)"), ps_v[b][:, 0:D], ACT.Copy).then_inc(s.kv_kept, 1)
                        act.wait_ge(s.q_rest, k + 1)
                        nc.scalar.activation(t.table3[:, bass.ds(k, 1), ROWW:ROWW + D].rearrange("p a m -> p (a m)"), qres[:, b, :], ACT.Copy).then_inc(s.q_mid, 1)
                rounds(act, CH, turn)

            @block.tensor
            def _(pe):
                pe.wait_ge(s.w_in, 16 * 6)
                def turn(c):
                    pe.wait_ge(s.enh_made, c + 1)
                    for w in range(CW):
                        if w < 2:
                            pe.wait_ge(s.enh_t_made, c * CW)
                        else:
                            pe.wait_ge(s.enh_t_made, c * CW + w - 1)
                        for half in range(2):
                            last = nc.tensor.transpose(ps_x[w % 2][:, half * P:(half + 1) * P], enh[:, w, half * P:(half + 1) * P], t.ident[:, :])
                        last.then_inc(s.turned, 1)
                    pe.wait_ge(s.enh_t_made, (c + 1) * CW)
                    for w in range(CW):
                        b = w % 2
                        if w < 2:
                            pe.wait_ge(s.kv_kept, c * CW)
                        else:
                            pe.wait_ge(s.kv_kept, c * CW + w - 1)
                        for k in range(2):
                            nc.tensor.matmul(ps_qk[b][:, :], enh_t[:, k, w * P:(w + 1) * P], wqkv[:, k, 0:2 * D], start=k == 0, stop=False)
                        nc.tensor.matmul(ps_qk[b][:, :], t.ones[0:1, 0:P], bqkv[0:1, 0:2 * D], start=False, stop=True)
                        for k in range(2):
                            nc.tensor.matmul(ps_v[b][:, 0:D], enh_t[:, k, w * P:(w + 1) * P], wqkv[:, k, 2 * D:3 * D], start=k == 0, stop=False)
                        nc.tensor.matmul(ps_v[b][:, 0:D], t.ones[0:1, 0:P], bqkv[0:1, 2 * D:3 * D], start=False, stop=True).then_inc(s.projected, 1)
                rounds(pe, CH, turn)


def layer1_scores(nc, i, t):
    with ExitStack() as ctx:
        sb, psum, sems, slot_sems = allocators(nc, ctx, "layer1_scores")
        rel = sb("rel", [RELS, HD], F32)
        rel_rest = sb("rel_rest", [RELS, HD], F32)
        rel3 = sb("rel3", [RELS, 3, HD], BF16)
        wide = sb("wide", [P, SL, 2, GE], I16)
        hot = sb("hot", [P, SL, GE], BF16)
        hot_r = sb("hot_r", [RELS, SL, GE], BF16)
        at = sb("at", [P, SL, TPG], U32)
        key = sb("key", [P, SL, TPG, D], F32)
        prod = sb("prod", [P, SL, TPG, D], F32)
        ps_q = [psum(f"ps_q{b}", [P, TPG, D]) for b in range(SL)]
        ps_r = [psum(f"ps_r{b}", [P, 512]) for b in range(SL)]
        s = sems("rel_in d turn load_turn")
        wide_in, hot_made, q_ready, at_set, with_rel, multiplied, reduced = slot_sems("wide_in hot_made q_ready at_set with_rel multiplied reduced")
        key_in = t.key_in
        with nc.Block() as block:
            @block.sync
            def _(sp):
                sp.dma_start(rel[:, :], i.L1_gnn_rel_w).then_inc(s.rel_in, 16)
                def turn(r):
                    for b in range(SL):
                        e0 = sp.value_load(t.first_edge[0:1, bass.ds(SL * r + b, 1)], min_val=0, max_val=E)
                        sp.wait_ge(hot_made[b], r)
                        sp.sem_inc(s.load_turn, 1)
                        sp.dma_start(wide[:, b, :, :], t.row_dram[1:3, bass.ds(e0, GE)].partition_broadcast(P)).then_inc(wide_in[b], 16)
                rounds(sp, NG // SL, turn)

            @block.gpsimd
            def _(pool):
                def turn(r):
                    for b in range(SL):
                        pool.wait_ge(at_set[b], r + 1)
                        pool.wait_ge(multiplied[b], r)
                        pool.sem_inc(s.turn, 1)
                        for q in range(TPG):
                            pool.indirect_dma_start(key[:, b, q, :], None, t.key_dram,
                                                    bass.IndirectOffsetOnAxis(ap=at[:, b, q:q + 1], axis=0)).then_inc(key_in[b], 16)
                rounds(pool, NG // SL, turn)

            @block.tensor
            def _(pe):
                def turn(r):
                    for b in range(SL):
                        win = pe.value_load(t.dst_win[0:1, bass.ds(SL * r + b, 1)], min_val=0, max_val=NW - 1)
                        pe.wait_ge(hot_made[b], r + 1)
                        pe.wait_ge(multiplied[b], r)
                        for q in range(TPG):
                            for k in range(3):
                                nc.tensor.matmul(ps_q[b][:, q, :], hot[:, b, q * P:(q + 1) * P],
                                                 t.table3[:, bass.ds(win, 1), k * ROWW:k * ROWW + D].rearrange("p a m -> p (a m)"),
                                                 start=k == 0, stop=k == 2)
                        for q in range(TPG):
                            for k in range(3):
                                last = nc.tensor.matmul(ps_r[b][:, q * HD:(q + 1) * HD], hot_r[:, b, q * P:(q + 1) * P], rel3[:, k, :],
                                                        start=k == 0, stop=k == 2)
                        last.then_inc(q_ready[b], 1)
                rounds(pe, NG // SL, turn)

            @block.vector
            def _(dve):
                dve.wait_ge(s.rel_in, 16)
                steps = (lambda: nc.vector.tensor_scalar(rel[:, :], rel[:, :], 0.2, None, ALU.mult),
                         lambda: nc.vector.tensor_copy(rel3[:, 0, :], rel[:, :]),
                         lambda: nc.vector.tensor_tensor(rel_rest[:, :], rel[:, :], rel3[:, 0, :], ALU.subtract),
                         lambda: nc.vector.tensor_copy(rel3[:, 1, :], rel_rest[:, :]),
                         lambda: nc.vector.tensor_tensor(rel3[:, 2, :], rel_rest[:, :], rel3[:, 1, :], ALU.subtract))
                for n, make in enumerate(steps):
                    make().then_inc(s.d, 1)
                    dve.wait_ge(s.d, n + 1)

                def one_hots(r, b, g):
                    dve.wait_ge(wide_in[b], 16 * (r + 1))
                    dve.wait_ge(q_ready[b], r)
                    nc.vector.tensor_scalar(hot[:, b, :], wide[:, b, 0, :], t.win_lane[:, bass.ds(g, 1)], None, ALU.is_equal)
                    nc.vector.tensor_scalar(hot_r[:, b, :], wide[0:RELS, b, 1, :], t.lane[0:RELS, 0:1], None, ALU.is_equal).then_inc(hot_made[b], 1)

                def addresses(r, b, g):
                    dve.wait_ge(key_in[b], 16 * TPG * r)
                    nc.vector.tensor_scalar(at[:, b, :], t.edge[:, bass.ds(g * TPG, TPG), 1], float(NPAD - 1), None, ALU.min).then_inc(at_set[b], 1)

                def multiply(r, b):
                    dve.wait_ge(key_in[b], 16 * TPG * (r + 1))
                    dve.wait_ge(q_ready[b], r + 1)
                    dve.wait_ge(reduced[b], r)
                    for q in range(TPG):
                        ins = nc.vector.tensor_tensor(prod[:, b, q, :].rearrange("p (h f) -> p h f", h=HEADS),
                                                      key[:, b, q, :].rearrange("p (h f) -> p h f", h=HEADS),
                                                      ps_r[b][:, q * HD:(q + 1) * HD].unsqueeze(1).broadcast_to([P, HEADS, HD]), ALU.add)
                    ins.then_inc(with_rel[b], 1)
                    dve.wait_ge(with_rel[b], r + 1)
                    nc.vector.tensor_tensor(prod[:, b, :, :], prod[:, b, :, :], ps_q[b][:, :, :], ALU.mult).then_inc(multiplied[b], 1)

                def body(r, last):
                    for b in range(SL):
                        if b < SL - 1:
                            one_hots(r, b + 1, SL * r + b + 1)
                        elif not last:
                            one_hots(r + 1, 0, SL * r + SL)
                        multiply(r, b)
                        if not last:
                            addresses(r + 1, b, SL * r + b + SL)

                for b in range(SL):
                    addresses(0, b, b)
                one_hots(0, 0, 0)
                body(0, False)
                with dve.Fori(1, NG // SL - 1) as r:
                    body(r, False)
                body(NG // SL - 1, True)

            @block.scalar
            def _(act):
                def turn(r):
                    for b in range(SL):
                        g = SL * r + b
                        act.wait_ge(multiplied[b], r + 1)
                        for q in range(TPG):
                            for h in range(HEADS):
                                terms = prod[:, b, q, h * HD:(h + 1) * HD]
                                last = nc.scalar.activation(terms, terms, ACT.Copy,
                                                            accum_out=t.score[:, bass.ds(g * TPG + q, 1), h])
                        last.then_inc(reduced[b], 1)
                rounds(act, NG // SL, turn)


def segment_max(nc, i, t):
    TB = P // HEADS
    NB = -(-NT // TB)
    NTP = NB * TB
    with ExitStack() as ctx:
        sb, psum, sems, slot_sems = allocators(nc, ctx, "segment_max")
        hide = sb("hide", [P, NT], F32)
        masked = sb("masked", [P, NTP, HEADS], F32)
        keys = sb("keys", [P, NTP, HEADS], F32)
        key1 = sb("key1", [P, NT], F32)
        val = sb("val", [P, NB, P], F32)
        key = sb("key", [P, NB, P], F32)
        spare = t.acc[:, :, :].rearrange("p w f -> p (w f)")
        starts, ends, fwd = (spare[:, k * NB * P:(k + 1) * NB * P].rearrange("p (b e) -> p b e", e=P) for k in range(3))
        bwd = sb("bwd", [P, NB, P], F32)
        edge4 = sb("edge4", [P, NB, 4], F32)
        by_tile = sb("by_tile", [HEADS, NTP, 4], F32)
        whole = sb("whole", [HEADS, NTP], F32)
        joined = sb("joined", [HEADS, NTP + 1], F32)
        gate = sb("gate", [HEADS, NTP], F32)
        run = sb("run", [HEADS, NTP], F32)
        carry = sb("carry", [HEADS, NTP, 2], F32)
        carry_b = sb("carry_b", [P, NB, 2], F32)
        ps = [psum(f"ps{b}", [P, 4, P]) for b in range(2)]
        s = sems("pads d laid turned kept edge_out tile_in carry_out carry_in max_made back added weights")
        BLOCKS4 = [(b, min(4, NB - b)) for b in range(0, NB, 4)]

        with nc.Block() as block:
            @block.gpsimd
            def _(pool):
                pool.memset(masked[:, NT:NTP, :], -BIG).then_inc(s.pads, 1)
                pool.memset(keys[:, NT:NTP, :], -1.0).then_inc(s.pads, 1)

            @block.tensor
            def _(pe):
                pe.wait_ge(s.laid, 1)
                n = 0
                for what in (masked, keys):
                    flat = what[:, :, :].rearrange("p n h -> p (n h)")
                    for b0, m in BLOCKS4:
                        if n >= 2:
                            pe.wait_ge(s.kept, n - 1)
                        for q in range(m):
                            last = nc.tensor.transpose(ps[n % 2][:, q, :], flat[:, (b0 + q) * P:(b0 + q + 1) * P], t.ident[:, :])
                        last.then_inc(s.turned, 1)
                        n += 1
                pe.wait_ge(s.max_made, 1)
                for b0, m in BLOCKS4:
                    pe.wait_ge(s.kept, n - 1)
                    for q in range(m):
                        last = nc.tensor.transpose(ps[n % 2][:, q, :], fwd[:, b0 + q, :], t.ident[:, :])
                    last.then_inc(s.turned, 1)
                    n += 1

            @block.scalar
            def _(act):
                n = 0
                for to in (val, key):
                    for b0, m in BLOCKS4:
                        act.wait_ge(s.turned, n + 1)
                        nc.scalar.activation(to[:, b0:b0 + m, :], ps[n % 2][:, 0:m, :], ACT.Copy).then_inc(s.kept, 1)
                        n += 1
                flat = keys[:, :, :].rearrange("p n h -> p (n h)")
                for b0, m in BLOCKS4:
                    act.wait_ge(s.turned, n + 1)
                    nc.scalar.activation(flat[:, b0 * P:(b0 + m) * P], ps[n % 2][:, 0:m, :].rearrange("p a e -> p (a e)"), ACT.Copy).then_inc(s.kept, 1)
                    n += 1
                act.wait_ge(s.added, 1)
                nc.scalar.activation(t.score[:, :, :], t.score[:, :, :], ACT.Exp, scale=float(HD) ** -0.5).then_inc(s.weights, 1)

            @block.sync
            def _(sp):
                rows = t.edge_dram.rearrange("(b p c) -> p b c", p=P, c=4)
                tiles = t.edge_dram.rearrange("(n h c) -> h n c", h=HEADS, c=4)
                crows = t.carry_dram.rearrange("(b p c) -> p b c", p=P, c=2)
                ctiles = t.carry_dram.rearrange("(n h c) -> h n c", h=HEADS, c=2)
                sp.wait_ge(s.edge_out, 1)
                sp.dma_start(rows, edge4[:, :, :]).then_inc(s.edge_out, 16)
                sp.wait_ge(s.edge_out, 17)
                sp.dma_start(by_tile[:, :, :], tiles).then_inc(s.tile_in, 16)
                sp.wait_ge(s.carry_out, 1)
                sp.dma_start(ctiles, carry[:, :, :]).then_inc(s.carry_out, 16)
                sp.wait_ge(s.carry_out, 17)
                sp.dma_start(carry_b[:, :, :], crows).then_inc(s.carry_in, 16)

            @block.vector
            def _(dve):
                done = [0]

                def step_done(ins):
                    done[0] += 1
                    ins.then_inc(s.d, 1)
                    dve.wait_ge(s.d, done[0])

                v = nc.vector
                tt, ts, stt = v.tensor_tensor, v.tensor_scalar, v.scalar_tensor_tensor
                step_done(ts(hide[:, :], t.valid[:, :], 1.0, BIG, ALU.subtract, ALU.mult))
                step_done(tt(masked[:, 0:NT, :], t.score[:, :, :], t.valid[:, :].unsqueeze(2).broadcast_to([P, NT, HEADS]), ALU.mult))
                step_done(tt(masked[:, 0:NT, :], masked[:, 0:NT, :], hide[:, :].unsqueeze(2).broadcast_to([P, NT, HEADS]), ALU.add))
                step_done(stt(key1[:, :], t.edge[:, :, 0], 1.0, t.valid[:, :], ALU.add, ALU.mult))
                step_done(ts(key1[:, :], key1[:, :], -1.0, None, ALU.add))
                step_done(v.tensor_copy(keys[:, 0:NT, :], key1[:, :].unsqueeze(2).broadcast_to([P, NT, HEADS])))
                dve.wait_ge(s.pads, 2)
                dve.sem_inc(s.laid, 1)
                dve.wait_ge(s.kept, 2 * len(BLOCKS4))
                step_done(v.memset(starts[:, :, 0:1], -BIG))
                step_done(v.memset(ends[:, :, P - 1:P], -BIG))
                step_done(tt(starts[:, :, 1:P], key[:, :, 1:P], key[:, :, 0:P - 1], ALU.not_equal))
                step_done(ts(starts[:, :, 1:P], starts[:, :, 1:P], -BIG, None, ALU.mult))
                step_done(v.tensor_copy(ends[:, :, 0:P - 1], starts[:, :, 1:P]))
                flat = lambda a: a[:, :, :].rearrange("p b e -> p (b e)")
                step_done(v.tensor_tensor_scan(flat(fwd), flat(starts), flat(val), -BIG, ALU.add, ALU.max))
                step_done(v.tensor_tensor_scan(flat(bwd)[:, ::-1], flat(ends)[:, ::-1], flat(val)[:, ::-1], -BIG, ALU.add, ALU.max))
                step_done(tt(val[:, :, :], fwd[:, :, :], bwd[:, :, :], ALU.max))
                step_done(v.tensor_copy(edge4[:, :, 0:1], key[:, :, 0:1]))
                step_done(v.tensor_copy(edge4[:, :, 1:2], key[:, :, P - 1:P]))
                step_done(v.tensor_copy(edge4[:, :, 2:3], val[:, :, 0:1]))
                v.tensor_copy(edge4[:, :, 3:4], val[:, :, P - 1:P]).then_inc(s.edge_out, 1)
                dve.wait_ge(s.tile_in, 16)
                k0, k1, m0, m1 = (by_tile[:, :, c] for c in range(4))
                step_done(tt(whole[:, :], k0, k1, ALU.is_equal))
                step_done(v.memset(joined[:, :], 0.0))
                step_done(tt(joined[:, 1:NTP], k0[:, 1:NTP], k1[:, 0:NTP - 1], ALU.is_equal))
                step_done(tt(gate[:, :], whole[:, :], joined[:, 0:NTP], ALU.mult))
                step_done(ts(gate[:, :], gate[:, :], 1.0, BIG, ALU.subtract, ALU.mult))
                step_done(v.tensor_tensor_scan(run[:, :], gate[:, :], m1, -BIG, ALU.add, ALU.max))
                step_done(v.memset(carry[:, :, :], -BIG))
                step_done(ts(gate[:, :], joined[:, 0:NTP], 1.0, BIG, ALU.subtract, ALU.mult))
                step_done(tt(carry[:, 1:NTP, 0], run[:, 0:NTP - 1], gate[:, 1:NTP], ALU.add))
                step_done(tt(gate[:, :], whole[:, :], joined[:, 1:NTP + 1], ALU.mult))
                step_done(ts(gate[:, :], gate[:, :], 1.0, BIG, ALU.subtract, ALU.mult))
                step_done(v.tensor_tensor_scan(run[:, ::-1], gate[:, ::-1], m0[:, ::-1], -BIG, ALU.add, ALU.max))
                step_done(ts(gate[:, :], joined[:, 1:NTP + 1], 1.0, BIG, ALU.subtract, ALU.mult))
                step_done(tt(carry[:, 0:NTP - 1, 1], run[:, 1:NTP], gate[:, 0:NTP - 1], ALU.add))
                v.nop().then_inc(s.carry_out, 1)
                bc = lambda a: a.broadcast_to([P, NB, P])
                step_done(tt(starts[:, :, :], key[:, :, :], bc(key[:, :, 0:1]), ALU.is_equal))
                step_done(tt(ends[:, :, :], key[:, :, :], bc(key[:, :, P - 1:P]), ALU.is_equal))
                for a in (starts, ends):
                    step_done(ts(a[:, :, :], a[:, :, :], 1.0, BIG, ALU.subtract, ALU.mult))
                dve.wait_ge(s.carry_in, 16)
                for a, c in ((starts, 0), (ends, 1)):
                    step_done(tt(a[:, :, :], a[:, :, :], bc(carry_b[:, :, c:c + 1]), ALU.add))
                    step_done(tt(val[:, :, :], val[:, :, :], a[:, :, :], ALU.max))
                v.tensor_copy(fwd[:, :, :], val[:, :, :]).then_inc(s.max_made, 1)
                dve.wait_ge(s.kept, 3 * len(BLOCKS4))
                tt(t.score[:, :, :], masked[:, 0:NT, :], keys[:, 0:NT, :], ALU.subtract).then_inc(s.added, 1)
                dve.wait_ge(s.weights, 1)
                step_done(tt(t.score[:, :, :], t.score[:, :, :], t.valid[:, :].unsqueeze(2).broadcast_to([P, NT, HEADS]), ALU.mult))


def layer1_sum(nc, i, t):
    with ExitStack() as ctx:
        sb, psum, sems, slot_sems = allocators(nc, ctx, "layer1_sum")
        at = sb("at", [P, SL, TPG], U32)
        vin = sb("vin", [P, SL, TPG, VROW], F32)
        hot = sb("hot", [P, SL, TPG, P], F32)
        rhs = sb("rhs", [P, SL, TPG, D + HEADS + 1], F32)
        ps = [psum(f"ps{b}", [P, 512]) for b in range(SL)]
        s = sems("acc_zero turn")
        at_set, hot_made, weighed, scaled, summed, kept = slot_sems("at_set hot_made weighed scaled summed kept")
        val_in = t.val_in
        with nc.Block() as block:
            @block.gpsimd
            def _(pool):
                pool.memset(t.acc[:, :, :], 0.0).then_inc(s.acc_zero, 1)
                def turn(r):
                    for b in range(SL):
                        pool.wait_ge(at_set[b], r + 1)
                        pool.wait_ge(scaled[b], r)
                        pool.wait_ge(weighed[b], r)
                        pool.sem_inc(s.turn, 1)
                        for q in range(TPG):
                            pool.indirect_dma_start(vin[:, b, q, :], None, t.val_dram,
                                                    bass.IndirectOffsetOnAxis(ap=at[:, b, q:q + 1], axis=0)).then_inc(val_in[b], 16)
                rounds(pool, NG // SL, turn)

            @block.scalar
            def _(act):
                def turn(r):
                    for b in range(SL):
                        g = SL * r + b
                        act.wait_ge(val_in[b], 16 * TPG * (r + 1))
                        act.wait_ge(summed[b], r)
                        nc.scalar.activation(rhs[:, b, :, D:D + HEADS], t.score[:, bass.ds(g * TPG, TPG), :], ACT.Copy)
                        nc.scalar.activation(rhs[:, b, :, D + HEADS], vin[:, b, :, D], ACT.Copy).then_inc(weighed[b], 1)
                rounds(act, NG // SL, turn)

            @block.tensor
            def _(pe):
                def turn(r):
                    for b in range(SL):
                        pe.wait_ge(hot_made[b], r + 1)
                        pe.wait_ge(weighed[b], r + 1)
                        pe.wait_ge(scaled[b], r + 1)
                        pe.wait_ge(kept[b], r)
                        for q in range(TPG):
                            last = nc.tensor.matmul(ps[b][:, 0:D + HEADS + 1], hot[:, b, q, :], rhs[:, b, q, :],
                                                    start=q == 0, stop=q == TPG - 1)
                        last.then_inc(summed[b], 1)
                rounds(pe, NG // SL, turn)

            @block.vector
            def _(dve):
                dve.wait_ge(s.acc_zero, 1)

                def addresses(r, b, g):
                    dve.wait_ge(val_in[b], 16 * TPG * r)
                    nc.vector.tensor_scalar(at[:, b, :], t.edge[:, bass.ds(g * TPG, TPG), 1], float(NPAD - 1), None, ALU.min).then_inc(at_set[b], 1)

                def one_hots(r, b, g):
                    dve.wait_ge(summed[b], r)
                    for q in range(TPG):
                        last = nc.vector.tensor_scalar(hot[:, b, q, :], t.cols[:, :], t.local[:, bass.ds(g * TPG + q, 1)], None, ALU.is_equal)
                    last.then_inc(hot_made[b], 1)

                def scale_group(r, b, g):
                    dve.wait_ge(val_in[b], 16 * TPG * (r + 1))
                    dve.wait_ge(summed[b], r)
                    for q in range(TPG):
                        last = nc.vector.tensor_tensor(rhs[:, b, q, 0:D].rearrange("p (h f) -> p h f", h=HEADS),
                                                       vin[:, b, q, 0:D].rearrange("p (h f) -> p h f", h=HEADS),
                                                       t.score[:, bass.ds(g * TPG + q, 1), :].rearrange("p a h -> p (a h)")
                                                       .unsqueeze(2).broadcast_to([P, HEADS, HD]), ALU.mult)
                    last.then_inc(scaled[b], 1)

                def add_group(r, b, g):
                    win = dve.value_load(t.dst_win[0:1, bass.ds(g, 1)], min_val=0, max_val=NW - 1)
                    sums = t.acc[:, bass.ds(win, 1), 0:D + HEADS + 1].rearrange("p a f -> p (a f)")
                    dve.wait_ge(summed[b], r + 1)
                    dve.wait_ge(kept[(b - 1) % SL], r + (b > 0))
                    nc.vector.tensor_tensor(sums, sums, ps[b][:, 0:D + HEADS + 1], ALU.add).then_inc(kept[b], 1)

                def body(r, last):
                    for b in range(SL):
                        if b < SL - 1:
                            one_hots(r, b + 1, SL * r + b + 1)
                            scale_group(r, b + 1, SL * r + b + 1)
                        elif not last:
                            one_hots(r + 1, 0, SL * r + SL)
                            scale_group(r + 1, 0, SL * r + SL)
                        if not last:
                            addresses(r + 1, b, SL * r + b + SL)
                        add_group(r, b, SL * r + b)

                for b in range(SL):
                    addresses(0, b, b)
                one_hots(0, 0, 0)
                scale_group(0, 0, 0)
                body(0, False)
                with dve.Fori(1, NG // SL - 1) as r:
                    body(r, False)
                body(NG // SL - 1, True)


def layer1_nodes(nc, i, t):
    with ExitStack() as ctx:
        sb, psum, sems, slot_sems = allocators(nc, ctx, "layer1_nodes")
        wo = sb("wo", [P, 2, D], F32)
        bo = sb("bo", [1, D], F32)
        gamma = sb("gamma", [P, D], F32)
        beta = sb("beta", [P, D], F32)
        alone = sb("alone", [P, CW, HEADS], F32)
        den = sb("den", [P, CW, HEADS], F32)
        msg = sb("msg", [P, CW, D], F32)
        own = sb("own", [P, CW, D], F32)
        msg_t = sb("msg_t", [P, 2, CW * P], F32)
        v = sb("v", [P, CW, D], F32)
        sq = sb("sq", [P, D], F32)
        mean = sb("mean", [P, CW], F32)
        ssq = sb("ssq", [P, CW], F32)
        rstd = sb("rstd", [P, CW], F32)
        fine = sb("fine", [P, CW], F32)
        ps_x = [psum(f"ps_x{b}", [P, 512]) for b in range(2)]
        ps_o = [psum(f"ps_o{b}", [P, 512]) for b in range(2)]
        s = sems("w_in d msg_made turned msg_t_made projected added squared rooted centred normed out_done")
        with nc.Block() as block:
            @block.sync
            def _(sp):
                sp.dma_start(wo[:, :, :], i.L1_gnn_Wo.rearrange("(k p) m -> p k m", p=P)).then_inc(s.w_in, 16)
                sp.dma_start(bo[:, :], i.L1_gnn_bo.rearrange("(a m) -> a m", a=1)).then_inc(s.w_in, 16)
                sp.dma_start(gamma[:, :], i.L1_gnn_gamma.partition_broadcast(P)).then_inc(s.w_in, 16)
                sp.dma_start(beta[:, :], i.L1_gnn_beta.partition_broadcast(P)).then_inc(s.w_in, 16)
                def turn(c):
                    sp.wait_ge(s.normed, 3 * (c + 1))
                    sp.dma_start(i.out[bass.ds(c * CW * P, CW * P), :].rearrange("(w p) m -> p w m", p=P), v[:, :, :]).then_inc(s.out_done, 16)
                rounds(sp, CH - 1, turn)
                first = (CH - 1) * CW * P
                sp.wait_ge(s.normed, 3 * CH)
                sp.dma_start(i.out[first:(NW - 1) * P, :].rearrange("(w p) m -> p w m", p=P), v[:, 0:CW - 1, :]).then_inc(s.out_done, 16)
                sp.dma_start(i.out[(NW - 1) * P:N, :], v[0:TAIL_NODES, CW - 1, :]).then_inc(s.out_done, 16)
                sp.wait_ge(s.out_done, 16 * (CH + 1))

            @block.tensor
            def _(pe):
                pe.wait_ge(s.w_in, 16 * 4)
                def turn(c):
                    pe.wait_ge(s.msg_made, c + 1)
                    for w in range(CW):
                        if w < 2:
                            pe.wait_ge(s.msg_t_made, c * CW)
                        else:
                            pe.wait_ge(s.msg_t_made, c * CW + w - 1)
                        for half in range(2):
                            last = nc.tensor.transpose(ps_x[w % 2][:, half * P:(half + 1) * P], msg[:, w, half * P:(half + 1) * P], t.ident[:, :])
                        last.then_inc(s.turned, 1)
                    pe.wait_ge(s.msg_t_made, (c + 1) * CW)
                    for w in range(CW):
                        if w < 2:
                            pe.wait_ge(s.added, c * CW)
                        else:
                            pe.wait_ge(s.added, c * CW + w - 1)
                        for k in range(2):
                            nc.tensor.matmul(ps_o[w % 2][:, 0:D], msg_t[:, k, w * P:(w + 1) * P], wo[:, k, :], start=k == 0, stop=False)
                        nc.tensor.matmul(ps_o[w % 2][:, 0:D], t.ones[0:1, 0:P], bo[0:1, :], start=False, stop=True).then_inc(s.projected, 1)
                rounds(pe, CH, turn)

            @block.scalar
            def _(act):
                def turn(c):
                    for w in range(CW):
                        act.wait_ge(s.turned, c * CW + w + 1)
                        nc.scalar.activation(msg_t[:, :, w * P:(w + 1) * P], ps_x[w % 2][:, 0:2 * P].rearrange("p (k n) -> p k n", k=2),
                                             ACT.Copy).then_inc(s.msg_t_made, 1)
                    for norm in range(2):
                        m = c * 2 + norm
                        act.wait_ge(s.centred, m + 1)
                        for w in range(CW):
                            nc.scalar.activation(sq[:, :], v[:, w, :], ACT.Square, accum_out=ssq[:, w:w + 1]).then_inc(s.squared, 1)
                            act.wait_ge(s.squared, m * CW + w + 1)
                        act.wait_ge(s.normed, 3 * c + norm + 1)
                        nc.scalar.activation(rstd[:, :], ssq[:, :], ACT.Sqrt).then_inc(s.rooted, 1)
                rounds(act, CH, turn)

            @block.vector
            def _(dve):
                DSTEPS = 28
                dve.wait_ge(s.w_in, 16 * 4)
                def turn(c):
                    n = [0]

                    def step_done(ins):
                        n[0] += 1
                        ins.then_inc(s.d, 1)
                        dve.wait_ge(s.d, c * DSTEPS + n[0])

                    tt, ts = nc.vector.tensor_tensor, nc.vector.tensor_scalar
                    weights = t.acc[:, bass.ds(c * CW, CW), D:D + HEADS]
                    x = t.x[:, bass.ds(c * CW, CW), :]
                    over = lambda a: a.unsqueeze(2).broadcast_to([P, CW, D])
                    step_done(ts(alone[:, :, :], weights, 0.0, None, ALU.is_equal))
                    step_done(tt(den[:, :, :], weights, alone[:, :, :], ALU.add))
                    step_done(nc.vector.reciprocal(den[:, :, :], den[:, :, :]))
                    for w in range(CW):
                        heads = lambda a: a.rearrange("p a (h f) -> p (a h) f", h=HEADS)
                        step_done(tt(msg[:, w, :].rearrange("p (h f) -> p h f", h=HEADS), heads(t.acc[:, bass.ds(c * CW + w, 1), 0:D]),
                                     den[:, w, :].unsqueeze(2).broadcast_to([P, HEADS, HD]), ALU.mult))
                        step_done(tt(own[:, w, :].rearrange("p (h f) -> p h f", h=HEADS), heads(t.val[:, bass.ds(c * CW + w, 1), 0:D]),
                                     alone[:, w, :].unsqueeze(2).broadcast_to([P, HEADS, HD]), ALU.mult))
                    tt(msg[:, :, :], msg[:, :, :], own[:, :, :], ALU.add).then_inc(s.msg_made, 1)
                    step_done(tt(fine[:, :], t.acc[:, bass.ds(c * CW, CW), D + HEADS], t.val[:, bass.ds(c * CW, CW), D], ALU.add))
                    step_done(ts(fine[:, :], fine[:, :], 0.0, None, ALU.is_equal))
                    step_done(nc.vector.reciprocal(mean[:, :], fine[:, :]))
                    step_done(tt(fine[:, :], fine[:, :], mean[:, :], ALU.mult))
                    dve.wait_ge(s.out_done, 16 * c)
                    for w in range(CW):
                        dve.wait_ge(s.projected, c * CW + w + 1)
                        tt(v[:, w, :], ps_o[w % 2][:, 0:D], t.x[:, bass.ds(c * CW + w, 1), :].rearrange("p a m -> p (a m)"), ALU.add).then_inc(s.added, 1)
                    dve.wait_ge(s.added, (c + 1) * CW)
                    for norm in range(2):
                        step_done(nc.vector.tensor_reduce(mean[:, :], v[:, :, :], AX.X, ALU.add))
                        step_done(ts(mean[:, :], mean[:, :], 1.0 / D, None, ALU.mult))
                        tt(v[:, :, :], v[:, :, :], over(mean[:, :]), ALU.subtract).then_inc(s.centred, 1)
                        dve.wait_ge(s.squared, (c * 2 + norm + 1) * CW)
                        ts(ssq[:, :], ssq[:, :], 1.0 / D, EPS, ALU.mult, ALU.add).then_inc(s.normed, 1)
                        dve.wait_ge(s.rooted, c * 2 + norm + 1)
                        step_done(nc.vector.reciprocal(rstd[:, :], rstd[:, :]))
                        if norm == 0:
                            step_done(tt(rstd[:, :], rstd[:, :], fine[:, :], ALU.mult))
                            step_done(tt(v[:, :, :], v[:, :, :], over(rstd[:, :]), ALU.mult))
                            step_done(tt(v[:, :, :], v[:, :, :], gamma[:, :].unsqueeze(1).broadcast_to([P, CW, D]), ALU.mult))
                            step_done(tt(v[:, :, :], v[:, :, :], beta[:, :].unsqueeze(1).broadcast_to([P, CW, D]), ALU.add))
                            step_done(tt(v[:, :, :], v[:, :, :], x, ALU.add))
                    tt(v[:, :, :], v[:, :, :], over(rstd[:, :]), ALU.mult).then_inc(s.normed, 1)
                    assert n[0] == DSTEPS, n[0]
                rounds(dve, CH, turn)


def build(nc, i):
    with ExitStack() as ctx:
        t = named()
        ring = lambda name: [ctx.enter_context(nc.semaphore(f"{name}_{b}")) for b in range(SL)]
        t.row_out, t.key_in, t.val_in = ring("row_out"), ring("key_in"), ring("val_in")
        sb = allocators(nc, ctx, "all")[0]
        t.x = sb("x", [P, NW, D], F32)
        t.table3 = sb("table3", [P, NW, 3 * ROWW], BF16)
        t.ident = sb("ident", [P, P], F32)
        t.lane = sb("lane", [P, 1], F32)
        t.trash = sb("trash", [P, 1], F32)
        t.cols = sb("cols", [P, P], F32)
        t.win_of_col = sb("win_of_col", [P, NW * HEADS], F32)
        t.ones = sb("ones", [P, P], F32)
        t.elem_w = sb("elem_w", [P, HEADS], F32)
        t.fill_at = sb("fill_at", [P, 2 * NW], I32)
        t.src_win = sb("src_win", [P, NG], I32)
        t.dst_win = sb("dst_win", [P, NG], I32)
        t.first_edge = sb("first_edge", [P, NG], I32)
        t.win_base = sb("win_base", [P, NG], F32)
        t.win_lane = sb("win_lane", [P, NG], F32)

        def dram(name, shape, dt):
            return nc.dram_tensor(name, shape, dt, kind="Internal").ap()

        t.rec_dram = dram("edge_records", [EPAD + GE, 8], F32)
        t.row_dram = dram("edge_rows16", [3, EPAD + GE], I16)
        t.rows_dram = dram("rows_by_src", [SCRAP + 2 * NW * GE, ROWW], F32)
        t.key_dram = dram("keys", [NPAD, D], F32)
        t.val_dram = dram("values", [NPAD, VROW], F32)
        tiles = -(-NT // (P // HEADS)) * P
        t.edge_dram = dram("tile_ends", [tiles * 4], F32)
        t.carry_dram = dram("tile_carries", [tiles * 2], F32)

        with ExitStack() as first:
            fb = allocators(nc, first, "first")[0]
            t.rec = fb("rec", [P, EPP, 8], F32)
            t.row16 = fb("row16", [P, 3, EPP], I16)
            prepare(nc, i, t)
            edge_tables(nc, i, t)
        t.edge = sb("edge", [P, NT, 8], F32)
        t.local = sb("local", [P, NT], F32)
        t.valid = sb("valid", [P, NT], F32)
        t.score = sb("score", [P, NT, HEADS], F32)
        t.acc = sb("acc", [P, NW, ROWW], F32)
        layer0_edges(nc, i, t)
        layer0_sum(nc, i, t)
        t.val = sb("val", [P, NW, VROW], F32)
        layer0_nodes(nc, i, t)
        layer1_scores(nc, i, t)
        segment_max(nc, i, t)
        layer1_sum(nc, i, t)
        layer1_nodes(nc, i, t)


INPUTS = ["x", "src", "dst", "edge_type_64", "edge_weight", "L0_gnn_W1", "L0_gnn_b1", "L0_gnn_W2", "L0_gnn_b2",
          "L0_gnn_attn_w", "L0_gnn_attn_b", "L1_gnn_query_emb", "L1_gnn_Wq", "L1_gnn_bq", "L1_gnn_Wk", "L1_gnn_bk",
          "L1_gnn_Wv", "L1_gnn_bv", "L1_gnn_rel_w", "L1_gnn_Wo", "L1_gnn_bo", "L1_gnn_gamma", "L1_gnn_beta"]


def kernel(**inputs):
    import numpy as np
    from concourse import bacc
    from concourse.bass_utils import run_bass_kernel_spmd

    nc = bacc.Bacc("TRN2", target_bir_lowering=False, num_devices=1)
    arrays, args = {}, {}
    for name in INPUTS:
        a = np.ascontiguousarray(inputs[name])
        arrays[f"in_{name}"] = a
        args[name] = nc.dram_tensor(f"in_{name}", a.shape, mybir.dt.from_np(a.dtype), kind="ExternalInput").ap()
    args["out"] = nc.dram_tensor("out_0", (N, D), F32, kind="ExternalOutput").ap()
    build(nc, named(**args))
    result = run_bass_kernel_spmd(nc, [arrays], core_ids=[0])
    return result.results[0]["out_0"]
```

```python
from contextlib import ExitStack

import concourse.bass as bass
from concourse import mybir

ALU = mybir.AluOpType
ACT = mybir.ActivationFunctionType
AX = mybir.AxisListType
F32 = mybir.dt.float32
BF16 = mybir.dt.bfloat16
I32 = mybir.dt.int32
U32 = mybir.dt.uint32
I16 = mybir.dt.int16

P = 128
N, E = 3125, 50000
D, HEADS, HD, RELS = 256, 4, 64, 64
HID = 256
NW = -(-N // P)
NPAD = NW * P
TAIL_NODES = N - (NW - 1) * P
EPP = -(-E // P)
EPAD = EPP * P
TAIL_EDGES = E - (P - 1) * EPP
TPG = 2
GE = TPG * P
NG = (E + NW * (GE - 1)) // GE
NT = NG * TPG
SL = 4
EL = 10
assert NG % SL == 0 and NG % EL == 0 and EL % 2 == 0 and GE == 256
NROWS = NG * GE
TRASH = NROWS
SCRAP = TRASH + P
ROWW = 264
VROW = 260
FH = HD + 2
NO_NODE = 8000
BIG = 1.0e30
EPS = 1.0e-5
CH = 5
CW = NW // CH
COUNT_AFTER = 2
LAYER0, LAYER1 = "layer 0", "layer 1"


def named(**things):
    return type("Named", (), things)


def rounds(eng, count, turn):
    turn(0)
    with eng.Fori(1, count) as r:
        turn(r)


def with_ahead(eng, slots, depth, prep, work):
    def turn(r, last):
        for b in range(slots):
            if b + depth < slots:
                prep(r, b + depth)
            elif not last:
                prep(r + 1, b + depth - slots)
            work(r, b)
    for b in range(depth):
        prep(0, b)
    turn(0, False)
    with eng.Fori(1, NG // slots - 1) as r:
        turn(r, False)
    turn(NG // slots - 1, True)


def allocators(nc, ctx, stage):
    numbers = []

    def sb(name, shape, dt):
        return ctx.enter_context(nc.sbuf_tensor(f"{stage}_{name}", shape, dt))

    def psum(name, shape):
        return ctx.enter_context(nc.psum_tensor(f"{stage}_{name}", shape, F32))

    def sem(name):
        handle = ctx.enter_context(nc.semaphore(f"{stage}_{name}"))
        numbers.append(handle.num)
        return handle

    def sems(names):
        return named(**{n: sem(n) for n in names.split()})

    def slot_sems(names, slots=SL):
        return [[sem(f"{n}_{b}") for b in range(slots)] for n in names.split()]

    def clear():
        if numbers:
            nc.all_engine_barrier(sems_to_clear=range(min(numbers), max(numbers) + 1))

    ctx.callback(clear)
    return sb, psum, sems, slot_sems


def prepare(nc, i, t):
    with ExitStack() as ctx:
        sb, psum, sems, slot_sems = allocators(nc, ctx, "prepare")
        w1 = sb("w1", [P, 2, HEADS * HID], F32)
        w2 = sb("w2", [P, HEADS, 2, HD], F32)
        w2x = sb("w2x", [P, HEADS, 2, FH], F32)
        aw = sb("aw", [P, HEADS, 2 * HD + 1], F32)
        ab = sb("ab", [P, HEADS], F32)
        b1 = sb("b1", [P, HEADS * 2], F32)
        b2 = sb("b2", [P, HEADS, HD], F32)
        b2x = sb("b2x", [P, HEADS, FH], F32)
        junk = sb("junk", [P, HD], F32)
        dots = sb("dots", [P, HEADS, 3, 2], F32)
        x_now = sb("x_now", [P, CW, D], F32)
        x_t = sb("x_t", [P, 2, CW * P], F32)
        hid = sb("hid", [P, HEADS * 2, CW * P], F32)
        ftmp = sb("ftmp", [P, CW, HEADS * FH], F32)
        rec = sb("rec", [P, EPP, 8], F32)
        row16 = sb("row16", [P, 3, EPP], I16)
        neutral = sb("neutral", [P, ROWW], F32)
        pad_rec = sb("pad_rec", [P, TPG, 8], F32)
        pad_row = sb("pad_row", [3, GE], I16)
        src_i = sb("src_i", [P, EPP], I32)
        dst_i = sb("dst_i", [P, EPP], I32)
        typ_i = sb("typ_i", [P, EPP], I32)
        wgt = sb("wgt", [P, EPP], F32)
        low_i = sb("low_i", [P, EPP], I32)
        ones_e = sb("ones_e", [P, EPP], BF16)
        mask = sb("mask", [P, NW, EPP], BF16)
        rank = sb("rank", [P, NW, EPP], F32)
        win_no = sb("win_no", [P, NW], F32)
        win_end = sb("win_end", [P, NW], F32)
        cnt = sb("cnt", [P, 2 * NW], F32)
        tot = sb("tot", [P, 2 * NW], F32)
        below = sb("below", [P, P], F32)
        base = sb("base", [P, NW], F32)
        gi = sb("gi", [P, 2, NW], I32)
        grp = sb("grp", [P, 2, NW], F32)
        cum = sb("cum", [P, 2, NW], F32)
        fst = sb("fst", [P, 2, NW], F32)
        fill = sb("fill", [P, 2, NW], F32)
        no_fill = sb("no_fill", [P, 2, NW], F32)
        scrap = sb("scrap", [P, 2, NW], F32)
        off = sb("off", [P, NW + 1], F32)
        step = sb("step", [P, NW], F32)
        g_no = sb("g_no", [P, NG], F32)
        reach = mask[:, :, :].rearrange("p k j -> p (k j)")[:, 0:NG * NW].rearrange("p (g k) -> p g k", k=NW)
        reach_o = rank[:, :, :].rearrange("p k j -> p (k j)")[:, 0:NG * NW].rearrange("p (g k) -> p g k", k=NW)
        acc_f = rank[:, :, :].rearrange("p k j -> p (k j)")[:, NG * NW:NG * (NW + 4)].rearrange("p (a g) -> p a g", a=4)
        ps_x = [psum(f"ps_x{b}", [P, 512]) for b in range(2)]
        ps_h = [psum(f"ps_h{b}", [P, 512]) for b in range(2)]
        ps_f = [psum(f"ps_f{b}", [P, 512]) for b in range(2)]
        ps_c = psum("ps_c", [P, 512])
        s = sems("pad_set const_set ident_set tri_set x_in w_in e_in prep w2x_set x_turned xt_copied hid_made "
                       "hid_kept f_made f_copied f_hi f_res f_mid f_lo x_staged d counted totals "
                       "neutral_set rows16_set fill_set ranked written")

        with nc.Block() as block:
            @block.sync
            def _(sp):
                sp.dma_start(t.x[:, 0:NW - 1, :], i.x[0:(NW - 1) * P, :].rearrange("(w p) c -> p w c", p=P)).then_inc(s.x_in, 16)
                sp.dma_start(w1[:, :, :].rearrange("p k (h m) -> p k h m", h=HEADS)[:, 0, :, :],
                             i.L0_gnn_W1[:, 0:P, :].rearrange("h p m -> p h m")).then_inc(s.w_in, 16)
                sp.dma_start(w1[:, :, :].rearrange("p k (h m) -> p k h m", h=HEADS)[:, 1, :, :],
                             i.L0_gnn_W1[:, P:2 * P, :].rearrange("h p m -> p h m")).then_inc(s.w_in, 16)
                sp.dma_start(w2[:, :, :, :], i.L0_gnn_W2.rearrange("h (k p) m -> p h k m", p=P)).then_inc(s.w_in, 16)
                sp.dma_start(aw[:, :, :], i.L0_gnn_attn_w.rearrange("h m o -> (h m o)").partition_broadcast(P)
                             .rearrange("p (h m) -> p h m", h=HEADS)).then_inc(s.w_in, 16)
                sp.dma_start(ab[:, :], i.L0_gnn_attn_b.rearrange("h o -> (h o)").partition_broadcast(P)).then_inc(s.w_in, 16)
                sp.dma_start(b1[:, :].rearrange("p (h k) -> p h k", k=2), i.L0_gnn_b1.rearrange("h (k p) -> p h k", p=P),
                             allow_slow_non_contiguous=True).then_inc(s.w_in, 16)
                sp.dma_start(b2[:, :, :], i.L0_gnn_b2.rearrange("h m -> (h m)").partition_broadcast(P)
                             .rearrange("p (h m) -> p h m", h=HEADS)).then_inc(s.w_in, 16)
                sp.wait_ge(s.pad_set, 5)
                sp.dma_start(t.x[0:TAIL_NODES, NW - 1, :], i.x[(NW - 1) * P:N, :]).then_inc(s.x_in, 16)
                for dst_tile, src in ((src_i, i.src), (dst_i, i.dst), (typ_i, i.edge_type_64), (wgt, i.edge_weight)):
                    sp.dma_start(dst_tile[0:P - 1, :], src[0:(P - 1) * EPP].rearrange("(p j) -> p j", p=P - 1)).then_inc(s.e_in, 16)
                    sp.dma_start(dst_tile[P - 1:P, 0:TAIL_EDGES], src[(P - 1) * EPP:E].rearrange("(a j) -> a j", a=1)).then_inc(s.e_in, 16)
                sp.wait_ge(s.rows16_set, 1)
                for r in range(3):
                    sp.dma_start(t.row_dram[r, 0:EPAD].rearrange("(p j) -> p j", p=P), row16[:, r, :]).then_inc(s.written, 16)
                sp.wait_ge(s.neutral_set, 5)
                sp.dma_start(t.rec_dram[EPAD:EPAD + GE, :].rearrange("(q p) c -> p q c", p=P), pad_rec[:, :, :]).then_inc(s.written, 16)
                sp.dma_start(t.row_dram[:, EPAD:EPAD + GE], pad_row[:, :]).then_inc(s.written, 16)
                sp.wait_ge(s.fill_set, 1)
                with sp.Fori(0, 2 * NW) as k:
                    at = sp.value_load(t.fill_at[0:1, bass.ds(k, 1)], min_val=0, max_val=SCRAP + (2 * NW - 1) * GE)
                    sp.dma_start(t.rows_dram[bass.ds(at, GE), :].rearrange("(q p) c -> p q c", p=P), neutral[:, :].unsqueeze(1).broadcast_to([P, TPG, ROWW])).then_inc(s.written, 16)
                sp.wait_ge(s.ranked, 1)
                sp.dma_start(t.rec_dram[0:EPAD, :].rearrange("(p j) c -> p (j c)", p=P),
                             rec[:, :, :].rearrange("p j c -> p (j c)")).then_inc(s.written, 16)
                sp.wait_ge(s.written, 16 * (6 + 2 * NW))

            @block.gpsimd
            def _(pool):
                pool.memset(t.x[:, NW - 1, :], 0.0).then_inc(s.pad_set, 1)
                pool.memset(src_i[:, TAIL_EDGES:EPP], NO_NODE).then_inc(s.pad_set, 1)
                pool.memset(dst_i[:, TAIL_EDGES:EPP], NO_NODE).then_inc(s.pad_set, 1)
                pool.memset(typ_i[:, TAIL_EDGES:EPP], 0).then_inc(s.pad_set, 1)
                pool.memset(wgt[:, TAIL_EDGES:EPP], 0.0).then_inc(s.pad_set, 1)
                pool.memset(t.ident[:, :], 0.0).then_inc(s.ident_set, 1)
                pool.memset(below[:, :], 1.0).then_inc(s.tri_set, 1)
                pool.wait_ge(s.ident_set, 1)
                pool.affine_select(out=t.ident[:, :], in_=t.ident[:, :], compare_op=ALU.not_equal, fill=1.0,
                                   base=0, pattern=[[-1, P]], channel_multiplier=1).then_inc(s.ident_set, 1)
                pool.wait_ge(s.tri_set, 1)
                pool.affine_select(out=below[:, :], in_=below[:, :], compare_op=ALU.is_gt, fill=0.0,
                                   base=0, pattern=[[1, P]], channel_multiplier=-1).then_inc(s.tri_set, 1)
                pool.iota(t.lane[:, :], pattern=[[0, 1]], base=0, channel_multiplier=1,
                          allow_small_or_imprecise_dtypes=True).then_inc(s.const_set, 1)
                pool.iota(t.trash[:, :], pattern=[[0, 1]], base=TRASH, channel_multiplier=1,
                          allow_small_or_imprecise_dtypes=True).then_inc(s.const_set, 1)
                pool.iota(win_no[:, :], pattern=[[1, NW]], base=0, channel_multiplier=0,
                          allow_small_or_imprecise_dtypes=True).then_inc(s.const_set, 1)
                pool.iota(win_end[:, :], pattern=[[P, NW]], base=P, channel_multiplier=0,
                          allow_small_or_imprecise_dtypes=True).then_inc(s.const_set, 1)
                pool.iota(scrap[:, :, :], pattern=[[GE, 2 * NW]], base=SCRAP, channel_multiplier=0,
                          allow_small_or_imprecise_dtypes=True).then_inc(s.const_set, 1)
                pool.iota(g_no[:, :], pattern=[[1, NG]], base=0, channel_multiplier=0,
                          allow_small_or_imprecise_dtypes=True).then_inc(s.const_set, 1)
                pool.iota(t.cols[:, :], pattern=[[1, P]], base=0, channel_multiplier=0,
                          allow_small_or_imprecise_dtypes=True).then_inc(s.const_set, 1)
                pool.iota(t.win_of_col[:, :], pattern=[[1, NW], [0, HEADS]], base=0, channel_multiplier=0,
                          allow_small_or_imprecise_dtypes=True).then_inc(s.const_set, 1)
                pool.memset(t.ones[:, :], 1.0).then_inc(s.const_set, 1)
                pool.memset(ones_e[:, :], 1.0).then_inc(s.const_set, 1)
                pool.memset(neutral[:, 0:D], 0.0).then_inc(s.neutral_set, 1)
                pool.memset(neutral[:, D:D + HEADS], -BIG).then_inc(s.neutral_set, 1)
                pool.memset(neutral[:, D + HEADS:ROWW], -1.0).then_inc(s.neutral_set, 1)
                pool.memset(pad_rec[:, :, :], float(NO_NODE)).then_inc(s.neutral_set, 1)
                pool.memset(pad_row[:, :], NO_NODE).then_inc(s.neutral_set, 1)
                pool.wait_ge(s.x_in, 32)
                pool.tensor_copy(x_now[:, :, :], t.x[:, 0:CW, :]).then_inc(s.x_staged, 1)

                def split_rest(c):
                    def part(w, k):
                        return t.table3[:, bass.ds(c * CW + w, 1), k * ROWW:k * ROWW + HEADS * FH].rearrange("p a f -> p (a f)")

                    def third(w):
                        pool.wait_ge(s.f_mid, c * CW + w + 1)
                        nc.gpsimd.tensor_tensor(part(w, 2), ftmp[:, w, :], part(w, 1), ALU.subtract).then_inc(s.f_lo, 1)
                    for w in range(CW):
                        pool.wait_ge(s.f_hi, c * CW + w + 1)
                        nc.gpsimd.tensor_tensor(ftmp[:, w, :], ftmp[:, w, :], part(w, 0), ALU.subtract).then_inc(s.f_res, 1)
                        if w >= 2:
                            third(w - 2)
                    third(CW - 2)
                    third(CW - 1)

                def turn(c):
                    pool.wait_ge(s.x_turned, (c + 1) * CW)
                    pool.tensor_copy(x_now[:, :, :], t.x[:, bass.ds(c * CW + CW, CW), :]).then_inc(s.x_staged, 1)
                    split_rest(c)
                rounds(pool, CH - 1, turn)
                split_rest(CH - 1)

            @block.tensor
            def _(pe):
                pe.wait_ge(s.ident_set, 2)
                pe.wait_ge(s.w_in, 16 * 7)
                pe.wait_ge(s.const_set, 10)
                def turn(c):
                    pe.wait_ge(s.x_staged, c + 1)
                    for w in range(CW):
                        k = c * CW + w
                        xw = x_now[:, w, :]
                        if w < 2:
                            pe.wait_ge(s.xt_copied, c * CW)
                        else:
                            pe.wait_ge(s.xt_copied, k - 1)
                        for half in range(2):
                            last = nc.tensor.transpose(ps_x[w % 2][:, half * P:(half + 1) * P], xw[:, half * P:(half + 1) * P], t.ident[:, :])
                        last.then_inc(s.x_turned, 1)
                    pe.wait_ge(s.xt_copied, (c + 1) * CW)
                    for m in range(HEADS * 2):
                        for nh in range(2):
                            k = m * 2 + nh
                            b = k % 2
                            if k < 2:
                                pe.wait_ge(s.hid_kept, c * HEADS * 4)
                            else:
                                pe.wait_ge(s.hid_kept, c * HEADS * 4 + k - 1)
                            half = CW * P // 2
                            for kk in range(2):
                                last = nc.tensor.matmul(ps_h[b][:, 0:half], w1[:, kk, m * P:(m + 1) * P],
                                                        x_t[:, kk, nh * half:(nh + 1) * half], start=kk == 0, stop=kk == 1)
                            last.then_inc(s.hid_made, 1)
                    pe.wait_ge(s.hid_kept, (c + 1) * HEADS * 4)
                    pe.wait_ge(s.w2x_set, 1)
                    for w in range(CW):
                        if w < 2:
                            pe.wait_ge(s.f_hi, c * CW)
                        else:
                            pe.wait_ge(s.f_hi, c * CW + w - 1)
                        nc.tensor.matmul(ps_f[w % 2][:, 0:HEADS * FH], t.ones[0:1, 0:P], b2x[0:1, :, :].rearrange("p h f -> p (h f)"),
                                         start=True, stop=False)
                        for h in range(HEADS):
                            for kk in range(2):
                                last = nc.tensor.matmul(ps_f[w % 2][:, h * FH:(h + 1) * FH], hid[:, 2 * h + kk, w * P:(w + 1) * P],
                                                        w2x[:, h, kk, :], start=False, stop=(h, kk) == (HEADS - 1, 1))
                        last.then_inc(s.f_made, 1)
                for c in range(COUNT_AFTER):
                    turn(c)
                pe.wait_ge(s.counted, 1)
                pe.wait_ge(s.tri_set, 2)
                nc.tensor.matmul(ps_c[:, 0:NW], below[:, :], cnt[:, 0:NW], start=True, stop=True)
                nc.tensor.matmul(ps_c[:, 64:64 + 2 * NW], t.ones[:, 0:P], cnt[:, :], start=True, stop=True).then_inc(s.totals, 1)
                with pe.Fori(COUNT_AFTER, CH) as c:
                    turn(c)

            @block.scalar
            def _(act):
                act.wait_ge(s.w_in, 16 * 7)
                def turn(c):
                    for w in range(CW):
                        act.wait_ge(s.x_turned, c * CW + w + 1)
                        nc.scalar.activation(x_t[:, :, w * P:(w + 1) * P], ps_x[w % 2][:, 0:2 * P].rearrange("p (k n) -> p k n", k=2),
                                             ACT.Copy).then_inc(s.xt_copied, 1)
                    for m in range(HEADS * 2):
                        for nh in range(2):
                            k = m * 2 + nh
                            half = CW * P // 2
                            act.wait_ge(s.hid_made, c * HEADS * 4 + k + 1)
                            nc.scalar.activation(hid[:, m, nh * half:(nh + 1) * half], ps_h[k % 2][:, 0:half], ACT.Relu,
                                                 bias=b1[:, m:m + 1]).then_inc(s.hid_kept, 1)
                    def second_part(w):
                        mid = t.table3[:, bass.ds(c * CW + w, 1), ROWW:ROWW + HEADS * FH].rearrange("p a f -> p (a f)")
                        act.wait_ge(s.f_res, c * CW + w + 1)
                        nc.scalar.activation(mid, ftmp[:, w, :], ACT.Copy).then_inc(s.f_mid, 1)
                    act.wait_ge(s.f_lo, c * CW)
                    for w in range(CW):
                        hi = t.table3[:, bass.ds(c * CW + w, 1), 0:HEADS * FH].rearrange("p a f -> p (a f)")
                        act.wait_ge(s.f_made, c * CW + w + 1)
                        nc.scalar.activation(ftmp[:, w, :], ps_f[w % 2][:, 0:HEADS * FH], ACT.Copy).then_inc(s.f_copied, 1)
                        nc.scalar.activation(hi, ps_f[w % 2][:, 0:HEADS * FH], ACT.Copy).then_inc(s.f_hi, 1)
                        if w >= 2:
                            second_part(w - 2)
                    second_part(CW - 2)
                    second_part(CW - 1)
                rounds(act, CH, turn)

            @block.vector
            def _(dve):
                done = [0]

                def step_done(ins):
                    done[0] += 1
                    ins.then_inc(s.d, 1)
                    dve.wait_ge(s.d, done[0])

                dve.wait_ge(s.w_in, 16 * 7)
                for h in range(HEADS):
                    for part in range(2):
                        a = aw[:, h, part * HD:(part + 1) * HD]
                        for q in range(3):
                            m = w2[:, h, q, :] if q < 2 else b2[:, h, :]
                            step_done(nc.vector.tensor_tensor_reduce(junk[:, :], m, a, 1.0, 0.0, ALU.mult, ALU.add,
                                                                     dots[:, h, q, part:part + 1]))
                nc.vector.tensor_copy(w2x[:, :, :, 0:HD], w2[:, :, :, :]).then_inc(s.prep, 1)
                nc.vector.tensor_copy(w2x[:, :, :, HD:FH], dots[:, :, 0:2, :]).then_inc(s.prep, 1)
                nc.vector.tensor_copy(b2x[:, :, 0:HD], b2[:, :, :]).then_inc(s.prep, 1)
                step_done(nc.vector.tensor_copy(b2x[:, :, HD:HD + 1], dots[:, :, 2, 0:1]))
                nc.vector.tensor_copy(t.elem_w[:, :], aw[:, :, 2 * HD]).then_inc(s.prep, 1)
                nc.vector.tensor_tensor(b2x[:, :, HD + 1], dots[:, :, 2, 1], ab[:, :], ALU.add).then_inc(s.prep, 1)
                dve.wait_ge(s.prep, 5)
                dve.sem_inc(s.w2x_set, 1)

                dve.wait_ge(s.e_in, 16 * 8)
                dve.wait_ge(s.const_set, 10)
                step_done(nc.vector.tensor_scalar(low_i[:, :], src_i[:, :], P - 1, None, ALU.bitwise_and))
                for c, v in ((0, dst_i), (1, src_i), (2, low_i), (4, wgt)):
                    step_done(nc.vector.tensor_copy(rec[:, :, c], v[:, :]))
                step_done(nc.vector.tensor_scalar(src_i[:, :], src_i[:, :], 7, None, ALU.arith_shift_right))
                step_done(nc.vector.tensor_copy(rec[:, :, 3], src_i[:, :]))
                step_done(nc.vector.memset(rec[:, :, 6:8], 0.0))
                for c, v in enumerate((low_i, dst_i, typ_i)):
                    step_done(nc.vector.tensor_copy(row16[:, c, :], v[:, :]))
                dve.sem_inc(s.rows16_set, 1)

                with dve.Fori(0, NW) as k:
                    row = mask[:, bass.ds(k, 1), :].rearrange("p a j -> p (a j)")
                    nc.vector.tensor_scalar(row, rec[:, :, 0], win_end[:, bass.ds(k, 1)], None, ALU.is_lt).then_inc(s.d, 1)
                done[0] += NW
                dve.wait_ge(s.d, done[0])
                step_done(nc.vector.tensor_reduce(cnt[:, NW:2 * NW], mask[:, :, :], AX.X, ALU.add))
                before = done[0]
                with dve.Fori(0, NW) as k:
                    row = mask[:, bass.ds(k, 1), :].rearrange("p a j -> p (a j)")
                    rnk = rank[:, bass.ds(k, 1), :].rearrange("p a j -> p (a j)")
                    nc.vector.tensor_scalar(row, rec[:, :, 3], win_no[:, bass.ds(k, 1)], None, ALU.is_equal).then_inc(s.d, 1)
                    dve.wait_ge(s.d, 2 * k + before + 1)
                    nc.vector.tensor_tensor_scan(rnk, ones_e[:, :], row, 0.0, ALU.mult, ALU.add).then_inc(s.d, 1)
                done[0] += 2 * NW
                dve.wait_ge(s.d, done[0])
                nc.vector.tensor_copy(cnt[:, 0:NW], rank[:, :, EPP - 1]).then_inc(s.counted, 1)
                dve.wait_ge(s.totals, 1)
                step_done(nc.vector.tensor_copy(tot[:, 0:NW], ps_c[:, 64:64 + NW]))
                step_done(nc.vector.tensor_copy(tot[:, NW:2 * NW], ps_c[:, 64 + NW:64 + 2 * NW]))
                step_done(nc.vector.tensor_copy(off[:, 1:NW + 1], tot[:, NW:2 * NW]))
                step_done(nc.vector.memset(off[:, 0:1], 0.0))
                step_done(nc.vector.tensor_tensor(tot[:, NW:2 * NW], off[:, 1:NW + 1], off[:, 0:NW], ALU.subtract))
                step_done(nc.vector.tensor_scalar(gi[:, :, :].rearrange("p a k -> p (a k)"), tot[:, :], float(GE - 1), None, ALU.add))
                step_done(nc.vector.tensor_scalar(gi[:, :, :], gi[:, :, :], 8, None, ALU.arith_shift_right))
                step_done(nc.vector.tensor_copy(grp[:, :, :], gi[:, :, :]))
                for a in range(2):
                    step_done(nc.vector.tensor_tensor_scan(cum[:, a, :], t.ones[:, 0:NW], grp[:, a, :], 0.0, ALU.mult, ALU.add))
                step_done(nc.vector.tensor_tensor(fst[:, :, :], cum[:, :, :], grp[:, :, :], ALU.subtract))
                step_done(nc.vector.tensor_scalar(base[:, :], fst[:, 0, :], float(GE), -1.0, ALU.mult, ALU.add))
                step_done(nc.vector.tensor_tensor(base[:, :], base[:, :], ps_c[:, 0:NW], ALU.add))
                step_done(nc.vector.tensor_scalar(fill[:, 0, :], cum[:, 0, :], -1.0, None, ALU.add))
                step_done(nc.vector.tensor_scalar(fill[:, 1, :], win_no[:, :], cum[:, 0, NW - 1:NW], None, ALU.add))
                step_done(nc.vector.tensor_scalar(no_fill[:, 0, :], grp[:, 0, :], 0.0, None, ALU.is_equal))
                step_done(nc.vector.tensor_scalar(no_fill[:, 1, :], fill[:, 1, :], float(NG), None, ALU.is_ge))
                step_done(nc.vector.tensor_scalar(fill[:, :, :], fill[:, :, :], float(GE), None, ALU.mult))
                step_done(nc.vector.tensor_tensor(scrap[:, :, :], scrap[:, :, :], fill[:, :, :], ALU.subtract))
                step_done(nc.vector.tensor_tensor(scrap[:, :, :], scrap[:, :, :], no_fill[:, :, :], ALU.mult))
                step_done(nc.vector.tensor_tensor(t.fill_at[:, :], fill[:, :, :].rearrange("p a k -> p (a k)"),
                                                  scrap[:, :, :].rearrange("p a k -> p (a k)"), ALU.add))
                dve.sem_inc(s.fill_set, 1)
                before = done[0]
                with dve.Fori(0, NW) as k:
                    row = mask[:, bass.ds(k, 1), :].rearrange("p a j -> p (a j)")
                    rnk = rank[:, bass.ds(k, 1), :].rearrange("p a j -> p (a j)")
                    nc.vector.scalar_tensor_tensor(rnk, rnk, base[:, bass.ds(k, 1)], row, ALU.add, ALU.mult).then_inc(s.d, 1)
                done[0] += NW
                dve.wait_ge(s.d, done[0])
                step_done(nc.vector.tensor_reduce(rec[:, :, 5], rank[:, :, :].rearrange("p k j -> p j k"), AX.X, ALU.add))
                dve.sem_inc(s.ranked, 1)

                def windows_passed(a):
                    step_done(nc.vector.tensor_tensor(reach[:, :, :], g_no[:, :].unsqueeze(2).broadcast_to([P, NG, NW]),
                                                      cum[:, a, :].unsqueeze(1).broadcast_to([P, NG, NW]), ALU.is_ge))
                    step_done(nc.vector.tensor_reduce(acc_f[:, a, :], reach[:, :, :], AX.X, ALU.add))
                    step_done(nc.vector.tensor_scalar(acc_f[:, a, :], acc_f[:, a, :], float(NW - 1), None, ALU.min))

                windows_passed(0)
                step_done(nc.vector.tensor_copy(t.src_win[:, :], acc_f[:, 0, :]))
                windows_passed(1)
                step_done(nc.vector.tensor_copy(t.dst_win[:, :], acc_f[:, 1, :]))
                step_done(nc.vector.tensor_scalar(t.win_base[:, :], acc_f[:, 1, :], float(P), None, ALU.mult))
                step_done(nc.vector.tensor_scalar(t.win_lane[:, :], t.win_base[:, :], t.lane[:, 0:1], None, ALU.add))
                step_done(nc.vector.scalar_tensor_tensor(off[:, 0:NW], fst[:, 1, :], -float(GE), off[:, 0:NW], ALU.mult, ALU.add))
                step_done(nc.vector.tensor_tensor(step[:, 0:NW - 1], off[:, 1:NW], off[:, 0:NW - 1], ALU.subtract))
                step_done(nc.vector.memset(step[:, NW - 1:NW], float(2 * E)))
                step_done(nc.vector.tensor_tensor(reach_o[:, :, :], reach[:, :, :], step[:, :].unsqueeze(1).broadcast_to([P, NG, NW]), ALU.mult))
                step_done(nc.vector.tensor_reduce(acc_f[:, 2, :], reach_o[:, :, :], AX.X, ALU.add))
                step_done(nc.vector.scalar_tensor_tensor(acc_f[:, 3, :], g_no[:, :], float(GE), acc_f[:, 2, :], ALU.mult, ALU.add))
                step_done(nc.vector.tensor_scalar(t.first_edge[:, :], acc_f[:, 3, :], float(E), None, ALU.min))


def layer0_edges(nc, i, t):
    with ExitStack() as ctx:
        sb, psum, sems, slot_sems = allocators(nc, ctx, "layer0_edges")
        TERMS = NW + 2
        DST_TERM, WEIGHT_TERM = NW * HEADS, (NW + 1) * HEADS
        wide = sb("wide", [P, EL, 2, GE], I16)
        hot = sb("hot", [P, EL, 2, GE], BF16)
        terms = sb("terms", [P, EL, TPG, TERMS * HEADS], F32)
        weighted = sb("weighted", [P, NT, HEADS], F32)
        row = sb("row", [P, EL, TPG, ROWW], F32)
        at = sb("at", [P, EL, TPG], U32)
        at_f = sb("at_f", [P, NT], F32)
        ps_f = [psum(f"ps_f{b}", [P, TPG, 512]) for b in range(2)]
        ps_a = [psum(f"ps_a{b}", [P, TPG, 256]) for b in range(2)]
        s = sems("d turn load_turn row_zero recorded")
        rec_in, wide_in, hot_made, a_ready, f_ready = slot_sems("rec_in wide_in hot_made a_ready f_ready", EL)
        picked, terms_in, at_set, summed, f_copied = slot_sems("picked terms_in at_set summed f_copied", EL)
        row_out = t.row_out
        with nc.Block() as block:
            @block.sync
            def _(sp):
                def turn(r):
                    sp.wait_ge(s.recorded, r)
                    sp.sem_inc(s.load_turn, 1)
                    for b in range(EL):
                        g = EL * r + b
                        e0 = sp.value_load(t.first_edge[0:1, bass.ds(g, 1)], min_val=0, max_val=E)
                        sp.dma_start(t.edge[:, bass.ds(g * TPG, TPG), :],
                                     t.rec_dram[bass.ds(e0, GE), :].rearrange("(q p) c -> p q c", p=P)).then_inc(rec_in[b], 16)
                        sp.wait_ge(hot_made[b], r)
                        sp.sem_inc(s.load_turn, 1)
                        sp.dma_start(wide[:, b, :, :], t.row_dram[0:2, bass.ds(e0, GE)].partition_broadcast(P)).then_inc(wide_in[b], 16)
                rounds(sp, NG // EL, turn)

            @block.vector
            def _(dve):
                nc.vector.memset(row[:, :, :, D + HEADS:ROWW], 0.0).then_inc(s.row_zero, 1)

                def one_hots(r, b, g):
                    dve.wait_ge(wide_in[b], 16 * (r + 1))
                    dve.wait_ge(f_ready[b], r)
                    nc.vector.tensor_scalar(hot[:, b, 0, :], wide[:, b, 0, :], t.lane[:, 0:1], None, ALU.is_equal)
                    nc.vector.tensor_scalar(hot[:, b, 1, :], wide[:, b, 1, :], t.win_lane[:, bass.ds(g, 1)], None,
                                            ALU.is_equal).then_inc(hot_made[b], 1)

                STEPS = 4

                def records(r):
                    n = r * STEPS
                    tiles = bass.ds(r * EL * TPG, EL * TPG)
                    groups = bass.ds(r * EL, EL)
                    dst = t.edge[:, tiles, 0].rearrange("p (g q) -> p g q", q=TPG)
                    for b in range(EL):
                        dve.wait_ge(rec_in[b], 16 * (r + 1))
                    nc.vector.tensor_tensor(t.local[:, tiles].rearrange("p (g q) -> p g q", q=TPG), dst,
                                            t.win_base[:, groups].unsqueeze(2).broadcast_to([P, EL, TPG]), ALU.subtract).then_inc(s.d, 1)
                    nc.vector.tensor_tensor(weighted[:, tiles, :], t.edge[:, tiles, 4:5].broadcast_to([P, EL * TPG, HEADS]),
                                            t.elem_w[:, :].unsqueeze(1).broadcast_to([P, EL * TPG, HEADS]), ALU.mult).then_inc(s.d, 1)
                    dve.wait_ge(s.d, n + 2)
                    nc.vector.tensor_scalar(t.valid[:, tiles], t.local[:, tiles], float(P), None, ALU.is_lt).then_inc(s.d, 1)
                    dve.wait_ge(s.d, n + 3)
                    nc.vector.scalar_tensor_tensor(at_f[:, tiles], t.edge[:, tiles, 5], t.trash[:, 0:1], t.valid[:, tiles],
                                                   ALU.subtract, ALU.mult).then_inc(s.d, 1)
                    dve.wait_ge(s.d, n + 4)
                    dve.sem_inc(s.recorded, 1)

                def pick(r, b, g):
                    dve.wait_ge(a_ready[b], r + 1)
                    dve.wait_ge(summed[b], r)
                    for q in range(TPG):
                        nc.vector.scalar_tensor_tensor(terms[:, b, q, 0:NW * HEADS], t.win_of_col[:, :],
                                                       t.edge[:, bass.ds(g * TPG + q, 1), 3:4].rearrange("p a c -> p (a c)"),
                                                       ps_a[b % 2][:, q, 0:NW * HEADS], ALU.is_equal, ALU.mult).then_inc(picked[b], 1)

                def addresses(r, b, g):
                    dve.wait_ge(row_out[b], 16 * TPG * r)
                    nc.vector.tensor_scalar(at[:, b, :], at_f[:, bass.ds(g * TPG, TPG)], t.trash[:, 0:1], None, ALU.add).then_inc(at_set[b], 1)

                def sum_terms(r, b):
                    dve.wait_ge(picked[b], TPG * (r + 1))
                    dve.wait_ge(terms_in[b], 2 * (r + 1))
                    nc.vector.tensor_reduce(row[:, b, :, D:D + HEADS], terms[:, b, :, :].rearrange("p q (w h) -> p q h w", h=HEADS),
                                            AX.X, ALU.add).then_inc(summed[b], 1)

                def keep_scores(r):
                    dve.wait_ge(summed[EL - 1], r + 1)
                    nc.vector.tensor_scalar(t.score[:, bass.ds(r * EL * TPG, EL * TPG), :],
                                            row[:, :, :, D:D + HEADS].rearrange("p g q h -> p (g q) h"), 0.0, None, ALU.add)

                def body(r, last):
                    for b in range(EL):
                        pick(r, b, EL * r + b)
                        if b < EL - 2:
                            one_hots(r, b + 2, EL * r + b + 2)
                        elif not last:
                            one_hots(r + 1, b + 2 - EL, EL * r + b + 2)
                        addresses(r, b, EL * r + b)
                        if b == EL - 1 and not last:
                            records(r + 1)
                        sum_terms(r, b)
                    keep_scores(r)

                one_hots(0, 0, 0)
                one_hots(0, 1, 1)
                records(0)
                dve.wait_ge(s.row_zero, 1)
                body(0, False)
                with dve.Fori(1, NG // EL - 1) as r:
                    body(r, False)
                body(NG // EL - 1, True)

            @block.tensor
            def _(pe):
                def turn(r):
                    for b in range(EL):
                        win = pe.value_load(t.dst_win[0:1, bass.ds(EL * r + b, 1)], min_val=0, max_val=NW - 1)
                        pe.wait_ge(hot_made[b], r + 1)
                        pe.wait_ge(picked[(b - 2) % EL], TPG * (r + (b >= 2)))
                        for q in range(TPG):
                            for k in range(3):
                                last = nc.tensor.matmul(ps_a[b % 2][:, q, 0:NW * HEADS], hot[:, b, 0, q * P:(q + 1) * P],
                                                        t.table3[:, :, k * ROWW + HD:k * ROWW + HEADS * FH:FH],
                                                        start=k == 0, stop=k == 2)
                        last.then_inc(a_ready[b], 1)
                        pe.wait_ge(f_copied[(b - 2) % EL], r + (b >= 2))
                        for q in range(TPG):
                            for k in range(3):
                                feats = t.table3[:, bass.ds(win, 1), k * ROWW:k * ROWW + HEADS * FH].rearrange("p a f -> p (a f)")
                                last = nc.tensor.matmul(ps_f[b % 2][:, q, 0:HEADS * FH], hot[:, b, 1, q * P:(q + 1) * P], feats,
                                                        start=k == 0, stop=k == 2)
                        last.then_inc(f_ready[b], 1)
                rounds(pe, NG // EL, turn)

            @block.scalar
            def _(act):
                act.wait_ge(s.row_zero, 1)
                def turn(r):
                    act.wait_ge(s.recorded, r + 1)
                    for b in range(EL):
                        tiles = bass.ds((EL * r + b) * TPG, TPG)
                        act.wait_ge(summed[b], r)
                        nc.scalar.activation(terms[:, b, :, WEIGHT_TERM:WEIGHT_TERM + HEADS], weighted[:, tiles, :], ACT.Copy).then_inc(terms_in[b], 1)
                        act.wait_ge(row_out[b], 16 * TPG * r)
                        nc.scalar.activation(row[:, b, :, D + HEADS], t.edge[:, tiles, 2], ACT.Copy)
                        act.wait_ge(f_ready[b], r + 1)
                        nc.scalar.activation(terms[:, b, :, DST_TERM:DST_TERM + HEADS], ps_f[b % 2][:, :, HD + 1:HEADS * FH:FH],
                                             ACT.Copy).then_inc(terms_in[b], 1)
                        for q in range(TPG):
                            last = nc.scalar.activation(row[:, b, q, 0:D].rearrange("p (h f) -> p h f", h=HEADS),
                                                        ps_f[b % 2][:, q, 0:HEADS * FH].rearrange("p (h f) -> p h f", h=HEADS)[:, :, 0:HD],
                                                        ACT.Copy)
                        last.then_inc(f_copied[b], 1)
                rounds(act, NG // EL, turn)

            @block.gpsimd
            def _(pool):
                def turn(r):
                    for b in range(EL):
                        pool.wait_ge(f_copied[b], r + 1)
                        pool.wait_ge(at_set[b], r + 1)
                        pool.wait_ge(summed[b], r + 1)
                        pool.sem_inc(s.turn, 1)
                        for q in range(TPG):
                            pool.indirect_dma_start(t.rows_dram, bass.IndirectOffsetOnAxis(ap=at[:, b, q:q + 1], axis=0),
                                                    row[:, b, q, :], None, bounds_check=NROWS - 1,
                                                    oob_is_err=False).then_inc(row_out[b], 16)
                rounds(pool, NG // EL, turn)
                for b in range(EL):
                    pool.wait_ge(row_out[b], 16 * TPG * (NG // EL))


def layer0_sum(nc, i, t):
    with ExitStack() as ctx:
        sb, psum, sems, slot_sems = allocators(nc, ctx, "layer0_sum")
        PSL = EL // 2
        hide = sb("hide", [P, NT], F32)
        masked = sb("masked", [P, NT, HEADS], F32)
        top_lane = sb("top_lane", [P, HEADS], F32)
        top = sb("top", [P, HEADS], F32)
        rin = sb("rin", [P, EL, TPG, ROWW], F32)
        rel = sb("rel", [P, EL, TPG, HEADS], F32)
        hot = sb("hot", [P, EL, TPG, P], F32)
        rhs = sb("rhs", [P, EL, TPG, D + HEADS], F32)
        ps = [psum(f"ps{b}", [P, 512]) for b in range(PSL)]
        s = sems("d lane_top top_set acc_zero")
        rows_in, rel_made, hot_made, weighed, summed, kept = slot_sems("rows_in rel_made hot_made weighed summed kept", EL)
        scaled_act, scaled_dve, scaled_pool = slot_sems("scaled_act scaled_dve scaled_pool", EL)

        with nc.Block() as block:
            @block.sync
            def _(sp):
                def turn(r):
                    for b in range(EL):
                        sp.wait_ge(hot_made[b], r)
                        sp.wait_ge(rel_made[b], r)
                        sp.wait_ge(scaled_act[b], r)
                        sp.wait_ge(scaled_dve[b], r)
                        sp.wait_ge(scaled_pool[b], r)
                        sp.dma_start(rin[:, b, :, :], t.rows_dram[bass.ds((EL * r + b) * GE, GE), :]
                                     .rearrange("(q p) c -> p q c", p=P)).then_inc(rows_in[b], 16)
                rounds(sp, NG // EL, turn)

            @block.gpsimd
            def _(pool):
                pool.memset(t.acc[:, :, :], 0.0).then_inc(s.acc_zero, 1)
                pool.wait_ge(s.lane_top, 1)
                pool.partition_all_reduce(top[:, :], top_lane[:, :], P, bass.bass_isa.ReduceOp.max).then_inc(s.top_set, 1)
                pool.wait_ge(s.top_set, 1)

                def below_top(r, b):
                    pool.wait_ge(rows_in[b], 16 * (r + 1))
                    pool.wait_ge(weighed[b], r)
                    nc.gpsimd.tensor_tensor(rel[:, b, :, :], rin[:, b, :, D:D + HEADS],
                                            top[:, :].unsqueeze(1).broadcast_to([P, TPG, HEADS]), ALU.subtract).then_inc(rel_made[b], 1)

                def scale(r, b):
                    pool.wait_ge(weighed[b], r + 1)
                    pool.wait_ge(summed[b], r)
                    nc.gpsimd.tensor_tensor(rhs[:, b, 1, 0:D].rearrange("p (h f) -> p h f", h=HEADS),
                                            rin[:, b, 1, 0:D].rearrange("p (h f) -> p h f", h=HEADS),
                                            rhs[:, b, 1, D:D + HEADS].unsqueeze(2).broadcast_to([P, HEADS, HD]),
                                            ALU.mult).then_inc(scaled_pool[b], 1)
                with_ahead(pool, EL, 2, below_top, scale)

            @block.scalar
            def _(act):
                def weights(r, b):
                    act.wait_ge(rel_made[b], r + 1)
                    act.wait_ge(summed[b], r)
                    nc.scalar.activation(rhs[:, b, :, D:D + HEADS], rel[:, b, :, :], ACT.Exp).then_inc(weighed[b], 1)

                def scale(r, b):
                    act.wait_ge(weighed[b], r + 1)
                    for h in range(HEADS // 2, HEADS):
                        last = nc.scalar.activation(rhs[:, b, 0, h * HD:(h + 1) * HD], rin[:, b, 0, h * HD:(h + 1) * HD], ACT.Copy,
                                                    scale=rhs[:, b, 0, D + h:D + h + 1])
                    last.then_inc(scaled_act[b], 1)
                with_ahead(act, EL, 1, weights, scale)

            @block.tensor
            def _(pe):
                def turn(r):
                    for b in range(EL):
                        pe.wait_ge(hot_made[b], r + 1)
                        pe.wait_ge(scaled_act[b], r + 1)
                        pe.wait_ge(scaled_dve[b], r + 1)
                        pe.wait_ge(scaled_pool[b], r + 1)
                        pe.wait_ge(kept[(b - PSL) % EL], r + (b >= PSL))
                        for q in range(TPG):
                            last = nc.tensor.matmul(ps[b % PSL][:, 0:D + HEADS], hot[:, b, q, :], rhs[:, b, q, :],
                                                    start=q == 0, stop=q == TPG - 1)
                        last.then_inc(summed[b], 1)
                rounds(pe, NG // EL, turn)

            @block.vector
            def _(dve):
                nc.vector.tensor_scalar(hide[:, :], t.valid[:, :], 1.0, BIG, ALU.subtract, ALU.mult).then_inc(s.d, 1)
                dve.wait_ge(s.d, 1)
                nc.vector.tensor_tensor(masked[:, :, :], t.score[:, :, :], hide[:, :].unsqueeze(2).broadcast_to([P, NT, HEADS]),
                                        ALU.add).then_inc(s.d, 1)
                dve.wait_ge(s.d, 2)
                nc.vector.tensor_reduce(top_lane[:, :], masked[:, :, :].rearrange("p n h -> p h n"), AX.X, ALU.max).then_inc(s.lane_top, 1)
                dve.wait_ge(s.acc_zero, 1)

                def one_hots(r, b):
                    dve.wait_ge(rows_in[b], 16 * (r + 1))
                    dve.wait_ge(summed[b], r)
                    for q in range(TPG):
                        last = nc.vector.tensor_scalar(hot[:, b, q, :], t.cols[:, :], rin[:, b, q, D + HEADS:D + HEADS + 1], None, ALU.is_equal)
                    last.then_inc(hot_made[b], 1)

                def add_group(r, b):
                    win = dve.value_load(t.src_win[0:1, bass.ds(EL * r + b, 1)], min_val=0, max_val=NW - 1)
                    sums = t.acc[:, bass.ds(win, 1), 0:D + HEADS].rearrange("p a f -> p (a f)")
                    dve.wait_ge(summed[b], r + 1)
                    dve.wait_ge(kept[(b - 1) % EL], r + (b > 0))
                    nc.vector.tensor_tensor(sums, sums, ps[b % PSL][:, 0:D + HEADS], ALU.add).then_inc(kept[b], 1)

                def scale(r, b):
                    dve.wait_ge(weighed[b], r + 1)
                    half = HEADS // 2
                    nc.vector.tensor_tensor(rhs[:, b, 0, 0:half * HD].rearrange("p (h f) -> p h f", h=half),
                                            rin[:, b, 0, 0:half * HD].rearrange("p (h f) -> p h f", h=half),
                                            rhs[:, b, 0, D:D + half].unsqueeze(2).broadcast_to([P, half, HD]),
                                            ALU.mult).then_inc(scaled_dve[b], 1)

                def turn(r, last):
                    for b in range(EL):
                        if b < EL - 3:
                            one_hots(r, b + 3)
                        elif not last:
                            one_hots(r + 1, b + 3 - EL)
                        if b < EL - 2:
                            scale(r, b + 2)
                        elif not last:
                            scale(r + 1, b + 2 - EL)
                        add_group(r, b)
                for b in range(3):
                    one_hots(0, b)
                for b in range(2):
                    scale(0, b)
                turn(0, False)
                with dve.Fori(1, NG // EL - 1) as r:
                    turn(r, False)
                turn(NG // EL - 1, True)


MOMENT_STEPS = 2 * CW


def moments(nc, dve, d, n, carried, v, stats, mean_var, var_eps, var_made):
    dve.wait_ge(d, n)
    for w in range(CW):
        nc.vector.bn_stats(stats[:, w, :], v[:, w, :]).then_inc(d, 1)
    dve.wait_ge(d, n + CW)
    dve.sem_inc(carried, 1)
    for w in range(CW):
        nc.vector.bn_aggr(mean_var[:, w, :], stats[:, w, :]).then_inc(d, 1)
    dve.wait_ge(d, n + 2 * CW)
    nc.vector.tensor_scalar(var_eps[:, :], mean_var[:, :, 1], EPS, None, ALU.add).then_inc(var_made, 1)


def layer0_nodes(nc, i, t):
    with ExitStack() as ctx:
        sb, psum, sems, slot_sems = allocators(nc, ctx, "layer0_nodes")
        wqkv = sb("wqkv", [P, 2, 3 * D], F32)
        bqkv = sb("bqkv", [1, 3 * D], F32)
        query = sb("query", [P, D], F32)
        node_no = sb("node_no", [P, NW], F32)
        zero_w = sb("zero_w", [P, CW, HEADS], F32)
        den = sb("den", [P, CW, HEADS], F32)
        v = sb("v", [P, CW, D], F32)
        any_zero = sb("any_zero", [P, CW], F32)
        stats = sb("stats", [P, CW, 6], F32)
        mean_var = sb("mean_var", [P, CW, 2], F32)
        var_eps = sb("var_eps", [P, CW], F32)
        rstd = sb("rstd", [P, CW], F32)
        enh = sb("enh", [P, CW, D], F32)
        enh_t = sb("enh_t", [P, 2, CW * P], F32)
        qtmp = sb("qtmp", [P, CW, D], F32)
        qres = sb("qres", [P, CW, D], F32)
        keys = sb("keys", [P, CW, D], F32)
        ps_x = [psum(f"ps_x{b}", [P, 512]) for b in range(2)]
        ps_qk = [psum(f"ps_qk{b}", [P, 512]) for b in range(2)]
        ps_v = [psum(f"ps_v{b}", [P, 512]) for b in range(2)]
        s = sems("w_in q_in pad_zero scaled d carried var_made rooted normed enh_made turned enh_t_made projected "
                 "q_hi q_rest q_mid q_lo kv_kept k_out v_out")
        with nc.Block() as block:
            @block.sync
            def _(sp):
                for c, w in enumerate((i.L1_gnn_Wq, i.L1_gnn_Wk, i.L1_gnn_Wv)):
                    sp.dma_start(wqkv[:, :, c * D:(c + 1) * D], w.rearrange("(k p) m -> p k m", p=P)).then_inc(s.w_in, 16)
                for c, w in enumerate((i.L1_gnn_bq, i.L1_gnn_bk, i.L1_gnn_bv)):
                    sp.dma_start(bqkv[:, c * D:(c + 1) * D], w.rearrange("(a m) -> a m", a=1)).then_inc(s.w_in, 16)
                sp.dma_start(query[:, :], i.L1_gnn_query_emb.partition_broadcast(P)).then_inc(s.q_in, 16)
                def turn(c):
                    sp.wait_ge(s.kv_kept, (c + 1) * CW)
                    sp.dma_start(t.key_dram[bass.ds(c * CW * P, CW * P), :].rearrange("(w p) m -> p w m", p=P), keys[:, :, :]).then_inc(s.k_out, 16)
                    sp.dma_start(t.val_dram[bass.ds(c * CW * P, CW * P), :].rearrange("(w p) m -> p w m", p=P),
                                 t.val[:, bass.ds(c * CW, CW), :]).then_inc(s.v_out, 16)
                rounds(sp, CH, turn)
                sp.wait_ge(s.k_out, 16 * CH)
                sp.wait_ge(s.v_out, 16 * CH)

            @block.gpsimd
            def _(pool):
                pool.memset(t.val[:, :, D:VROW], 0.0).then_inc(s.pad_zero, 1)
                pool.iota(node_no[:, :], pattern=[[P, NW]], base=0, channel_multiplier=1,
                          allow_small_or_imprecise_dtypes=True).then_inc(s.pad_zero, 1)
                pool.wait_ge(s.q_in, 16)
                pool.tensor_scalar(query[:, :], query[:, :], 0.1, None, ALU.mult).then_inc(s.scaled, 1)

            @block.vector
            def _(dve):
                dve.wait_ge(s.pad_zero, 2)
                dve.wait_ge(s.scaled, 1)

                def norm(c):
                    n = c * DSTEPS
                    weights = t.acc[:, bass.ds(c * CW, CW), D:D + HEADS]
                    x = t.x[:, bass.ds(c * CW, CW), :]
                    nc.vector.tensor_scalar(zero_w[:, :, :], weights, 0.0, None, ALU.is_equal).then_inc(s.d, 1)
                    dve.wait_ge(s.d, n + 1)
                    nc.vector.tensor_tensor(den[:, :, :], weights, zero_w[:, :, :], ALU.add).then_inc(s.d, 1)
                    nc.vector.tensor_reduce(any_zero[:, :], zero_w[:, :, :], AX.X, ALU.max).then_inc(s.d, 1)
                    dve.wait_ge(s.d, n + 2)
                    nc.vector.reciprocal(den[:, :, :], den[:, :, :]).then_inc(s.d, 1)
                    dve.wait_ge(s.d, n + 3)
                    nc.vector.scalar_tensor_tensor(t.val[:, bass.ds(c * CW, CW), D], node_no[:, bass.ds(c * CW, CW)], float(N), any_zero[:, :],
                                                   ALU.is_lt, ALU.mult).then_inc(s.d, 1)
                    dve.wait_ge(s.d, n + 5)
                    for w in range(CW):
                        nc.vector.tensor_tensor(v[:, w, :].rearrange("p (h f) -> p h f", h=HEADS),
                                                t.acc[:, bass.ds(c * CW + w, 1), 0:D].rearrange("p a (h f) -> p (a h) f", h=HEADS),
                                                den[:, w, :].unsqueeze(2).broadcast_to([P, HEADS, HD]), ALU.mult).then_inc(s.d, 1)
                    dve.wait_ge(s.d, n + 5 + CW)
                    nc.vector.tensor_tensor(v[:, :, :], v[:, :, :], x, ALU.add).then_inc(s.d, 1)
                    moments(nc, dve, s.d, n + 6 + CW, s.carried, v, stats, mean_var, var_eps, s.var_made)
                    dve.wait_ge(s.rooted, c + 1)
                    nc.vector.reciprocal(rstd[:, :], rstd[:, :]).then_inc(s.d, 1)
                    dve.wait_ge(s.d, n + DSTEPS)
                    for w in range(CW):
                        nc.vector.tensor_scalar(t.x[:, bass.ds(c * CW + w, 1), :].rearrange("p a m -> p (a m)"), v[:, w, :],
                                                mean_var[:, w, 0:1], rstd[:, w:w + 1], ALU.subtract, ALU.mult).then_inc(s.normed, 1)
                    dve.wait_ge(s.normed, (c + 1) * CW)
                    dve.wait_ge(s.turned, c * CW)
                    nc.vector.tensor_tensor(enh[:, :, :], x, query[:, :].unsqueeze(1).broadcast_to([P, CW, D]), ALU.add).then_inc(s.enh_made, 1)

                DSTEPS = 6 + CW + MOMENT_STEPS + 1

                def query_part(c, w, part):
                    return t.table3[:, bass.ds(c * CW + w, 1), part * ROWW:part * ROWW + D].rearrange("p a m -> p (a m)")

                def queries_rest(c):
                    def third(w):
                        dve.wait_ge(s.q_mid, c * CW + w + 1)
                        nc.vector.tensor_tensor(query_part(c, w, 2), qres[:, w, :], query_part(c, w, 1), ALU.subtract).then_inc(s.q_lo, 1)
                    for w in range(CW):
                        dve.wait_ge(s.q_hi, c * CW + w + 1)
                        nc.vector.tensor_tensor(qres[:, w, :], qtmp[:, w, :], query_part(c, w, 0), ALU.subtract).then_inc(s.q_rest, 1)
                        if w >= 2:
                            third(w - 2)
                    third(CW - 2)
                    third(CW - 1)

                norm(0)
                norm(1)
                queries_rest(0)
                with dve.Fori(1, CH - 1) as c:
                    norm(c + 1)
                    queries_rest(c)
                queries_rest(CH - 1)

            @block.scalar
            def _(act):
                def root(c):
                    act.wait_ge(s.var_made, c + 1)
                    nc.scalar.activation(rstd[:, :], var_eps[:, :], ACT.Sqrt).then_inc(s.rooted, 1)

                def turned_kept(c):
                    for w in range(CW):
                        act.wait_ge(s.turned, c * CW + w + 1)
                        nc.scalar.activation(enh_t[:, :, w * P:(w + 1) * P], ps_x[w % 2][:, 0:2 * P].rearrange("p (k n) -> p k n", k=2),
                                             ACT.Copy).then_inc(s.enh_t_made, 1)

                def second_part(c, w):
                    act.wait_ge(s.q_rest, c * CW + w + 1)
                    nc.scalar.activation(t.table3[:, bass.ds(c * CW + w, 1), ROWW:ROWW + D].rearrange("p a m -> p (a m)"), qres[:, w, :],
                                         ACT.Copy).then_inc(s.q_mid, 1)

                def projections_kept(c):
                    act.wait_ge(s.k_out, 16 * c)
                    act.wait_ge(s.q_lo, c * CW)
                    for w in range(CW):
                        k, b = c * CW + w, w % 2
                        act.wait_ge(s.projected, k + 1)
                        nc.scalar.activation(qtmp[:, w, :], ps_qk[b][:, 0:D], ACT.Copy)
                        nc.scalar.activation(t.table3[:, bass.ds(k, 1), 0:D].rearrange("p a m -> p (a m)"), ps_qk[b][:, 0:D], ACT.Copy).then_inc(s.q_hi, 1)
                        nc.scalar.activation(keys[:, w, :], ps_qk[b][:, D:2 * D], ACT.Copy)
                        nc.scalar.activation(t.val[:, bass.ds(k, 1), 0:D].rearrange("p a m -> p (a m)"), ps_v[b][:, 0:D], ACT.Copy).then_inc(s.kv_kept, 1)
                        if w >= 2:
                            second_part(c, w - 2)
                    second_part(c, CW - 2)
                    second_part(c, CW - 1)

                root(0)
                turned_kept(0)
                root(1)
                projections_kept(0)
                with act.Fori(1, CH - 1) as c:
                    turned_kept(c)
                    root(c + 1)
                    projections_kept(c)
                turned_kept(CH - 1)
                projections_kept(CH - 1)

            @block.tensor
            def _(pe):
                pe.wait_ge(s.w_in, 16 * 6)
                def turn(c):
                    pe.wait_ge(s.enh_made, c + 1)
                    for w in range(CW):
                        if w < 2:
                            pe.wait_ge(s.enh_t_made, c * CW)
                        else:
                            pe.wait_ge(s.enh_t_made, c * CW + w - 1)
                        for half in range(2):
                            last = nc.tensor.transpose(ps_x[w % 2][:, half * P:(half + 1) * P], enh[:, w, half * P:(half + 1) * P], t.ident[:, :])
                        last.then_inc(s.turned, 1)
                    pe.wait_ge(s.enh_t_made, (c + 1) * CW)
                    for w in range(CW):
                        b = w % 2
                        if w < 2:
                            pe.wait_ge(s.kv_kept, c * CW)
                        else:
                            pe.wait_ge(s.kv_kept, c * CW + w - 1)
                        for k in range(2):
                            nc.tensor.matmul(ps_qk[b][:, :], enh_t[:, k, w * P:(w + 1) * P], wqkv[:, k, 0:2 * D], start=k == 0, stop=False)
                        nc.tensor.matmul(ps_qk[b][:, :], t.ones[0:1, 0:P], bqkv[0:1, 0:2 * D], start=False, stop=True)
                        for k in range(2):
                            nc.tensor.matmul(ps_v[b][:, 0:D], enh_t[:, k, w * P:(w + 1) * P], wqkv[:, k, 2 * D:3 * D], start=k == 0, stop=False)
                        nc.tensor.matmul(ps_v[b][:, 0:D], t.ones[0:1, 0:P], bqkv[0:1, 2 * D:3 * D], start=False, stop=True).then_inc(s.projected, 1)
                rounds(pe, CH, turn)


def layer1_scores(nc, i, t):
    with ExitStack() as ctx:
        sb, psum, sems, slot_sems = allocators(nc, ctx, "layer1_scores")
        rel = sb("rel", [RELS, HD], F32)
        rel_rest = sb("rel_rest", [RELS, HD], F32)
        rel3 = sb("rel3", [RELS, 3, HD], BF16)
        wide = sb("wide", [P, SL, 2, GE], I16)
        hot = sb("hot", [P, SL, GE], BF16)
        hot_r = sb("hot_r", [RELS, SL, GE], BF16)
        at = sb("at", [P, SL, TPG], U32)
        key = sb("key", [P, SL, TPG, D], F32)
        prod = sb("prod", [P, SL, TPG, D], F32)
        ps_q = [psum(f"ps_q{b}", [P, TPG, D]) for b in range(SL)]
        ps_r = [psum(f"ps_r{b}", [P, 512]) for b in range(SL)]
        s = sems("rel_in d turn load_turn")
        wide_in, hot_made, q_ready, at_set, with_rel, multiplied, reduced = slot_sems("wide_in hot_made q_ready at_set with_rel multiplied reduced")
        key_in = t.key_in
        with nc.Block() as block:
            @block.sync
            def _(sp):
                sp.dma_start(rel[:, :], i.L1_gnn_rel_w).then_inc(s.rel_in, 16)
                def turn(r):
                    for b in range(SL):
                        e0 = sp.value_load(t.first_edge[0:1, bass.ds(SL * r + b, 1)], min_val=0, max_val=E)
                        sp.wait_ge(hot_made[b], r)
                        sp.sem_inc(s.load_turn, 1)
                        sp.dma_start(wide[:, b, :, :], t.row_dram[1:3, bass.ds(e0, GE)].partition_broadcast(P)).then_inc(wide_in[b], 16)
                rounds(sp, NG // SL, turn)

            @block.gpsimd
            def _(pool):
                def turn(r):
                    for b in range(SL):
                        pool.wait_ge(at_set[b], r + 1)
                        pool.wait_ge(multiplied[b], r)
                        pool.sem_inc(s.turn, 1)
                        for q in range(TPG):
                            pool.indirect_dma_start(key[:, b, q, :], None, t.key_dram,
                                                    bass.IndirectOffsetOnAxis(ap=at[:, b, q:q + 1], axis=0)).then_inc(key_in[b], 16)
                rounds(pool, NG // SL, turn)

            @block.tensor
            def _(pe):
                def turn(r):
                    for b in range(SL):
                        win = pe.value_load(t.dst_win[0:1, bass.ds(SL * r + b, 1)], min_val=0, max_val=NW - 1)
                        pe.wait_ge(hot_made[b], r + 1)
                        pe.wait_ge(multiplied[b], r)
                        for q in range(TPG):
                            for k in range(3):
                                nc.tensor.matmul(ps_q[b][:, q, :], hot[:, b, q * P:(q + 1) * P],
                                                 t.table3[:, bass.ds(win, 1), k * ROWW:k * ROWW + D].rearrange("p a m -> p (a m)"),
                                                 start=k == 0, stop=k == 2)
                        for q in range(TPG):
                            for k in range(3):
                                last = nc.tensor.matmul(ps_r[b][:, q * HD:(q + 1) * HD], hot_r[:, b, q * P:(q + 1) * P], rel3[:, k, :],
                                                        start=k == 0, stop=k == 2)
                        last.then_inc(q_ready[b], 1)
                rounds(pe, NG // SL, turn)

            @block.vector
            def _(dve):
                dve.wait_ge(s.rel_in, 16)
                steps = (lambda: nc.vector.tensor_scalar(rel[:, :], rel[:, :], 0.2, None, ALU.mult),
                         lambda: nc.vector.tensor_copy(rel3[:, 0, :], rel[:, :]),
                         lambda: nc.vector.tensor_tensor(rel_rest[:, :], rel[:, :], rel3[:, 0, :], ALU.subtract),
                         lambda: nc.vector.tensor_copy(rel3[:, 1, :], rel_rest[:, :]),
                         lambda: nc.vector.tensor_tensor(rel3[:, 2, :], rel_rest[:, :], rel3[:, 1, :], ALU.subtract))
                for n, make in enumerate(steps):
                    make().then_inc(s.d, 1)
                    dve.wait_ge(s.d, n + 1)

                def one_hots(r, b, g):
                    dve.wait_ge(wide_in[b], 16 * (r + 1))
                    dve.wait_ge(q_ready[b], r)
                    nc.vector.tensor_scalar(hot[:, b, :], wide[:, b, 0, :], t.win_lane[:, bass.ds(g, 1)], None, ALU.is_equal)
                    nc.vector.tensor_scalar(hot_r[:, b, :], wide[0:RELS, b, 1, :], t.lane[0:RELS, 0:1], None, ALU.is_equal).then_inc(hot_made[b], 1)

                def addresses(r, b, g):
                    dve.wait_ge(key_in[b], 16 * TPG * r)
                    nc.vector.tensor_scalar(at[:, b, :], t.edge[:, bass.ds(g * TPG, TPG), 1], float(NPAD - 1), None, ALU.min).then_inc(at_set[b], 1)

                def multiply(r, b):
                    dve.wait_ge(key_in[b], 16 * TPG * (r + 1))
                    dve.wait_ge(q_ready[b], r + 1)
                    dve.wait_ge(reduced[b], r)
                    for q in range(TPG):
                        ins = nc.vector.tensor_tensor(prod[:, b, q, :].rearrange("p (h f) -> p h f", h=HEADS),
                                                      key[:, b, q, :].rearrange("p (h f) -> p h f", h=HEADS),
                                                      ps_r[b][:, q * HD:(q + 1) * HD].unsqueeze(1).broadcast_to([P, HEADS, HD]), ALU.add)
                    ins.then_inc(with_rel[b], 1)
                    dve.wait_ge(with_rel[b], r + 1)
                    nc.vector.tensor_tensor(prod[:, b, :, :], prod[:, b, :, :], ps_q[b][:, :, :], ALU.mult).then_inc(multiplied[b], 1)

                def body(r, last):
                    for b in range(SL):
                        if b < SL - 1:
                            one_hots(r, b + 1, SL * r + b + 1)
                        elif not last:
                            one_hots(r + 1, 0, SL * r + SL)
                        multiply(r, b)
                        if not last:
                            addresses(r + 1, b, SL * r + b + SL)

                for b in range(SL):
                    addresses(0, b, b)
                one_hots(0, 0, 0)
                body(0, False)
                with dve.Fori(1, NG // SL - 1) as r:
                    body(r, False)
                body(NG // SL - 1, True)

            @block.scalar
            def _(act):
                def turn(r):
                    for b in range(SL):
                        g = SL * r + b
                        act.wait_ge(multiplied[b], r + 1)
                        for q in range(TPG):
                            for h in range(HEADS):
                                terms = prod[:, b, q, h * HD:(h + 1) * HD]
                                last = nc.scalar.activation(terms, terms, ACT.Copy,
                                                            accum_out=t.score[:, bass.ds(g * TPG + q, 1), h])
                        last.then_inc(reduced[b], 1)
                rounds(act, NG // SL, turn)


def segment_max(nc, i, t):
    TB = P // HEADS
    NB = -(-NT // TB)
    NTP = NB * TB
    with ExitStack() as ctx:
        sb, psum, sems, slot_sems = allocators(nc, ctx, "segment_max")
        hide = sb("hide", [P, NT], F32)
        masked = sb("masked", [P, NTP, HEADS], F32)
        keys = sb("keys", [P, NTP, HEADS], F32)
        key1 = sb("key1", [P, NT], F32)
        val = sb("val", [P, NB, P], F32)
        key = sb("key", [P, NB, P], F32)
        spare = t.acc[:, :, :].rearrange("p w f -> p (w f)")
        starts, ends, fwd = (spare[:, k * NB * P:(k + 1) * NB * P].rearrange("p (b e) -> p b e", e=P) for k in range(3))
        bwd = sb("bwd", [P, NB, P], F32)
        edge4 = sb("edge4", [P, NB, 4], F32)
        by_tile = sb("by_tile", [HEADS, NTP, 4], F32)
        whole = sb("whole", [HEADS, NTP], F32)
        joined = sb("joined", [HEADS, NTP + 1], F32)
        gate = sb("gate", [HEADS, NTP], F32)
        run = sb("run", [HEADS, NTP], F32)
        carry = sb("carry", [HEADS, NTP, 2], F32)
        carry_b = sb("carry_b", [P, NB, 2], F32)
        ps = [psum(f"ps{b}", [P, 4, P]) for b in range(2)]
        s = sems("pads d laid turned kept edge_out tile_in carry_out carry_in max_made back added weights")
        BLOCKS4 = [(b, min(4, NB - b)) for b in range(0, NB, 4)]

        with nc.Block() as block:
            @block.gpsimd
            def _(pool):
                pool.memset(masked[:, NT:NTP, :], -BIG).then_inc(s.pads, 1)
                pool.memset(keys[:, NT:NTP, :], -1.0).then_inc(s.pads, 1)

            @block.tensor
            def _(pe):
                pe.wait_ge(s.laid, 1)
                n = 0
                for what in (masked, keys):
                    flat = what[:, :, :].rearrange("p n h -> p (n h)")
                    for b0, m in BLOCKS4:
                        if n >= 2:
                            pe.wait_ge(s.kept, n - 1)
                        for q in range(m):
                            last = nc.tensor.transpose(ps[n % 2][:, q, :], flat[:, (b0 + q) * P:(b0 + q + 1) * P], t.ident[:, :])
                        last.then_inc(s.turned, 1)
                        n += 1
                pe.wait_ge(s.max_made, 1)
                for b0, m in BLOCKS4:
                    pe.wait_ge(s.kept, n - 1)
                    for q in range(m):
                        last = nc.tensor.transpose(ps[n % 2][:, q, :], fwd[:, b0 + q, :], t.ident[:, :])
                    last.then_inc(s.turned, 1)
                    n += 1

            @block.scalar
            def _(act):
                n = 0
                for to in (val, key):
                    for b0, m in BLOCKS4:
                        act.wait_ge(s.turned, n + 1)
                        nc.scalar.activation(to[:, b0:b0 + m, :], ps[n % 2][:, 0:m, :], ACT.Copy).then_inc(s.kept, 1)
                        n += 1
                flat = keys[:, :, :].rearrange("p n h -> p (n h)")
                for b0, m in BLOCKS4:
                    act.wait_ge(s.turned, n + 1)
                    nc.scalar.activation(flat[:, b0 * P:(b0 + m) * P], ps[n % 2][:, 0:m, :].rearrange("p a e -> p (a e)"), ACT.Copy).then_inc(s.kept, 1)
                    n += 1
                act.wait_ge(s.added, 1)
                nc.scalar.activation(t.score[:, :, :], t.score[:, :, :], ACT.Exp, scale=float(HD) ** -0.5).then_inc(s.weights, 1)

            @block.sync
            def _(sp):
                rows = t.edge_dram.rearrange("(b p c) -> p b c", p=P, c=4)
                tiles = t.edge_dram.rearrange("(n h c) -> h n c", h=HEADS, c=4)
                crows = t.carry_dram.rearrange("(b p c) -> p b c", p=P, c=2)
                ctiles = t.carry_dram.rearrange("(n h c) -> h n c", h=HEADS, c=2)
                sp.wait_ge(s.edge_out, 1)
                sp.dma_start(rows, edge4[:, :, :]).then_inc(s.edge_out, 16)
                sp.wait_ge(s.edge_out, 17)
                sp.dma_start(by_tile[:, :, :], tiles).then_inc(s.tile_in, 16)
                sp.wait_ge(s.carry_out, 1)
                sp.dma_start(ctiles, carry[:, :, :]).then_inc(s.carry_out, 16)
                sp.wait_ge(s.carry_out, 17)
                sp.dma_start(carry_b[:, :, :], crows).then_inc(s.carry_in, 16)

            @block.vector
            def _(dve):
                done = [0]

                def step_done(ins):
                    done[0] += 1
                    ins.then_inc(s.d, 1)
                    dve.wait_ge(s.d, done[0])

                v = nc.vector
                tt, ts, stt = v.tensor_tensor, v.tensor_scalar, v.scalar_tensor_tensor
                step_done(ts(hide[:, :], t.valid[:, :], 1.0, BIG, ALU.subtract, ALU.mult))
                step_done(tt(masked[:, 0:NT, :], t.score[:, :, :], t.valid[:, :].unsqueeze(2).broadcast_to([P, NT, HEADS]), ALU.mult))
                step_done(tt(masked[:, 0:NT, :], masked[:, 0:NT, :], hide[:, :].unsqueeze(2).broadcast_to([P, NT, HEADS]), ALU.add))
                step_done(stt(key1[:, :], t.edge[:, :, 0], 1.0, t.valid[:, :], ALU.add, ALU.mult))
                step_done(ts(key1[:, :], key1[:, :], -1.0, None, ALU.add))
                step_done(v.tensor_copy(keys[:, 0:NT, :], key1[:, :].unsqueeze(2).broadcast_to([P, NT, HEADS])))
                dve.wait_ge(s.pads, 2)
                dve.sem_inc(s.laid, 1)
                dve.wait_ge(s.kept, 2 * len(BLOCKS4))
                step_done(v.memset(starts[:, :, 0:1], -BIG))
                step_done(v.memset(ends[:, :, P - 1:P], -BIG))
                step_done(tt(starts[:, :, 1:P], key[:, :, 1:P], key[:, :, 0:P - 1], ALU.not_equal))
                step_done(ts(starts[:, :, 1:P], starts[:, :, 1:P], -BIG, None, ALU.mult))
                step_done(v.tensor_copy(ends[:, :, 0:P - 1], starts[:, :, 1:P]))
                flat = lambda a: a[:, :, :].rearrange("p b e -> p (b e)")
                step_done(v.tensor_tensor_scan(flat(fwd), flat(starts), flat(val), -BIG, ALU.add, ALU.max))
                step_done(v.tensor_tensor_scan(flat(bwd)[:, ::-1], flat(ends)[:, ::-1], flat(val)[:, ::-1], -BIG, ALU.add, ALU.max))
                step_done(tt(val[:, :, :], fwd[:, :, :], bwd[:, :, :], ALU.max))
                step_done(v.tensor_copy(edge4[:, :, 0:1], key[:, :, 0:1]))
                step_done(v.tensor_copy(edge4[:, :, 1:2], key[:, :, P - 1:P]))
                step_done(v.tensor_copy(edge4[:, :, 2:3], val[:, :, 0:1]))
                v.tensor_copy(edge4[:, :, 3:4], val[:, :, P - 1:P]).then_inc(s.edge_out, 1)
                dve.wait_ge(s.tile_in, 16)
                k0, k1, m0, m1 = (by_tile[:, :, c] for c in range(4))
                step_done(tt(whole[:, :], k0, k1, ALU.is_equal))
                step_done(v.memset(joined[:, :], 0.0))
                step_done(tt(joined[:, 1:NTP], k0[:, 1:NTP], k1[:, 0:NTP - 1], ALU.is_equal))
                step_done(tt(gate[:, :], whole[:, :], joined[:, 0:NTP], ALU.mult))
                step_done(ts(gate[:, :], gate[:, :], 1.0, BIG, ALU.subtract, ALU.mult))
                step_done(v.tensor_tensor_scan(run[:, :], gate[:, :], m1, -BIG, ALU.add, ALU.max))
                step_done(v.memset(carry[:, :, :], -BIG))
                step_done(ts(gate[:, :], joined[:, 0:NTP], 1.0, BIG, ALU.subtract, ALU.mult))
                step_done(tt(carry[:, 1:NTP, 0], run[:, 0:NTP - 1], gate[:, 1:NTP], ALU.add))
                step_done(tt(gate[:, :], whole[:, :], joined[:, 1:NTP + 1], ALU.mult))
                step_done(ts(gate[:, :], gate[:, :], 1.0, BIG, ALU.subtract, ALU.mult))
                step_done(v.tensor_tensor_scan(run[:, ::-1], gate[:, ::-1], m0[:, ::-1], -BIG, ALU.add, ALU.max))
                step_done(ts(gate[:, :], joined[:, 1:NTP + 1], 1.0, BIG, ALU.subtract, ALU.mult))
                step_done(tt(carry[:, 0:NTP - 1, 1], run[:, 1:NTP], gate[:, 0:NTP - 1], ALU.add))
                v.nop().then_inc(s.carry_out, 1)
                bc = lambda a: a.broadcast_to([P, NB, P])
                step_done(tt(starts[:, :, :], key[:, :, :], bc(key[:, :, 0:1]), ALU.is_equal))
                step_done(tt(ends[:, :, :], key[:, :, :], bc(key[:, :, P - 1:P]), ALU.is_equal))
                for a in (starts, ends):
                    step_done(ts(a[:, :, :], a[:, :, :], 1.0, BIG, ALU.subtract, ALU.mult))
                dve.wait_ge(s.carry_in, 16)
                for a, c in ((starts, 0), (ends, 1)):
                    step_done(tt(a[:, :, :], a[:, :, :], bc(carry_b[:, :, c:c + 1]), ALU.add))
                    step_done(tt(val[:, :, :], val[:, :, :], a[:, :, :], ALU.max))
                v.tensor_copy(fwd[:, :, :], val[:, :, :]).then_inc(s.max_made, 1)
                dve.wait_ge(s.kept, 3 * len(BLOCKS4))
                tt(t.score[:, :, :], masked[:, 0:NT, :], keys[:, 0:NT, :], ALU.subtract).then_inc(s.added, 1)
                dve.wait_ge(s.weights, 1)
                step_done(tt(t.score[:, :, :], t.score[:, :, :], t.valid[:, :].unsqueeze(2).broadcast_to([P, NT, HEADS]), ALU.mult))


def layer1_sum(nc, i, t):
    with ExitStack() as ctx:
        sb, psum, sems, slot_sems = allocators(nc, ctx, "layer1_sum")
        at = sb("at", [P, SL, TPG], U32)
        vin = sb("vin", [P, SL, TPG, VROW], F32)
        hot = sb("hot", [P, SL, TPG, P], F32)
        rhs = sb("rhs", [P, SL, TPG, D + HEADS + 1], F32)
        ps = [psum(f"ps{b}", [P, 512]) for b in range(SL)]
        s = sems("acc_zero turn")
        at_set, hot_made, weighed, scaled, summed, kept = slot_sems("at_set hot_made weighed scaled summed kept")
        val_in = t.val_in
        with nc.Block() as block:
            @block.gpsimd
            def _(pool):
                pool.memset(t.acc[:, :, :], 0.0).then_inc(s.acc_zero, 1)
                def turn(r):
                    for b in range(SL):
                        pool.wait_ge(at_set[b], r + 1)
                        pool.wait_ge(scaled[b], r)
                        pool.wait_ge(weighed[b], r)
                        pool.sem_inc(s.turn, 1)
                        for q in range(TPG):
                            pool.indirect_dma_start(vin[:, b, q, :], None, t.val_dram,
                                                    bass.IndirectOffsetOnAxis(ap=at[:, b, q:q + 1], axis=0)).then_inc(val_in[b], 16)
                rounds(pool, NG // SL, turn)

            @block.scalar
            def _(act):
                def turn(r):
                    for b in range(SL):
                        g = SL * r + b
                        act.wait_ge(val_in[b], 16 * TPG * (r + 1))
                        act.wait_ge(summed[b], r)
                        nc.scalar.activation(rhs[:, b, :, D:D + HEADS], t.score[:, bass.ds(g * TPG, TPG), :], ACT.Copy)
                        nc.scalar.activation(rhs[:, b, :, D + HEADS], vin[:, b, :, D], ACT.Copy).then_inc(weighed[b], 1)
                rounds(act, NG // SL, turn)

            @block.tensor
            def _(pe):
                def turn(r):
                    for b in range(SL):
                        pe.wait_ge(hot_made[b], r + 1)
                        pe.wait_ge(weighed[b], r + 1)
                        pe.wait_ge(scaled[b], r + 1)
                        pe.wait_ge(kept[b], r)
                        for q in range(TPG):
                            last = nc.tensor.matmul(ps[b][:, 0:D + HEADS + 1], hot[:, b, q, :], rhs[:, b, q, :],
                                                    start=q == 0, stop=q == TPG - 1)
                        last.then_inc(summed[b], 1)
                rounds(pe, NG // SL, turn)

            @block.vector
            def _(dve):
                dve.wait_ge(s.acc_zero, 1)

                def addresses(r, b, g):
                    dve.wait_ge(val_in[b], 16 * TPG * r)
                    nc.vector.tensor_scalar(at[:, b, :], t.edge[:, bass.ds(g * TPG, TPG), 1], float(NPAD - 1), None, ALU.min).then_inc(at_set[b], 1)

                def one_hots(r, b, g):
                    dve.wait_ge(summed[b], r)
                    for q in range(TPG):
                        last = nc.vector.tensor_scalar(hot[:, b, q, :], t.cols[:, :], t.local[:, bass.ds(g * TPG + q, 1)], None, ALU.is_equal)
                    last.then_inc(hot_made[b], 1)

                def scale_group(r, b, g):
                    dve.wait_ge(val_in[b], 16 * TPG * (r + 1))
                    dve.wait_ge(summed[b], r)
                    for q in range(TPG):
                        last = nc.vector.tensor_tensor(rhs[:, b, q, 0:D].rearrange("p (h f) -> p h f", h=HEADS),
                                                       vin[:, b, q, 0:D].rearrange("p (h f) -> p h f", h=HEADS),
                                                       t.score[:, bass.ds(g * TPG + q, 1), :].rearrange("p a h -> p (a h)")
                                                       .unsqueeze(2).broadcast_to([P, HEADS, HD]), ALU.mult)
                    last.then_inc(scaled[b], 1)

                def add_group(r, b, g):
                    win = dve.value_load(t.dst_win[0:1, bass.ds(g, 1)], min_val=0, max_val=NW - 1)
                    sums = t.acc[:, bass.ds(win, 1), 0:D + HEADS + 1].rearrange("p a f -> p (a f)")
                    dve.wait_ge(summed[b], r + 1)
                    dve.wait_ge(kept[(b - 1) % SL], r + (b > 0))
                    nc.vector.tensor_tensor(sums, sums, ps[b][:, 0:D + HEADS + 1], ALU.add).then_inc(kept[b], 1)

                def body(r, last):
                    for b in range(SL):
                        if b < SL - 1:
                            one_hots(r, b + 1, SL * r + b + 1)
                            scale_group(r, b + 1, SL * r + b + 1)
                        elif not last:
                            one_hots(r + 1, 0, SL * r + SL)
                            scale_group(r + 1, 0, SL * r + SL)
                        if not last:
                            addresses(r + 1, b, SL * r + b + SL)
                        add_group(r, b, SL * r + b)

                for b in range(SL):
                    addresses(0, b, b)
                one_hots(0, 0, 0)
                scale_group(0, 0, 0)
                body(0, False)
                with dve.Fori(1, NG // SL - 1) as r:
                    body(r, False)
                body(NG // SL - 1, True)


def layer1_nodes(nc, i, t):
    with ExitStack() as ctx:
        sb, psum, sems, slot_sems = allocators(nc, ctx, "layer1_nodes")
        wo = sb("wo", [P, 2, D], F32)
        bo = sb("bo", [1, D], F32)
        gamma = sb("gamma", [P, D], F32)
        beta = sb("beta", [P, D], F32)
        alone = sb("alone", [P, NW, HEADS], F32)
        den = sb("den", [P, NW, HEADS], F32)
        msg = sb("msg", [P, CW, D], F32)
        own = sb("own", [P, CW, D], F32)
        msg_t = sb("msg_t", [P, 2, CW * P], F32)
        shifted = sb("shifted", [P, CW, D], F32)
        v = sb("v", [P, CW, D], F32)
        result = sb("result", [P, CW, D], F32)
        stats = sb("stats", [P, CW, 6], F32)
        mean_var = sb("mean_var", [P, CW, 2], F32)
        var_eps = sb("var_eps", [P, CW], F32)
        rstd = sb("rstd", [P, CW], F32)
        inverse = sb("inverse", [P, NW], F32)
        fine = sb("fine", [P, NW], F32)
        ps_x = [psum(f"ps_x{b}", [P, 512]) for b in range(2)]
        ps_o = [psum(f"ps_o{b}", [P, 512]) for b in range(2)]
        s = sems("w_in d p carried msg_made shifted_made combined turned msg_t_made projected added var_made rooted normed out_done")
        with nc.Block() as block:
            @block.sync
            def _(sp):
                sp.dma_start(wo[:, :, :], i.L1_gnn_Wo.rearrange("(k p) m -> p k m", p=P)).then_inc(s.w_in, 16)
                sp.dma_start(bo[:, :], i.L1_gnn_bo.rearrange("(a m) -> a m", a=1)).then_inc(s.w_in, 16)
                sp.dma_start(gamma[:, :], i.L1_gnn_gamma.partition_broadcast(P)).then_inc(s.w_in, 16)
                sp.dma_start(beta[:, :], i.L1_gnn_beta.partition_broadcast(P)).then_inc(s.w_in, 16)
                def turn(c):
                    sp.wait_ge(s.normed, (c + 1) * CW)
                    sp.dma_start(i.out[bass.ds(c * CW * P, CW * P), :].rearrange("(w p) m -> p w m", p=P), result[:, :, :]).then_inc(s.out_done, 16)
                rounds(sp, CH - 1, turn)
                first = (CH - 1) * CW * P
                sp.wait_ge(s.normed, CH * CW)
                sp.dma_start(i.out[first:(NW - 1) * P, :].rearrange("(w p) m -> p w m", p=P), result[:, 0:CW - 1, :]).then_inc(s.out_done, 16)
                sp.dma_start(i.out[(NW - 1) * P:N, :], result[0:TAIL_NODES, CW - 1, :]).then_inc(s.out_done, 16)
                sp.wait_ge(s.out_done, 16 * (CH + 1))

            @block.tensor
            def _(pe):
                pe.wait_ge(s.w_in, 16 * 4)
                def turn(c):
                    for w in range(CW):
                        pe.wait_ge(s.msg_made, c * CW + w + 1)
                        if w < 2:
                            pe.wait_ge(s.msg_t_made, c * CW)
                        else:
                            pe.wait_ge(s.msg_t_made, c * CW + w - 1)
                        for half in range(2):
                            last = nc.tensor.transpose(ps_x[w % 2][:, half * P:(half + 1) * P], msg[:, w, half * P:(half + 1) * P], t.ident[:, :])
                        last.then_inc(s.turned, 1)
                    pe.wait_ge(s.msg_t_made, (c + 1) * CW)
                    for w in range(CW):
                        if w < 2:
                            pe.wait_ge(s.added, c * CW)
                        else:
                            pe.wait_ge(s.added, c * CW + w - 1)
                        for k in range(2):
                            nc.tensor.matmul(ps_o[w % 2][:, 0:D], msg_t[:, k, w * P:(w + 1) * P], wo[:, k, :], start=k == 0, stop=False)
                        nc.tensor.matmul(ps_o[w % 2][:, 0:D], t.ones[0:1, 0:P], bo[0:1, :], start=False, stop=True).then_inc(s.projected, 1)
                rounds(pe, CH, turn)

            @block.scalar
            def _(act):
                def turned_kept(c):
                    for w in range(CW):
                        act.wait_ge(s.turned, c * CW + w + 1)
                        nc.scalar.activation(msg_t[:, :, w * P:(w + 1) * P], ps_x[w % 2][:, 0:2 * P].rearrange("p (k n) -> p k n", k=2),
                                             ACT.Copy).then_inc(s.msg_t_made, 1)

                def roots(c):
                    for norm in range(2):
                        act.wait_ge(s.var_made, c * 2 + norm + 1)
                        nc.scalar.activation(rstd[:, :], var_eps[:, :], ACT.Sqrt).then_inc(s.rooted, 1)

                turned_kept(0)
                turned_kept(1)
                roots(0)
                with act.Fori(1, CH - 1) as c:
                    turned_kept(c + 1)
                    roots(c)
                roots(CH - 1)

            @block.gpsimd
            def _(pool):
                pool.wait_ge(s.w_in, 16 * 4)
                pool.wait_ge(s.d, 7)
                PSTEPS = 2 * CW

                def turn(c):
                    n = c * PSTEPS
                    tt = nc.gpsimd.tensor_tensor
                    heads = lambda a: a.rearrange("p a (h f) -> p (a h) f", h=HEADS)
                    pool.wait_ge(s.turned, c * CW)
                    for w in range(CW):
                        by_head = lambda a: a[:, w, :].rearrange("p (h f) -> p h f", h=HEADS)
                        over = lambda a: a[:, bass.ds(c * CW + w, 1), :].rearrange("p a h -> p (a h)").unsqueeze(2).broadcast_to([P, HEADS, HD])
                        tt(by_head(msg), heads(t.acc[:, bass.ds(c * CW + w, 1), 0:D]), over(den), ALU.mult).then_inc(s.p, 1)
                        tt(by_head(own), heads(t.val[:, bass.ds(c * CW + w, 1), 0:D]), over(alone), ALU.mult).then_inc(s.p, 1)
                        pool.wait_ge(s.p, n + 2 * (w + 1))
                        tt(msg[:, w, :], msg[:, w, :], own[:, w, :], ALU.add).then_inc(s.msg_made, 1)
                    pool.wait_ge(s.combined, c * CW)
                    tt(shifted[:, :, :], t.x[:, bass.ds(c * CW, CW), :], beta[:, :].unsqueeze(1).broadcast_to([P, CW, D]), ALU.add).then_inc(s.shifted_made, 1)
                rounds(pool, CH, turn)

            @block.vector
            def _(dve):
                tt, ts, stt = nc.vector.tensor_tensor, nc.vector.tensor_scalar, nc.vector.scalar_tensor_tensor
                weights = t.acc[:, :, D:D + HEADS]
                ts(alone[:, :, :], weights, 0.0, None, ALU.is_equal).then_inc(s.d, 1)
                tt(fine[:, :], t.acc[:, :, D + HEADS], t.val[:, :, D], ALU.add).then_inc(s.d, 1)
                dve.wait_ge(s.d, 2)
                tt(den[:, :, :], weights, alone[:, :, :], ALU.add).then_inc(s.d, 1)
                ts(fine[:, :], fine[:, :], 0.0, None, ALU.is_equal).then_inc(s.d, 1)
                dve.wait_ge(s.d, 4)
                nc.vector.reciprocal(den[:, :, :], den[:, :, :]).then_inc(s.d, 1)
                nc.vector.reciprocal(inverse[:, :], fine[:, :]).then_inc(s.d, 1)
                dve.wait_ge(s.d, 6)
                tt(fine[:, :], fine[:, :], inverse[:, :], ALU.mult).then_inc(s.d, 1)
                dve.wait_ge(s.d, 7)
                FIRST_STEPS = 7
                DSTEPS = 2 * MOMENT_STEPS + CW + 3
                dve.wait_ge(s.w_in, 16 * 4)

                def turn(c):
                    n = c * DSTEPS + FIRST_STEPS
                    dve.wait_ge(s.normed, c * CW)
                    for w in range(CW):
                        dve.wait_ge(s.projected, c * CW + w + 1)
                        tt(v[:, w, :], ps_o[w % 2][:, 0:D], t.x[:, bass.ds(c * CW + w, 1), :].rearrange("p a m -> p (a m)"), ALU.add).then_inc(s.added, 1)
                    dve.wait_ge(s.added, (c + 1) * CW)
                    moments(nc, dve, s.d, n, s.carried, v, stats, mean_var, var_eps, s.var_made)
                    n += MOMENT_STEPS
                    for w in range(CW):
                        stt(v[:, w, :], v[:, w, :], mean_var[:, w, 0:1], gamma[:, :], ALU.subtract, ALU.mult).then_inc(s.d, 1)
                    dve.wait_ge(s.rooted, c * 2 + 1)
                    nc.vector.reciprocal(rstd[:, :], rstd[:, :]).then_inc(s.d, 1)
                    dve.wait_ge(s.d, n + CW + 1)
                    tt(rstd[:, :], rstd[:, :], fine[:, bass.ds(c * CW, CW)], ALU.mult).then_inc(s.d, 1)
                    dve.wait_ge(s.d, n + CW + 2)
                    dve.wait_ge(s.shifted_made, c + 1)
                    for w in range(CW):
                        stt(v[:, w, :], v[:, w, :], rstd[:, w:w + 1], shifted[:, w, :], ALU.mult, ALU.add).then_inc(s.combined, 1)
                    dve.wait_ge(s.combined, (c + 1) * CW)
                    moments(nc, dve, s.d, n + CW + 2, s.carried, v, stats, mean_var, var_eps, s.var_made)
                    n += CW + 2 + MOMENT_STEPS
                    dve.wait_ge(s.rooted, c * 2 + 2)
                    nc.vector.reciprocal(rstd[:, :], rstd[:, :]).then_inc(s.d, 1)
                    dve.wait_ge(s.d, n + 1)
                    dve.wait_ge(s.out_done, 16 * c)
                    for w in range(CW):
                        ts(result[:, w, :], v[:, w, :], mean_var[:, w, 0:1], rstd[:, w:w + 1], ALU.subtract, ALU.mult).then_inc(s.normed, 1)
                rounds(dve, CH, turn)


def build(nc, i):
    with ExitStack() as ctx:
        t = named()
        ring = lambda name, slots: [ctx.enter_context(nc.semaphore(f"{name}_{b}")) for b in range(slots)]
        t.row_out, t.key_in, t.val_in = ring("row_out", EL), ring("key_in", SL), ring("val_in", SL)
        sb = allocators(nc, ctx, "all")[0]
        t.x = sb("x", [P, NW, D], F32)
        t.table3 = sb("table3", [P, NW, 3 * ROWW], BF16)
        t.ident = sb("ident", [P, P], F32)
        t.lane = sb("lane", [P, 1], F32)
        t.trash = sb("trash", [P, 1], F32)
        t.cols = sb("cols", [P, P], F32)
        t.win_of_col = sb("win_of_col", [P, NW * HEADS], F32)
        t.ones = sb("ones", [P, P], F32)
        t.elem_w = sb("elem_w", [P, HEADS], F32)
        t.fill_at = sb("fill_at", [P, 2 * NW], I32)
        t.src_win = sb("src_win", [P, NG], I32)
        t.dst_win = sb("dst_win", [P, NG], I32)
        t.first_edge = sb("first_edge", [P, NG], I32)
        t.win_base = sb("win_base", [P, NG], F32)
        t.win_lane = sb("win_lane", [P, NG], F32)

        def dram(name, shape, dt):
            return nc.dram_tensor(name, shape, dt, kind="Internal").ap()

        t.rec_dram = dram("edge_records", [EPAD + GE, 8], F32)
        t.row_dram = dram("edge_rows16", [3, EPAD + GE], I16)
        t.rows_dram = dram("rows_by_src", [SCRAP + 2 * NW * GE, ROWW], F32)
        t.key_dram = dram("keys", [NPAD, D], F32)
        t.val_dram = dram("values", [NPAD, VROW], F32)
        tiles = -(-NT // (P // HEADS)) * P
        t.edge_dram = dram("tile_ends", [tiles * 4], F32)
        t.carry_dram = dram("tile_carries", [tiles * 2], F32)

        prepare(nc, i, t)
        t.edge = sb("edge", [P, NT, 8], F32)
        t.local = sb("local", [P, NT], F32)
        t.valid = sb("valid", [P, NT], F32)
        t.score = sb("score", [P, NT, HEADS], F32)
        t.acc = sb("acc", [P, NW, ROWW], F32)
        layer0_edges(nc, i, t)
        layer0_sum(nc, i, t)
        t.val = sb("val", [P, NW, VROW], F32)
        layer0_nodes(nc, i, t)
        layer1_scores(nc, i, t)
        segment_max(nc, i, t)
        layer1_sum(nc, i, t)
        layer1_nodes(nc, i, t)


INPUTS = ["x", "src", "dst", "edge_type_64", "edge_weight", "L0_gnn_W1", "L0_gnn_b1", "L0_gnn_W2", "L0_gnn_b2",
          "L0_gnn_attn_w", "L0_gnn_attn_b", "L1_gnn_query_emb", "L1_gnn_Wq", "L1_gnn_bq", "L1_gnn_Wk", "L1_gnn_bk",
          "L1_gnn_Wv", "L1_gnn_bv", "L1_gnn_rel_w", "L1_gnn_Wo", "L1_gnn_bo", "L1_gnn_gamma", "L1_gnn_beta"]


def kernel(**inputs):
    import numpy as np
    from concourse import bacc
    from concourse.bass_utils import run_bass_kernel_spmd

    nc = bacc.Bacc("TRN2", target_bir_lowering=False, num_devices=1)
    arrays, args = {}, {}
    for name in INPUTS:
        a = np.ascontiguousarray(inputs[name])
        arrays[f"in_{name}"] = a
        args[name] = nc.dram_tensor(f"in_{name}", a.shape, mybir.dt.from_np(a.dtype), kind="ExternalInput").ap()
    args["out"] = nc.dram_tensor("out_0", (N, D), F32, kind="ExternalOutput").ap()
    build(nc, named(**args))
    result = run_bass_kernel_spmd(nc, [arrays], core_ids=[0])
    return result.results[0]["out_0"]
```

```python
from contextlib import ExitStack

import concourse.bass as bass
from concourse import mybir

ALU = mybir.AluOpType
ACT = mybir.ActivationFunctionType
AX = mybir.AxisListType
F32 = mybir.dt.float32
BF16 = mybir.dt.bfloat16
I32 = mybir.dt.int32
U32 = mybir.dt.uint32
I16 = mybir.dt.int16

P = 128
N, E = 3125, 50000
D, HEADS, HD, RELS = 256, 4, 64, 64
HID = 256
NW = -(-N // P)
NPAD = NW * P
TAIL_NODES = N - (NW - 1) * P
EPP = -(-E // P)
EPAD = EPP * P
TAIL_EDGES = E - (P - 1) * EPP
TPG = 2
GE = TPG * P
NG = (E + NW * (GE - 1)) // GE
NT = NG * TPG
EL = 10
BANKS = EL // 2
assert NG % EL == 0 and EL % 2 == 0 and GE == 256
NROWS = NG * GE
TRASH = NROWS
SCRAP = TRASH + P
ROWW = 264
VROW = 260
FH = HD + 2
NO_NODE = 8000
BIG = 1.0e30
EPS = 1.0e-5
CH = 5
CW = NW // CH
COUNT_AFTER = 2


def named(**things):
    return type("Named", (), things)


def rounds(eng, count, turn):
    turn(0)
    with eng.Fori(1, count) as r:
        turn(r)


def with_ahead(eng, slots, depth, prep, work):
    def turn(r, last):
        for b in range(slots):
            if b + depth < slots:
                prep(r, b + depth)
            elif not last:
                prep(r + 1, b + depth - slots)
            work(r, b)
    for b in range(depth):
        prep(0, b)
    turn(0, False)
    with eng.Fori(1, NG // slots - 1) as r:
        turn(r, False)
    turn(NG // slots - 1, True)


def allocators(nc, ctx, stage):
    numbers = []

    def sb(name, shape, dt):
        return ctx.enter_context(nc.sbuf_tensor(f"{stage}_{name}", shape, dt))

    def psum(name, shape):
        return ctx.enter_context(nc.psum_tensor(f"{stage}_{name}", shape, F32))

    def sem(name):
        handle = ctx.enter_context(nc.semaphore(f"{stage}_{name}"))
        numbers.append(handle.num)
        return handle

    def sems(names):
        return named(**{n: sem(n) for n in names.split()})

    def slot_sems(names):
        return [[sem(f"{n}_{b}") for b in range(EL)] for n in names.split()]

    def clear():
        if numbers:
            nc.all_engine_barrier(sems_to_clear=range(min(numbers), max(numbers) + 1))

    ctx.callback(clear)
    return sb, psum, sems, slot_sems


def prepare(nc, i, t):
    with ExitStack() as ctx:
        sb, psum, sems, slot_sems = allocators(nc, ctx, "prepare")
        w1 = sb("w1", [P, 2, HEADS * HID], F32)
        w2 = sb("w2", [P, HEADS, 2, HD], F32)
        w2x = sb("w2x", [P, HEADS, 2, FH], F32)
        aw = sb("aw", [P, HEADS, 2 * HD + 1], F32)
        ab = sb("ab", [P, HEADS], F32)
        b1 = sb("b1", [P, HEADS * 2], F32)
        b2 = sb("b2", [P, HEADS, HD], F32)
        b2x = sb("b2x", [P, HEADS, FH], F32)
        junk = sb("junk", [P, HD], F32)
        dots = sb("dots", [P, HEADS, 3, 2], F32)
        x_now = sb("x_now", [P, CW, D], F32)
        x_t = sb("x_t", [P, 2, CW * P], F32)
        hid = sb("hid", [P, HEADS * 2, CW * P], F32)
        ftmp = sb("ftmp", [P, CW, HEADS * FH], F32)
        rec = sb("rec", [P, EPP, 8], F32)
        row16 = sb("row16", [P, 3, EPP], I16)
        neutral = sb("neutral", [P, ROWW], F32)
        pad_rec = sb("pad_rec", [P, TPG, 8], F32)
        pad_row = sb("pad_row", [3, GE], I16)
        src_i = sb("src_i", [P, EPP], I32)
        dst_i = sb("dst_i", [P, EPP], I32)
        typ_i = sb("typ_i", [P, EPP], I32)
        wgt = sb("wgt", [P, EPP], F32)
        low_i = sb("low_i", [P, EPP], I32)
        ones_e = sb("ones_e", [P, EPP], BF16)
        mask = sb("mask", [P, NW, EPP], BF16)
        rank = sb("rank", [P, NW, EPP], F32)
        win_no = sb("win_no", [P, NW], F32)
        win_end = sb("win_end", [P, NW], F32)
        cnt = sb("cnt", [P, 2 * NW], F32)
        tot = sb("tot", [P, 2 * NW], F32)
        below = sb("below", [P, P], F32)
        base = sb("base", [P, NW], F32)
        gi = sb("gi", [P, 2, NW], I32)
        grp = sb("grp", [P, 2, NW], F32)
        cum = sb("cum", [P, 2, NW], F32)
        fst = sb("fst", [P, 2, NW], F32)
        fill = sb("fill", [P, 2, NW], F32)
        no_fill = sb("no_fill", [P, 2, NW], F32)
        scrap = sb("scrap", [P, 2, NW], F32)
        off = sb("off", [P, NW + 1], F32)
        step = sb("step", [P, NW], F32)
        g_no = sb("g_no", [P, NG], F32)
        reach = mask[:, :, :].rearrange("p k j -> p (k j)")[:, 0:NG * NW].rearrange("p (g k) -> p g k", k=NW)
        reach_o = rank[:, :, :].rearrange("p k j -> p (k j)")[:, 0:NG * NW].rearrange("p (g k) -> p g k", k=NW)
        acc_f = rank[:, :, :].rearrange("p k j -> p (k j)")[:, NG * NW:NG * (NW + 4)].rearrange("p (a g) -> p a g", a=4)
        ps_x = [psum(f"ps_x{b}", [P, 512]) for b in range(2)]
        ps_h = [psum(f"ps_h{b}", [P, 512]) for b in range(2)]
        ps_f = [psum(f"ps_f{b}", [P, 512]) for b in range(2)]
        ps_c = psum("ps_c", [P, 512])
        s = sems("rest_in pad_set const_set ident_set tri_set x_in w_in e_in prep w2x_set x_turned xt_copied hid_made "
                       "hid_kept f_made f_copied f_hi f_res f_mid f_lo x_staged d counted totals "
                       "neutral_set rows16_set fill_set ranked written")

        with nc.Block() as block:
            @block.sync
            def _(sp):
                sp.dma_start(t.x[:, 0:CW, :], i.x[0:CW * P, :].rearrange("(w p) c -> p w c", p=P)).then_inc(s.x_in, 16)
                sp.dma_start(w1[:, :, :].rearrange("p k (h m) -> p k h m", h=HEADS)[:, 0, :, :],
                             i.L0_gnn_W1[:, 0:P, :].rearrange("h p m -> p h m")).then_inc(s.w_in, 16)
                sp.dma_start(w1[:, :, :].rearrange("p k (h m) -> p k h m", h=HEADS)[:, 1, :, :],
                             i.L0_gnn_W1[:, P:2 * P, :].rearrange("h p m -> p h m")).then_inc(s.w_in, 16)
                sp.dma_start(w2[:, :, :, :], i.L0_gnn_W2.rearrange("h (k p) m -> p h k m", p=P)).then_inc(s.w_in, 16)
                sp.dma_start(aw[:, :, :], i.L0_gnn_attn_w.rearrange("h m o -> (h m o)").partition_broadcast(P)
                             .rearrange("p (h m) -> p h m", h=HEADS)).then_inc(s.w_in, 16)
                sp.dma_start(ab[:, :], i.L0_gnn_attn_b.rearrange("h o -> (h o)").partition_broadcast(P)).then_inc(s.w_in, 16)
                sp.dma_start(b1[:, :].rearrange("p (h k) -> p h k", k=2), i.L0_gnn_b1.rearrange("h (k p) -> p h k", p=P),
                             allow_slow_non_contiguous=True).then_inc(s.w_in, 16)
                sp.dma_start(b2[:, :, :], i.L0_gnn_b2.rearrange("h m -> (h m)").partition_broadcast(P)
                             .rearrange("p (h m) -> p h m", h=HEADS)).then_inc(s.w_in, 16)
                sp.dma_start(t.x[:, CW:NW - 1, :], i.x[CW * P:(NW - 1) * P, :].rearrange("(w p) c -> p w c", p=P)).then_inc(s.rest_in, 16)
                sp.wait_ge(s.pad_set, 5)
                sp.dma_start(t.x[0:TAIL_NODES, NW - 1, :], i.x[(NW - 1) * P:N, :]).then_inc(s.rest_in, 16)
                for dst_tile, src in ((src_i, i.src), (dst_i, i.dst), (typ_i, i.edge_type_64), (wgt, i.edge_weight)):
                    sp.dma_start(dst_tile[0:P - 1, :], src[0:(P - 1) * EPP].rearrange("(p j) -> p j", p=P - 1)).then_inc(s.e_in, 16)
                    sp.dma_start(dst_tile[P - 1:P, 0:TAIL_EDGES], src[(P - 1) * EPP:E].rearrange("(a j) -> a j", a=1)).then_inc(s.e_in, 16)
                sp.wait_ge(s.rows16_set, 1)
                for r in range(3):
                    sp.dma_start(t.row_dram[r, 0:EPAD].rearrange("(p j) -> p j", p=P), row16[:, r, :]).then_inc(s.written, 16)
                sp.wait_ge(s.neutral_set, 5)
                sp.dma_start(t.rec_dram[EPAD:EPAD + GE, :].rearrange("(q p) c -> p q c", p=P), pad_rec[:, :, :]).then_inc(s.written, 16)
                sp.dma_start(t.row_dram[:, EPAD:EPAD + GE], pad_row[:, :]).then_inc(s.written, 16)
                sp.wait_ge(s.fill_set, 1)
                with sp.Fori(0, 2 * NW) as k:
                    at = sp.value_load(t.fill_at[0:1, bass.ds(k, 1)], min_val=0, max_val=SCRAP + (2 * NW - 1) * GE)
                    sp.dma_start(t.rows_dram[bass.ds(at, GE), :].rearrange("(q p) c -> p q c", p=P), neutral[:, :].unsqueeze(1).broadcast_to([P, TPG, ROWW])).then_inc(s.written, 16)
                sp.wait_ge(s.ranked, 1)
                sp.dma_start(t.rec_dram[0:EPAD, :].rearrange("(p j) c -> p (j c)", p=P),
                             rec[:, :, :].rearrange("p j c -> p (j c)")).then_inc(s.written, 16)
                sp.wait_ge(s.written, 16 * (6 + 2 * NW))

            @block.gpsimd
            def _(pool):
                pool.memset(t.x[:, NW - 1, :], 0.0).then_inc(s.pad_set, 1)
                pool.memset(src_i[:, TAIL_EDGES:EPP], NO_NODE).then_inc(s.pad_set, 1)
                pool.memset(dst_i[:, TAIL_EDGES:EPP], NO_NODE).then_inc(s.pad_set, 1)
                pool.memset(typ_i[:, TAIL_EDGES:EPP], 0).then_inc(s.pad_set, 1)
                pool.memset(wgt[:, TAIL_EDGES:EPP], 0.0).then_inc(s.pad_set, 1)
                pool.memset(t.ident[:, :], 0.0).then_inc(s.ident_set, 1)
                pool.memset(below[:, :], 1.0).then_inc(s.tri_set, 1)
                pool.wait_ge(s.ident_set, 1)
                pool.affine_select(out=t.ident[:, :], in_=t.ident[:, :], compare_op=ALU.not_equal, fill=1.0,
                                   base=0, pattern=[[-1, P]], channel_multiplier=1).then_inc(s.ident_set, 1)
                pool.wait_ge(s.tri_set, 1)
                pool.affine_select(out=below[:, :], in_=below[:, :], compare_op=ALU.is_gt, fill=0.0,
                                   base=0, pattern=[[1, P]], channel_multiplier=-1).then_inc(s.tri_set, 1)
                pool.iota(t.lane[:, :], pattern=[[0, 1]], base=0, channel_multiplier=1,
                          allow_small_or_imprecise_dtypes=True).then_inc(s.const_set, 1)
                pool.iota(t.trash[:, :], pattern=[[0, 1]], base=TRASH, channel_multiplier=1,
                          allow_small_or_imprecise_dtypes=True).then_inc(s.const_set, 1)
                pool.iota(win_no[:, :], pattern=[[1, NW]], base=0, channel_multiplier=0,
                          allow_small_or_imprecise_dtypes=True).then_inc(s.const_set, 1)
                pool.iota(win_end[:, :], pattern=[[P, NW]], base=P, channel_multiplier=0,
                          allow_small_or_imprecise_dtypes=True).then_inc(s.const_set, 1)
                pool.iota(scrap[:, :, :], pattern=[[GE, 2 * NW]], base=SCRAP, channel_multiplier=0,
                          allow_small_or_imprecise_dtypes=True).then_inc(s.const_set, 1)
                pool.iota(g_no[:, :], pattern=[[1, NG]], base=0, channel_multiplier=0,
                          allow_small_or_imprecise_dtypes=True).then_inc(s.const_set, 1)
                pool.iota(t.cols[:, :], pattern=[[1, P]], base=0, channel_multiplier=0,
                          allow_small_or_imprecise_dtypes=True).then_inc(s.const_set, 1)
                pool.iota(t.win_of_col[:, :], pattern=[[1, NW], [0, HEADS]], base=0, channel_multiplier=0,
                          allow_small_or_imprecise_dtypes=True).then_inc(s.const_set, 1)
                pool.memset(t.ones[:, :], 1.0).then_inc(s.const_set, 1)
                pool.memset(ones_e[:, :], 1.0).then_inc(s.const_set, 1)
                pool.memset(neutral[:, 0:D], 0.0).then_inc(s.neutral_set, 1)
                pool.memset(neutral[:, D:D + HEADS], -BIG).then_inc(s.neutral_set, 1)
                pool.memset(neutral[:, D + HEADS:ROWW], -1.0).then_inc(s.neutral_set, 1)
                pool.memset(pad_rec[:, :, :], float(NO_NODE)).then_inc(s.neutral_set, 1)
                pool.memset(pad_row[:, :], NO_NODE).then_inc(s.neutral_set, 1)
                pool.wait_ge(s.x_in, 16)
                pool.tensor_copy(x_now[:, :, :], t.x[:, 0:CW, :]).then_inc(s.x_staged, 1)
                pool.wait_ge(s.rest_in, 32)

                def split_rest(c):
                    def part(w, k):
                        return t.table3[:, bass.ds(c * CW + w, 1), k * ROWW:k * ROWW + HEADS * FH].rearrange("p a f -> p (a f)")

                    def third(w):
                        pool.wait_ge(s.f_mid, c * CW + w + 1)
                        nc.gpsimd.tensor_tensor(part(w, 2), ftmp[:, w, :], part(w, 1), ALU.subtract).then_inc(s.f_lo, 1)
                    for w in range(CW):
                        pool.wait_ge(s.f_hi, c * CW + w + 1)
                        nc.gpsimd.tensor_tensor(ftmp[:, w, :], ftmp[:, w, :], part(w, 0), ALU.subtract).then_inc(s.f_res, 1)
                        if w >= 2:
                            third(w - 2)
                    third(CW - 2)
                    third(CW - 1)

                def turn(c):
                    pool.wait_ge(s.x_turned, (c + 1) * CW)
                    pool.tensor_copy(x_now[:, :, :], t.x[:, bass.ds(c * CW + CW, CW), :]).then_inc(s.x_staged, 1)
                    split_rest(c)
                rounds(pool, CH - 1, turn)
                split_rest(CH - 1)

            @block.tensor
            def _(pe):
                pe.wait_ge(s.ident_set, 2)
                pe.wait_ge(s.const_set, 10)
                def turn(c):
                    pe.wait_ge(s.x_staged, c + 1)
                    for w in range(CW):
                        k = c * CW + w
                        xw = x_now[:, w, :]
                        if w < 2:
                            pe.wait_ge(s.xt_copied, c * CW)
                        else:
                            pe.wait_ge(s.xt_copied, k - 1)
                        for half in range(2):
                            last = nc.tensor.transpose(ps_x[w % 2][:, half * P:(half + 1) * P], xw[:, half * P:(half + 1) * P], t.ident[:, :])
                        last.then_inc(s.x_turned, 1)
                    pe.wait_ge(s.xt_copied, (c + 1) * CW)
                    pe.wait_ge(s.w_in, 16 * 7)
                    for m in range(HEADS * 2):
                        for nh in range(2):
                            k = m * 2 + nh
                            b = k % 2
                            if k < 2:
                                pe.wait_ge(s.hid_kept, c * HEADS * 4)
                            else:
                                pe.wait_ge(s.hid_kept, c * HEADS * 4 + k - 1)
                            half = CW * P // 2
                            for kk in range(2):
                                last = nc.tensor.matmul(ps_h[b][:, 0:half], w1[:, kk, m * P:(m + 1) * P],
                                                        x_t[:, kk, nh * half:(nh + 1) * half], start=kk == 0, stop=kk == 1)
                            last.then_inc(s.hid_made, 1)
                    pe.wait_ge(s.hid_kept, (c + 1) * HEADS * 4)
                    pe.wait_ge(s.w2x_set, 1)
                    for w in range(CW):
                        if w < 2:
                            pe.wait_ge(s.f_hi, c * CW)
                        else:
                            pe.wait_ge(s.f_hi, c * CW + w - 1)
                        nc.tensor.matmul(ps_f[w % 2][:, 0:HEADS * FH], t.ones[0:1, 0:P], b2x[0:1, :, :].rearrange("p h f -> p (h f)"),
                                         start=True, stop=False)
                        for h in range(HEADS):
                            for kk in range(2):
                                last = nc.tensor.matmul(ps_f[w % 2][:, h * FH:(h + 1) * FH], hid[:, 2 * h + kk, w * P:(w + 1) * P],
                                                        w2x[:, h, kk, :], start=False, stop=(h, kk) == (HEADS - 1, 1))
                        last.then_inc(s.f_made, 1)
                for c in range(COUNT_AFTER):
                    turn(c)
                pe.wait_ge(s.counted, 1)
                pe.wait_ge(s.tri_set, 2)
                nc.tensor.matmul(ps_c[:, 0:NW], below[:, :], cnt[:, 0:NW], start=True, stop=True)
                nc.tensor.matmul(ps_c[:, 64:64 + 2 * NW], t.ones[:, 0:P], cnt[:, :], start=True, stop=True).then_inc(s.totals, 1)
                with pe.Fori(COUNT_AFTER, CH) as c:
                    turn(c)

            @block.scalar
            def _(act):
                act.wait_ge(s.w_in, 16 * 7)
                def turn(c):
                    for w in range(CW):
                        act.wait_ge(s.x_turned, c * CW + w + 1)
                        nc.scalar.activation(x_t[:, :, w * P:(w + 1) * P], ps_x[w % 2][:, 0:2 * P].rearrange("p (k n) -> p k n", k=2),
                                             ACT.Copy).then_inc(s.xt_copied, 1)
                    for m in range(HEADS * 2):
                        for nh in range(2):
                            k = m * 2 + nh
                            half = CW * P // 2
                            act.wait_ge(s.hid_made, c * HEADS * 4 + k + 1)
                            nc.scalar.activation(hid[:, m, nh * half:(nh + 1) * half], ps_h[k % 2][:, 0:half], ACT.Relu,
                                                 bias=b1[:, m:m + 1]).then_inc(s.hid_kept, 1)
                    def second_part(w):
                        mid = t.table3[:, bass.ds(c * CW + w, 1), ROWW:ROWW + HEADS * FH].rearrange("p a f -> p (a f)")
                        act.wait_ge(s.f_res, c * CW + w + 1)
                        nc.scalar.activation(mid, ftmp[:, w, :], ACT.Copy).then_inc(s.f_mid, 1)
                    act.wait_ge(s.f_lo, c * CW)
                    for w in range(CW):
                        hi = t.table3[:, bass.ds(c * CW + w, 1), 0:HEADS * FH].rearrange("p a f -> p (a f)")
                        act.wait_ge(s.f_made, c * CW + w + 1)
                        nc.scalar.activation(ftmp[:, w, :], ps_f[w % 2][:, 0:HEADS * FH], ACT.Copy).then_inc(s.f_copied, 1)
                        nc.scalar.activation(hi, ps_f[w % 2][:, 0:HEADS * FH], ACT.Copy).then_inc(s.f_hi, 1)
                        if w >= 2:
                            second_part(w - 2)
                    second_part(CW - 2)
                    second_part(CW - 1)
                rounds(act, CH, turn)

            @block.vector
            def _(dve):
                done = [0]

                def step_done(ins):
                    done[0] += 1
                    ins.then_inc(s.d, 1)
                    dve.wait_ge(s.d, done[0])

                dve.wait_ge(s.w_in, 16 * 7)
                for h in range(HEADS):
                    for part in range(2):
                        a = aw[:, h, part * HD:(part + 1) * HD]
                        for q in range(3):
                            m = w2[:, h, q, :] if q < 2 else b2[:, h, :]
                            step_done(nc.vector.tensor_tensor_reduce(junk[:, :], m, a, 1.0, 0.0, ALU.mult, ALU.add,
                                                                     dots[:, h, q, part:part + 1]))
                nc.vector.tensor_copy(w2x[:, :, :, 0:HD], w2[:, :, :, :]).then_inc(s.prep, 1)
                nc.vector.tensor_copy(w2x[:, :, :, HD:FH], dots[:, :, 0:2, :]).then_inc(s.prep, 1)
                nc.vector.tensor_copy(b2x[:, :, 0:HD], b2[:, :, :]).then_inc(s.prep, 1)
                step_done(nc.vector.tensor_copy(b2x[:, :, HD:HD + 1], dots[:, :, 2, 0:1]))
                nc.vector.tensor_copy(t.elem_w[:, :], aw[:, :, 2 * HD]).then_inc(s.prep, 1)
                nc.vector.tensor_tensor(b2x[:, :, HD + 1], dots[:, :, 2, 1], ab[:, :], ALU.add).then_inc(s.prep, 1)
                dve.wait_ge(s.prep, 5)
                dve.sem_inc(s.w2x_set, 1)

                dve.wait_ge(s.e_in, 16 * 8)
                dve.wait_ge(s.const_set, 10)
                step_done(nc.vector.tensor_scalar(low_i[:, :], src_i[:, :], P - 1, None, ALU.bitwise_and))
                for c, v in ((0, dst_i), (1, src_i), (2, low_i), (4, wgt)):
                    step_done(nc.vector.tensor_copy(rec[:, :, c], v[:, :]))
                step_done(nc.vector.tensor_scalar(src_i[:, :], src_i[:, :], 7, None, ALU.arith_shift_right))
                step_done(nc.vector.tensor_copy(rec[:, :, 3], src_i[:, :]))
                step_done(nc.vector.memset(rec[:, :, 6:8], 0.0))
                for c, v in enumerate((low_i, dst_i, typ_i)):
                    step_done(nc.vector.tensor_copy(row16[:, c, :], v[:, :]))
                dve.sem_inc(s.rows16_set, 1)

                with dve.Fori(0, NW) as k:
                    row = mask[:, bass.ds(k, 1), :].rearrange("p a j -> p (a j)")
                    nc.vector.tensor_scalar(row, rec[:, :, 0], win_end[:, bass.ds(k, 1)], None, ALU.is_lt).then_inc(s.d, 1)
                done[0] += NW
                dve.wait_ge(s.d, done[0])
                step_done(nc.vector.tensor_reduce(cnt[:, NW:2 * NW], mask[:, :, :], AX.X, ALU.add))
                before = done[0]
                with dve.Fori(0, NW) as k:
                    row = mask[:, bass.ds(k, 1), :].rearrange("p a j -> p (a j)")
                    rnk = rank[:, bass.ds(k, 1), :].rearrange("p a j -> p (a j)")
                    nc.vector.tensor_scalar(row, rec[:, :, 3], win_no[:, bass.ds(k, 1)], None, ALU.is_equal).then_inc(s.d, 1)
                    dve.wait_ge(s.d, 2 * k + before + 1)
                    nc.vector.tensor_tensor_scan(rnk, ones_e[:, :], row, 0.0, ALU.mult, ALU.add).then_inc(s.d, 1)
                done[0] += 2 * NW
                dve.wait_ge(s.d, done[0])
                nc.vector.tensor_copy(cnt[:, 0:NW], rank[:, :, EPP - 1]).then_inc(s.counted, 1)
                dve.wait_ge(s.totals, 1)
                step_done(nc.vector.tensor_copy(tot[:, 0:NW], ps_c[:, 64:64 + NW]))
                step_done(nc.vector.tensor_copy(tot[:, NW:2 * NW], ps_c[:, 64 + NW:64 + 2 * NW]))
                step_done(nc.vector.tensor_copy(off[:, 1:NW + 1], tot[:, NW:2 * NW]))
                step_done(nc.vector.memset(off[:, 0:1], 0.0))
                step_done(nc.vector.tensor_tensor(tot[:, NW:2 * NW], off[:, 1:NW + 1], off[:, 0:NW], ALU.subtract))
                step_done(nc.vector.tensor_scalar(gi[:, :, :].rearrange("p a k -> p (a k)"), tot[:, :], float(GE - 1), None, ALU.add))
                step_done(nc.vector.tensor_scalar(gi[:, :, :], gi[:, :, :], 8, None, ALU.arith_shift_right))
                step_done(nc.vector.tensor_copy(grp[:, :, :], gi[:, :, :]))
                for a in range(2):
                    step_done(nc.vector.tensor_tensor_scan(cum[:, a, :], t.ones[:, 0:NW], grp[:, a, :], 0.0, ALU.mult, ALU.add))
                step_done(nc.vector.tensor_tensor(fst[:, :, :], cum[:, :, :], grp[:, :, :], ALU.subtract))
                step_done(nc.vector.tensor_scalar(base[:, :], fst[:, 0, :], float(GE), -1.0, ALU.mult, ALU.add))
                step_done(nc.vector.tensor_tensor(base[:, :], base[:, :], ps_c[:, 0:NW], ALU.add))
                step_done(nc.vector.tensor_scalar(fill[:, 0, :], cum[:, 0, :], -1.0, None, ALU.add))
                step_done(nc.vector.tensor_scalar(fill[:, 1, :], win_no[:, :], cum[:, 0, NW - 1:NW], None, ALU.add))
                step_done(nc.vector.tensor_scalar(no_fill[:, 0, :], grp[:, 0, :], 0.0, None, ALU.is_equal))
                step_done(nc.vector.tensor_scalar(no_fill[:, 1, :], fill[:, 1, :], float(NG), None, ALU.is_ge))
                step_done(nc.vector.tensor_scalar(fill[:, :, :], fill[:, :, :], float(GE), None, ALU.mult))
                step_done(nc.vector.tensor_tensor(scrap[:, :, :], scrap[:, :, :], fill[:, :, :], ALU.subtract))
                step_done(nc.vector.tensor_tensor(scrap[:, :, :], scrap[:, :, :], no_fill[:, :, :], ALU.mult))
                step_done(nc.vector.tensor_tensor(t.fill_at[:, :], fill[:, :, :].rearrange("p a k -> p (a k)"),
                                                  scrap[:, :, :].rearrange("p a k -> p (a k)"), ALU.add))
                dve.sem_inc(s.fill_set, 1)
                before = done[0]
                with dve.Fori(0, NW) as k:
                    row = mask[:, bass.ds(k, 1), :].rearrange("p a j -> p (a j)")
                    rnk = rank[:, bass.ds(k, 1), :].rearrange("p a j -> p (a j)")
                    nc.vector.scalar_tensor_tensor(rnk, rnk, base[:, bass.ds(k, 1)], row, ALU.add, ALU.mult).then_inc(s.d, 1)
                done[0] += NW
                dve.wait_ge(s.d, done[0])
                step_done(nc.vector.tensor_reduce(rec[:, :, 5], rank[:, :, :].rearrange("p k j -> p j k"), AX.X, ALU.add))
                dve.sem_inc(s.ranked, 1)

                def windows_passed(a):
                    step_done(nc.vector.tensor_tensor(reach[:, :, :], g_no[:, :].unsqueeze(2).broadcast_to([P, NG, NW]),
                                                      cum[:, a, :].unsqueeze(1).broadcast_to([P, NG, NW]), ALU.is_ge))
                    step_done(nc.vector.tensor_reduce(acc_f[:, a, :], reach[:, :, :], AX.X, ALU.add))
                    step_done(nc.vector.tensor_scalar(acc_f[:, a, :], acc_f[:, a, :], float(NW - 1), None, ALU.min))

                windows_passed(0)
                step_done(nc.vector.scalar_tensor_tensor(t.src_pair[:, :], acc_f[:, 0, 0::2], float(NW), acc_f[:, 0, 1::2], ALU.mult, ALU.add))
                windows_passed(1)
                step_done(nc.vector.tensor_copy(t.dst_win[:, :], acc_f[:, 1, :]))
                step_done(nc.vector.scalar_tensor_tensor(t.dst_pair[:, :], acc_f[:, 1, 0::2], float(NW), acc_f[:, 1, 1::2], ALU.mult, ALU.add))
                step_done(nc.vector.tensor_scalar(t.win_base[:, :], acc_f[:, 1, :], float(P), None, ALU.mult))
                step_done(nc.vector.tensor_scalar(t.win_lane[:, :], t.win_base[:, :], t.lane[:, 0:1], None, ALU.add))
                step_done(nc.vector.scalar_tensor_tensor(off[:, 0:NW], fst[:, 1, :], -float(GE), off[:, 0:NW], ALU.mult, ALU.add))
                step_done(nc.vector.tensor_tensor(step[:, 0:NW - 1], off[:, 1:NW], off[:, 0:NW - 1], ALU.subtract))
                step_done(nc.vector.memset(step[:, NW - 1:NW], float(2 * E)))
                step_done(nc.vector.tensor_tensor(reach_o[:, :, :], reach[:, :, :], step[:, :].unsqueeze(1).broadcast_to([P, NG, NW]), ALU.mult))
                step_done(nc.vector.tensor_reduce(acc_f[:, 2, :], reach_o[:, :, :], AX.X, ALU.add))
                step_done(nc.vector.scalar_tensor_tensor(acc_f[:, 3, :], g_no[:, :], float(GE), acc_f[:, 2, :], ALU.mult, ALU.add))
                step_done(nc.vector.tensor_scalar(t.first_edge[:, :], acc_f[:, 3, :], float(E), None, ALU.min))


def layer0_edges(nc, i, t):
    with ExitStack() as ctx:
        sb, psum, sems, slot_sems = allocators(nc, ctx, "layer0_edges")
        TERMS = NW + 2
        PAIRS = EL // 2
        DST_TERM, WEIGHT_TERM = NW * HEADS, (NW + 1) * HEADS
        wide = sb("wide", [P, EL, 2, GE], I16)
        hot = sb("hot", [P, EL, 2, GE], BF16)
        terms = sb("terms", [P, EL, TPG, TERMS * HEADS], F32)
        weighted = sb("weighted", [P, NT, HEADS], F32)
        row = sb("row", [P, EL, TPG, ROWW], F32)
        at = sb("at", [P, EL, TPG], U32)
        at_f = sb("at_f", [P, NT], F32)
        ps_f = [psum(f"ps_f{b}", [P, TPG, 512]) for b in range(2)]
        ps_a = [psum(f"ps_a{b}", [P, TPG, 256]) for b in range(2)]
        s = sems("d turn load_turn row_zero recorded")
        rec_in, wide_in, hot_made, a_ready, f_ready = slot_sems("rec_in wide_in hot_made a_ready f_ready")
        picked, terms_in, at_set, summed, f_copied = slot_sems("picked terms_in at_set summed f_copied")
        row_out = t.row_out
        with nc.Block() as block:
            @block.sync
            def _(sp):
                def turn(r, first):
                    for b in range(EL):
                        g = EL * r + b
                        if b % 2 == 0 and not first:
                            sp.wait_ge(s.recorded, PAIRS * r + b // 2 + 1 - PAIRS)
                            sp.sem_inc(s.load_turn, 1)
                        e0 = sp.value_load(t.first_edge[0:1, bass.ds(g, 1)], min_val=0, max_val=E)
                        sp.dma_start(t.edge[:, bass.ds(g * TPG, TPG), :],
                                     t.rec_dram[bass.ds(e0, GE), :].rearrange("(q p) c -> p q c", p=P)).then_inc(rec_in[b], 16)
                        sp.wait_ge(hot_made[b], r)
                        sp.sem_inc(s.load_turn, 1)
                        sp.dma_start(wide[:, b, :, :], t.row_dram[0:2, bass.ds(e0, GE)].partition_broadcast(P)).then_inc(wide_in[b], 16)
                turn(0, True)
                with sp.Fori(1, NG // EL) as r:
                    turn(r, False)

            @block.vector
            def _(dve):
                nc.vector.memset(row[:, :, :, D + HEADS:ROWW], 0.0).then_inc(s.row_zero, 1)

                def one_hots(r, b, g):
                    dve.wait_ge(wide_in[b], 16 * (r + 1))
                    dve.wait_ge(f_ready[b], r)
                    nc.vector.tensor_scalar(hot[:, b, 0, :], wide[:, b, 0, :], t.lane[:, 0:1], None, ALU.is_equal)
                    nc.vector.tensor_scalar(hot[:, b, 1, :], wide[:, b, 1, :], t.win_lane[:, bass.ds(g, 1)], None,
                                            ALU.is_equal).then_inc(hot_made[b], 1)

                STEPS = 4

                def records(r, pair):
                    n = (PAIRS * r + pair) * STEPS
                    tiles = bass.ds((EL * r + 2 * pair) * TPG, 2 * TPG)
                    groups = bass.ds(EL * r + 2 * pair, 2)
                    dst = t.edge[:, tiles, 0].rearrange("p (g q) -> p g q", q=TPG)
                    for b in (2 * pair, 2 * pair + 1):
                        dve.wait_ge(rec_in[b], 16 * (r + 1))
                    nc.vector.tensor_tensor(t.local[:, tiles].rearrange("p (g q) -> p g q", q=TPG), dst,
                                            t.win_base[:, groups].unsqueeze(2).broadcast_to([P, 2, TPG]), ALU.subtract).then_inc(s.d, 1)
                    nc.vector.tensor_tensor(weighted[:, tiles, :], t.edge[:, tiles, 4:5].broadcast_to([P, 2 * TPG, HEADS]),
                                            t.elem_w[:, :].unsqueeze(1).broadcast_to([P, 2 * TPG, HEADS]), ALU.mult).then_inc(s.d, 1)
                    dve.wait_ge(s.d, n + 2)
                    nc.vector.tensor_scalar(t.valid[:, tiles], t.local[:, tiles], float(P), None, ALU.is_lt).then_inc(s.d, 1)
                    dve.wait_ge(s.d, n + 3)
                    nc.vector.scalar_tensor_tensor(at_f[:, tiles], t.edge[:, tiles, 5], t.trash[:, 0:1], t.valid[:, tiles],
                                                   ALU.subtract, ALU.mult).then_inc(s.d, 1)
                    dve.wait_ge(s.d, n + 4)
                    dve.sem_inc(s.recorded, 1)

                def pick(r, b, g):
                    dve.wait_ge(a_ready[b], r + 1)
                    dve.wait_ge(summed[b], r)
                    for q in range(TPG):
                        nc.vector.scalar_tensor_tensor(terms[:, b, q, 0:NW * HEADS], t.win_of_col[:, :],
                                                       t.edge[:, bass.ds(g * TPG + q, 1), 3:4].rearrange("p a c -> p (a c)"),
                                                       ps_a[b % 2][:, q, 0:NW * HEADS], ALU.is_equal, ALU.mult).then_inc(picked[b], 1)

                def addresses(r, b, g):
                    dve.wait_ge(row_out[b], 16 * TPG * r)
                    nc.vector.tensor_scalar(at[:, b, :], at_f[:, bass.ds(g * TPG, TPG)], t.trash[:, 0:1], None, ALU.add).then_inc(at_set[b], 1)

                def sum_terms(r, b):
                    dve.wait_ge(picked[b], TPG * (r + 1))
                    dve.wait_ge(terms_in[b], 2 * (r + 1))
                    nc.vector.tensor_reduce(row[:, b, :, D:D + HEADS], terms[:, b, :, :].rearrange("p q (w h) -> p q h w", h=HEADS),
                                            AX.X, ALU.add).then_inc(summed[b], 1)

                def keep_scores(r):
                    dve.wait_ge(summed[EL - 1], r + 1)
                    nc.vector.tensor_scalar(t.score[:, bass.ds(r * EL * TPG, EL * TPG), :],
                                            row[:, :, :, D:D + HEADS].rearrange("p g q h -> p (g q) h"), 0.0, None, ALU.add)

                def body(r, last):
                    for b in range(EL):
                        pick(r, b, EL * r + b)
                        if b < EL - 2:
                            one_hots(r, b + 2, EL * r + b + 2)
                        elif not last:
                            one_hots(r + 1, b + 2 - EL, EL * r + b + 2)
                        addresses(r, b, EL * r + b)
                        if b % 2 == 1 and b < EL - 1:
                            records(r, b // 2 + 1)
                        elif b % 2 == 1 and not last:
                            records(r + 1, 0)
                        sum_terms(r, b)
                    keep_scores(r)

                one_hots(0, 0, 0)
                one_hots(0, 1, 1)
                records(0, 0)
                dve.wait_ge(s.row_zero, 1)
                body(0, False)
                with dve.Fori(1, NG // EL - 1) as r:
                    body(r, False)
                body(NG // EL - 1, True)

            @block.tensor
            def _(pe):
                def turn(r):
                    for b in range(EL):
                        win = pe.value_load(t.dst_win[0:1, bass.ds(EL * r + b, 1)], min_val=0, max_val=NW - 1)
                        pe.wait_ge(hot_made[b], r + 1)
                        pe.wait_ge(picked[(b - 2) % EL], TPG * (r + (b >= 2)))
                        for q in range(TPG):
                            for k in range(3):
                                last = nc.tensor.matmul(ps_a[b % 2][:, q, 0:NW * HEADS], hot[:, b, 0, q * P:(q + 1) * P],
                                                        t.table3[:, :, k * ROWW + HD:k * ROWW + HEADS * FH:FH],
                                                        start=k == 0, stop=k == 2)
                        last.then_inc(a_ready[b], 1)
                        pe.wait_ge(f_copied[(b - 2) % EL], r + (b >= 2))
                        for q in range(TPG):
                            for k in range(3):
                                feats = t.table3[:, bass.ds(win, 1), k * ROWW:k * ROWW + HEADS * FH].rearrange("p a f -> p (a f)")
                                last = nc.tensor.matmul(ps_f[b % 2][:, q, 0:HEADS * FH], hot[:, b, 1, q * P:(q + 1) * P], feats,
                                                        start=k == 0, stop=k == 2)
                        last.then_inc(f_ready[b], 1)
                rounds(pe, NG // EL, turn)

            @block.scalar
            def _(act):
                act.wait_ge(s.row_zero, 1)
                def turn(r):
                    for b in range(EL):
                        act.wait_ge(s.recorded, PAIRS * r + b // 2 + 1)
                        tiles = bass.ds((EL * r + b) * TPG, TPG)
                        act.wait_ge(summed[b], r)
                        nc.scalar.activation(terms[:, b, :, WEIGHT_TERM:WEIGHT_TERM + HEADS], weighted[:, tiles, :], ACT.Copy).then_inc(terms_in[b], 1)
                        act.wait_ge(row_out[b], 16 * TPG * r)
                        nc.scalar.activation(row[:, b, :, D + HEADS], t.edge[:, tiles, 2], ACT.Copy)
                        act.wait_ge(f_ready[b], r + 1)
                        nc.scalar.activation(terms[:, b, :, DST_TERM:DST_TERM + HEADS], ps_f[b % 2][:, :, HD + 1:HEADS * FH:FH],
                                             ACT.Copy).then_inc(terms_in[b], 1)
                        for q in range(TPG):
                            last = nc.scalar.activation(row[:, b, q, 0:D].rearrange("p (h f) -> p h f", h=HEADS),
                                                        ps_f[b % 2][:, q, 0:HEADS * FH].rearrange("p (h f) -> p h f", h=HEADS)[:, :, 0:HD],
                                                        ACT.Copy)
                        last.then_inc(f_copied[b], 1)
                rounds(act, NG // EL, turn)

            @block.gpsimd
            def _(pool):
                def turn(r):
                    for b in range(EL):
                        pool.wait_ge(f_copied[b], r + 1)
                        pool.wait_ge(at_set[b], r + 1)
                        pool.wait_ge(summed[b], r + 1)
                        pool.sem_inc(s.turn, 1)
                        for q in range(TPG):
                            pool.indirect_dma_start(t.rows_dram, bass.IndirectOffsetOnAxis(ap=at[:, b, q:q + 1], axis=0),
                                                    row[:, b, q, :], None, bounds_check=NROWS - 1,
                                                    oob_is_err=False).then_inc(row_out[b], 16)
                rounds(pool, NG // EL, turn)
                for b in range(EL):
                    pool.wait_ge(row_out[b], 16 * TPG * (NG // EL))


def layer0_sum(nc, i, t):
    with ExitStack() as ctx:
        sb, psum, sems, slot_sems = allocators(nc, ctx, "layer0_sum")
        hide = sb("hide", [P, NT], F32)
        masked = sb("masked", [P, NT, HEADS], F32)
        top_lane = sb("top_lane", [P, HEADS], F32)
        top = sb("top", [P, HEADS], F32)
        rin = sb("rin", [P, EL, TPG, ROWW], F32)
        rel = sb("rel", [P, EL, TPG, HEADS], F32)
        hot = sb("hot", [P, EL, TPG, P], F32)
        rhs = sb("rhs", [P, EL, TPG, D + HEADS], F32)
        ps = [psum(f"ps{b}", [P, 512]) for b in range(BANKS)]
        s = sems("d lane_top top_set acc_zero")
        rows_in, rel_made, hot_made, weighed, summed, kept = slot_sems("rows_in rel_made hot_made weighed summed kept")
        scaled_act, scaled_first, scaled_pool = slot_sems("scaled_act scaled_first scaled_pool")

        with nc.Block() as block:
            @block.sync
            def _(sp):
                def turn(r):
                    for b in range(EL):
                        sp.wait_ge(hot_made[b], r)
                        sp.wait_ge(rel_made[b], r)
                        sp.wait_ge(scaled_act[b], r)
                        sp.wait_ge(scaled_first[b], r)
                        sp.wait_ge(scaled_pool[b], r)
                        sp.dma_start(rin[:, b, :, :], t.rows_dram[bass.ds((EL * r + b) * GE, GE), :]
                                     .rearrange("(q p) c -> p q c", p=P)).then_inc(rows_in[b], 16)
                rounds(sp, NG // EL, turn)

            @block.gpsimd
            def _(pool):
                pool.memset(t.acc[:, :, :], 0.0).then_inc(s.acc_zero, 1)
                pool.wait_ge(s.lane_top, 1)
                pool.partition_all_reduce(top[:, :], top_lane[:, :], P, bass.bass_isa.ReduceOp.max).then_inc(s.top_set, 1)
                pool.wait_ge(s.top_set, 1)

                def below_top(r, b):
                    pool.wait_ge(rows_in[b], 16 * (r + 1))
                    pool.wait_ge(weighed[b], r)
                    nc.gpsimd.tensor_tensor(rel[:, b, :, :], rin[:, b, :, D:D + HEADS],
                                            top[:, :].unsqueeze(1).broadcast_to([P, TPG, HEADS]), ALU.subtract).then_inc(rel_made[b], 1)

                def scale(r, b):
                    pool.wait_ge(weighed[b], r + 1)
                    pool.wait_ge(summed[b], r)
                    nc.gpsimd.tensor_tensor(rhs[:, b, 0, 0:HD], rin[:, b, 0, 0:HD], rhs[:, b, 0, D:D + 1].broadcast_to([P, HD]),
                                            ALU.mult).then_inc(scaled_first[b], 1)
                    nc.gpsimd.tensor_tensor(rhs[:, b, 1, 0:D].rearrange("p (h f) -> p h f", h=HEADS),
                                            rin[:, b, 1, 0:D].rearrange("p (h f) -> p h f", h=HEADS),
                                            rhs[:, b, 1, D:D + HEADS].unsqueeze(2).broadcast_to([P, HEADS, HD]),
                                            ALU.mult).then_inc(scaled_pool[b], 1)
                with_ahead(pool, EL, 2, below_top, scale)

            @block.scalar
            def _(act):
                def weights(r, b):
                    act.wait_ge(rel_made[b], r + 1)
                    act.wait_ge(summed[b], r)
                    nc.scalar.activation(rhs[:, b, :, D:D + HEADS], rel[:, b, :, :], ACT.Exp).then_inc(weighed[b], 1)

                def scale(r, b):
                    act.wait_ge(weighed[b], r + 1)
                    for h in range(1, HEADS):
                        last = nc.scalar.activation(rhs[:, b, 0, h * HD:(h + 1) * HD], rin[:, b, 0, h * HD:(h + 1) * HD], ACT.Copy,
                                                    scale=rhs[:, b, 0, D + h:D + h + 1])
                    last.then_inc(scaled_act[b], 1)
                with_ahead(act, EL, 1, weights, scale)

            @block.tensor
            def _(pe):
                def turn(r):
                    for b in range(EL):
                        pe.wait_ge(hot_made[b], r + 1)
                        pe.wait_ge(scaled_act[b], r + 1)
                        pe.wait_ge(scaled_first[b], r + 1)
                        pe.wait_ge(scaled_pool[b], r + 1)
                        pe.wait_ge(kept[(b - BANKS) % EL], r + (b >= BANKS))
                        for q in range(TPG):
                            last = nc.tensor.matmul(ps[b % BANKS][:, 0:D + HEADS], hot[:, b, q, :], rhs[:, b, q, :],
                                                    start=q == 0, stop=q == TPG - 1)
                        last.then_inc(summed[b], 1)
                rounds(pe, NG // EL, turn)

            @block.vector
            def _(dve):
                nc.vector.tensor_scalar(hide[:, :], t.valid[:, :], 1.0, BIG, ALU.subtract, ALU.mult).then_inc(s.d, 1)
                dve.wait_ge(s.d, 1)
                nc.vector.tensor_tensor(masked[:, :, :], t.score[:, :, :], hide[:, :].unsqueeze(2).broadcast_to([P, NT, HEADS]),
                                        ALU.add).then_inc(s.d, 1)
                dve.wait_ge(s.d, 2)
                nc.vector.tensor_reduce(top_lane[:, :], masked[:, :, :].rearrange("p n h -> p h n"), AX.X, ALU.max).then_inc(s.lane_top, 1)
                dve.wait_ge(s.acc_zero, 1)

                def one_hots(r, b):
                    dve.wait_ge(rows_in[b], 16 * (r + 1))
                    dve.wait_ge(summed[b], r)
                    for q in range(TPG):
                        last = nc.vector.tensor_scalar(hot[:, b, q, :], t.cols[:, :], rin[:, b, q, D + HEADS:D + HEADS + 1], None, ALU.is_equal)
                    last.then_inc(hot_made[b], 1)

                pair = []

                def add_group(r, b):
                    if b % 2 == 0:
                        pair[:] = [dve.value_load(t.src_pair[0:1, bass.ds(EL // 2 * r + b // 2, 1)], min_val=0, max_val=NW * NW - 1)]
                    win = pair[0] // NW if b % 2 == 0 else pair[0] % NW
                    sums = t.acc[:, bass.ds(win, 1), 0:D + HEADS].rearrange("p a f -> p (a f)")
                    dve.wait_ge(summed[b], r + 1)
                    dve.wait_ge(kept[(b - 1) % EL], r + (b > 0))
                    nc.vector.tensor_tensor(sums, sums, ps[b % BANKS][:, 0:D + HEADS], ALU.add).then_inc(kept[b], 1)
                with_ahead(dve, EL, 3, one_hots, add_group)


MOMENT_STEPS = 2 * CW


def moments(nc, dve, d, n, carried, v, stats, mean_var, var_eps, var_made):
    dve.wait_ge(d, n)
    for w in range(CW):
        nc.vector.bn_stats(stats[:, w, :], v[:, w, :]).then_inc(d, 1)
    dve.wait_ge(d, n + CW)
    dve.sem_inc(carried, 1)
    for w in range(CW):
        nc.vector.bn_aggr(mean_var[:, w, :], stats[:, w, :]).then_inc(d, 1)
    dve.wait_ge(d, n + 2 * CW)
    nc.vector.tensor_scalar(var_eps[:, :], mean_var[:, :, 1], EPS, None, ALU.add).then_inc(var_made, 1)


def layer0_nodes(nc, i, t):
    with ExitStack() as ctx:
        sb, psum, sems, slot_sems = allocators(nc, ctx, "layer0_nodes")
        wqkv = sb("wqkv", [P, 2, 3 * D], F32)
        bqkv = sb("bqkv", [3, 3 * D], F32)
        b_part = sb("b_part", [3, 3, 3 * D], BF16)
        bqkv3 = sb("bqkv3", [3, 3 * D], BF16)
        ones3 = sb("ones3", [3, P], BF16)
        query = sb("query", [P, D], F32)
        node_no = sb("node_no", [P, NW], F32)
        zero_w = sb("zero_w", [P, CW, HEADS], F32)
        den = sb("den", [P, CW, HEADS], F32)
        v = sb("v", [P, CW, D], F32)
        any_zero = sb("any_zero", [P, CW], F32)
        stats = sb("stats", [P, CW, 6], F32)
        mean_var = sb("mean_var", [P, CW, 2], F32)
        var_eps = sb("var_eps", [P, CW], F32)
        rstd = sb("rstd", [P, CW], F32)
        enh = sb("enh", [P, CW, D], F32)
        enh_t = sb("enh_t", [P, 2, CW * P], F32)
        qtmp = sb("qtmp", [P, CW, D], F32)
        qres = sb("qres", [P, CW, D], F32)
        keys = sb("keys", [P, CW, D], F32)
        ps_x = [psum(f"ps_x{b}", [P, 512]) for b in range(4)]
        ps_qk = [psum(f"ps_qk{b}", [P, 512]) for b in range(2)]
        ps_v = [psum(f"ps_v{b}", [P, 512]) for b in range(2)]
        s = sems("b_in b w_in q_in pad_zero scaled d carried var_made rooted normed enh_made turned enh_t_made projected "
                 "q_hi q_rest q_mid q_lo kv_kept k_out v_out")
        with nc.Block() as block:
            @block.sync
            def _(sp):
                for c, w in enumerate((i.L1_gnn_Wq, i.L1_gnn_Wk, i.L1_gnn_Wv)):
                    sp.dma_start(wqkv[:, :, c * D:(c + 1) * D], w.rearrange("(k p) m -> p k m", p=P)).then_inc(s.w_in, 16)
                for c, w in enumerate((i.L1_gnn_bq, i.L1_gnn_bk, i.L1_gnn_bv)):
                    sp.dma_start(bqkv[:, c * D:(c + 1) * D], w.partition_broadcast(3)).then_inc(s.b_in, 16)
                sp.dma_start(query[:, :], i.L1_gnn_query_emb.partition_broadcast(P)).then_inc(s.q_in, 16)
                def turn(c):
                    sp.wait_ge(s.kv_kept, (c + 1) * CW)
                    sp.dma_start(t.key_dram[bass.ds(c * CW * P, CW * P), :].rearrange("(w p) m -> p w m", p=P), keys[:, :, :]).then_inc(s.k_out, 16)
                    sp.dma_start(t.val_dram[bass.ds(c * CW * P, CW * P), :].rearrange("(w p) m -> p w m", p=P),
                                 t.val[:, bass.ds(c * CW, CW), :]).then_inc(s.v_out, 16)
                    both = t.both_dram[bass.ds(c * CW * P, CW * P), :].rearrange("(w p) m -> p w m", p=P)
                    sp.dma_start(both[:, :, 0:D], keys[:, :, :]).then_inc(s.k_out, 16)
                    sp.dma_start(both[:, :, D:D + VROW], t.val[:, bass.ds(c * CW, CW), :]).then_inc(s.v_out, 16)
                rounds(sp, CH, turn)
                sp.wait_ge(s.k_out, 32 * CH)
                sp.wait_ge(s.v_out, 32 * CH)

            @block.gpsimd
            def _(pool):
                pool.memset(t.val[:, :, D:VROW], 0.0).then_inc(s.pad_zero, 1)
                pool.memset(ones3[:, :], 1.0).then_inc(s.pad_zero, 1)
                pool.iota(node_no[:, :], pattern=[[P, NW]], base=0, channel_multiplier=1,
                          allow_small_or_imprecise_dtypes=True).then_inc(s.pad_zero, 1)
                pool.wait_ge(s.q_in, 16)
                pool.tensor_scalar(query[:, :], query[:, :], 0.1, None, ALU.mult).then_inc(s.scaled, 1)

            @block.vector
            def _(dve):
                dve.wait_ge(s.pad_zero, 3)

                def norm(c):
                    n = c * DSTEPS
                    weights = t.acc[:, bass.ds(c * CW, CW), D:D + HEADS]
                    x = t.x[:, bass.ds(c * CW, CW), :]
                    nc.vector.tensor_scalar(zero_w[:, :, :], weights, 0.0, None, ALU.is_equal).then_inc(s.d, 1)
                    dve.wait_ge(s.d, n + 1)
                    nc.vector.tensor_tensor(den[:, :, :], weights, zero_w[:, :, :], ALU.add).then_inc(s.d, 1)
                    nc.vector.tensor_reduce(any_zero[:, :], zero_w[:, :, :], AX.X, ALU.max).then_inc(s.d, 1)
                    dve.wait_ge(s.d, n + 2)
                    nc.vector.reciprocal(den[:, :, :], den[:, :, :]).then_inc(s.d, 1)
                    dve.wait_ge(s.d, n + 3)
                    nc.vector.scalar_tensor_tensor(t.val[:, bass.ds(c * CW, CW), D], node_no[:, bass.ds(c * CW, CW)], float(N), any_zero[:, :],
                                                   ALU.is_lt, ALU.mult).then_inc(s.d, 1)
                    dve.wait_ge(s.d, n + 5)
                    for w in range(CW):
                        nc.vector.tensor_tensor(v[:, w, :].rearrange("p (h f) -> p h f", h=HEADS),
                                                t.acc[:, bass.ds(c * CW + w, 1), 0:D].rearrange("p a (h f) -> p (a h) f", h=HEADS),
                                                den[:, w, :].unsqueeze(2).broadcast_to([P, HEADS, HD]), ALU.mult).then_inc(s.d, 1)
                    dve.wait_ge(s.d, n + 5 + CW)
                    nc.vector.tensor_tensor(v[:, :, :], v[:, :, :], x, ALU.add).then_inc(s.d, 1)
                    moments(nc, dve, s.d, n + 6 + CW, s.carried, v, stats, mean_var, var_eps, s.var_made)
                    dve.wait_ge(s.rooted, c + 1)
                    nc.vector.reciprocal(rstd[:, :], rstd[:, :]).then_inc(s.d, 1)
                    dve.wait_ge(s.d, n + DSTEPS)
                    for w in range(CW):
                        nc.vector.tensor_scalar(t.x[:, bass.ds(c * CW + w, 1), :].rearrange("p a m -> p (a m)"), v[:, w, :],
                                                mean_var[:, w, 0:1], rstd[:, w:w + 1], ALU.subtract, ALU.mult).then_inc(s.normed, 1)
                    dve.wait_ge(s.normed, (c + 1) * CW)
                    dve.wait_ge(s.scaled, 1)
                    dve.wait_ge(s.turned, c * CW)
                    nc.vector.tensor_tensor(enh[:, :, :], x, query[:, :].unsqueeze(1).broadcast_to([P, CW, D]), ALU.add).then_inc(s.enh_made, 1)

                DSTEPS = 6 + CW + MOMENT_STEPS + 1

                def query_part(c, w, part):
                    return t.table3[:, bass.ds(c * CW + w, 1), part * ROWW:part * ROWW + D].rearrange("p a m -> p (a m)")

                def queries_rest(c):
                    def third(w):
                        dve.wait_ge(s.q_mid, c * CW + w + 1)
                        nc.vector.tensor_tensor(query_part(c, w, 2), qres[:, w, :], query_part(c, w, 1), ALU.subtract).then_inc(s.q_lo, 1)
                    for w in range(CW):
                        dve.wait_ge(s.q_hi, c * CW + w + 1)
                        nc.vector.tensor_tensor(qres[:, w, :], qtmp[:, w, :], query_part(c, w, 0), ALU.subtract).then_inc(s.q_rest, 1)
                        if w >= 2:
                            third(w - 2)
                    third(CW - 2)
                    third(CW - 1)

                norm(0)
                dve.wait_ge(s.b_in, 16 * 3)
                parts = (lambda: nc.vector.tensor_copy(b_part[:, 0, :], bqkv[:, :]),
                         lambda: nc.vector.tensor_tensor(bqkv[:, :], bqkv[:, :], b_part[:, 0, :], ALU.subtract),
                         lambda: nc.vector.tensor_copy(b_part[:, 1, :], bqkv[:, :]),
                         lambda: nc.vector.tensor_tensor(b_part[:, 2, :], bqkv[:, :], b_part[:, 1, :], ALU.subtract),
                         lambda: nc.vector.tensor_scalar(bqkv3[:, :], b_part[:, 0, :], t.ident[0:3, 0:1], None, ALU.mult),
                         lambda: nc.vector.scalar_tensor_tensor(bqkv3[:, :], b_part[:, 1, :], t.ident[0:3, 1:2], bqkv3[:, :], ALU.mult, ALU.add),
                         lambda: nc.vector.scalar_tensor_tensor(bqkv3[:, :], b_part[:, 2, :], t.ident[0:3, 2:3], bqkv3[:, :], ALU.mult, ALU.add))
                for n, make in enumerate(parts):
                    make().then_inc(s.b, 1)
                    dve.wait_ge(s.b, n + 1)
                norm(1)
                queries_rest(0)
                with dve.Fori(1, CH - 1) as c:
                    norm(c + 1)
                    queries_rest(c)
                queries_rest(CH - 1)

            @block.scalar
            def _(act):
                def root(c):
                    act.wait_ge(s.var_made, c + 1)
                    nc.scalar.activation(rstd[:, :], var_eps[:, :], ACT.Sqrt).then_inc(s.rooted, 1)

                def turned_kept(c):
                    for w in range(CW):
                        act.wait_ge(s.turned, c * CW + w + 1)
                        nc.scalar.activation(enh_t[:, :, w * P:(w + 1) * P], ps_x[w % 4][:, 0:2 * P].rearrange("p (k n) -> p k n", k=2),
                                             ACT.Copy).then_inc(s.enh_t_made, 1)

                def second_part(c, w):
                    act.wait_ge(s.q_rest, c * CW + w + 1)
                    nc.scalar.activation(t.table3[:, bass.ds(c * CW + w, 1), ROWW:ROWW + D].rearrange("p a m -> p (a m)"), qres[:, w, :],
                                         ACT.Copy).then_inc(s.q_mid, 1)

                def projections_kept(c):
                    act.wait_ge(s.k_out, 32 * c)
                    act.wait_ge(s.q_lo, c * CW)
                    for w in range(CW):
                        k, b = c * CW + w, w % 2
                        act.wait_ge(s.projected, k + 1)
                        nc.scalar.activation(qtmp[:, w, :], ps_qk[b][:, 0:D], ACT.Copy)
                        nc.scalar.activation(t.table3[:, bass.ds(k, 1), 0:D].rearrange("p a m -> p (a m)"), ps_qk[b][:, 0:D], ACT.Copy).then_inc(s.q_hi, 1)
                        nc.scalar.activation(keys[:, w, :], ps_qk[b][:, D:2 * D], ACT.Copy)
                        nc.scalar.activation(t.val[:, bass.ds(k, 1), 0:D].rearrange("p a m -> p (a m)"), ps_v[b][:, 0:D], ACT.Copy).then_inc(s.kv_kept, 1)
                        if w >= 2:
                            second_part(c, w - 2)
                    second_part(c, CW - 2)
                    second_part(c, CW - 1)

                root(0)
                turned_kept(0)
                root(1)
                projections_kept(0)
                with act.Fori(1, CH - 1) as c:
                    turned_kept(c)
                    root(c + 1)
                    projections_kept(c)
                turned_kept(CH - 1)
                projections_kept(CH - 1)

            @block.tensor
            def _(pe):
                pe.wait_ge(s.w_in, 16 * 3)
                pe.wait_ge(s.b, 7)
                pe.wait_ge(s.pad_zero, 3)
                def turn(c):
                    pe.wait_ge(s.enh_made, c + 1)
                    for w in range(CW):
                        if w < 4:
                            pe.wait_ge(s.enh_t_made, c * CW)
                        else:
                            pe.wait_ge(s.enh_t_made, c * CW + w - 3)
                        for half in range(2):
                            last = nc.tensor.transpose(ps_x[w % 4][:, half * P:(half + 1) * P], enh[:, w, half * P:(half + 1) * P], t.ident[:, :])
                        last.then_inc(s.turned, 1)
                    for w in range(CW):
                        pe.wait_ge(s.enh_t_made, c * CW + w + 1)
                        b = w % 2
                        if w < 2:
                            pe.wait_ge(s.kv_kept, c * CW)
                        else:
                            pe.wait_ge(s.kv_kept, c * CW + w - 1)
                        for k in range(2):
                            nc.tensor.matmul(ps_qk[b][:, :], enh_t[:, k, w * P:(w + 1) * P], wqkv[:, k, 0:2 * D], start=k == 0, stop=False)
                        nc.tensor.matmul(ps_qk[b][:, :], ones3[:, :], bqkv3[:, 0:2 * D], start=False, stop=True)
                        for k in range(2):
                            nc.tensor.matmul(ps_v[b][:, 0:D], enh_t[:, k, w * P:(w + 1) * P], wqkv[:, k, 2 * D:3 * D], start=k == 0, stop=False)
                        nc.tensor.matmul(ps_v[b][:, 0:D], ones3[:, :], bqkv3[:, 2 * D:3 * D], start=False, stop=True).then_inc(s.projected, 1)
                rounds(pe, CH, turn)


def layer1_scores(nc, i, t):
    with ExitStack() as ctx:
        sb, psum, sems, slot_sems = allocators(nc, ctx, "layer1_scores")
        rel = sb("rel", [RELS, HD], F32)
        rel_rest = sb("rel_rest", [RELS, HD], F32)
        rel3 = sb("rel3", [RELS, 3, HD], BF16)
        wide = sb("wide", [P, EL, 2, GE], I16)
        hot = sb("hot", [P, EL, GE], BF16)
        hot_r = sb("hot_r", [RELS, EL, GE], BF16)
        at = sb("at", [P, EL, TPG], U32)
        key = sb("key", [P, EL // 2, TPG, D], F32)
        both = sb("both", [P, EL // 2, TPG, D + VROW], F32)
        prod = sb("prod", [P, BANKS, TPG, D], F32)
        ps_q = [psum(f"ps_q{b}", [P, TPG, D]) for b in range(BANKS)]
        ps_r = [psum(f"ps_r{b}", [P, 512]) for b in range(2)]
        s = sems("rel_in d turn load_turn")
        wide_in, hot_made, q_ready, at_set, with_rel, multiplied, reduced, val_out = slot_sems(
            "wide_in hot_made q_ready at_set with_rel multiplied reduced val_out")
        key_in = t.key_in

        def gathered(b, q):
            return key[:, b // 2, q, :] if b % 2 == 0 else both[:, b // 2, q, :]

        with nc.Block() as block:
            @block.sync
            def _(sp):
                sp.dma_start(rel[:, :], i.L1_gnn_rel_w).then_inc(s.rel_in, 16)
                def store_values(r, b):
                    sp.wait_ge(key_in[b], 16 * TPG * (r + 1))
                    sp.dma_start(t.slot_val_dram[bass.ds((EL * r + b) * GE, GE), :].rearrange("(q p) c -> p q c", p=P),
                                 both[:, b // 2, :, D:D + VROW]).then_inc(val_out[b], 16)

                def turn(r, stored):
                    for b in range(EL):
                        if b % 2 == 1 and stored:
                            store_values(r - 1, b)
                        e0 = sp.value_load(t.first_edge[0:1, bass.ds(EL * r + b, 1)], min_val=0, max_val=E)
                        sp.wait_ge(hot_made[b], r)
                        sp.sem_inc(s.load_turn, 1)
                        sp.dma_start(wide[:, b, :, :], t.row_dram[1:3, bass.ds(e0, GE)].partition_broadcast(P)).then_inc(wide_in[b], 16)
                turn(0, False)
                with sp.Fori(1, NG // EL) as r:
                    turn(r, True)
                for b in range(1, EL, 2):
                    store_values(NG // EL - 1, b)
                for b in range(1, EL, 2):
                    sp.wait_ge(val_out[b], 16 * (NG // EL))

            @block.gpsimd
            def _(pool):
                def turn(r):
                    for b in range(EL):
                        pool.wait_ge(at_set[b], r + 1)
                        pool.wait_ge(multiplied[b], r)
                        if b % 2 == 1:
                            pool.wait_ge(val_out[b], 16 * r)
                        pool.sem_inc(s.turn, 1)
                        for q in range(TPG):
                            pool.indirect_dma_start(gathered(b, q), None, t.key_dram if b % 2 == 0 else t.both_dram,
                                                    bass.IndirectOffsetOnAxis(ap=at[:, b, q:q + 1], axis=0)).then_inc(key_in[b], 16)
                rounds(pool, NG // EL, turn)

            @block.tensor
            def _(pe):
                def turn(r):
                    for b in range(EL):
                        win = pe.value_load(t.dst_win[0:1, bass.ds(EL * r + b, 1)], min_val=0, max_val=NW - 1)
                        pe.wait_ge(hot_made[b], r + 1)
                        pe.wait_ge(multiplied[(b - BANKS) % EL], r + (b >= BANKS))
                        for q in range(TPG):
                            for k in range(3):
                                nc.tensor.matmul(ps_q[b % BANKS][:, q, :], hot[:, b, q * P:(q + 1) * P],
                                                 t.table3[:, bass.ds(win, 1), k * ROWW:k * ROWW + D].rearrange("p a m -> p (a m)"),
                                                 start=k == 0, stop=k == 2)
                        pe.wait_ge(with_rel[(b - 2) % EL], r + (b >= 2))
                        for q in range(TPG):
                            for k in range(3):
                                last = nc.tensor.matmul(ps_r[b % 2][:, q * HD:(q + 1) * HD], hot_r[:, b, q * P:(q + 1) * P], rel3[:, k, :],
                                                        start=k == 0, stop=k == 2)
                        last.then_inc(q_ready[b], 1)
                rounds(pe, NG // EL, turn)

            @block.vector
            def _(dve):
                dve.wait_ge(s.rel_in, 16)
                steps = (lambda: nc.vector.tensor_scalar(rel[:, :], rel[:, :], 0.2, None, ALU.mult),
                         lambda: nc.vector.tensor_copy(rel3[:, 0, :], rel[:, :]),
                         lambda: nc.vector.tensor_tensor(rel_rest[:, :], rel[:, :], rel3[:, 0, :], ALU.subtract),
                         lambda: nc.vector.tensor_copy(rel3[:, 1, :], rel_rest[:, :]),
                         lambda: nc.vector.tensor_tensor(rel3[:, 2, :], rel_rest[:, :], rel3[:, 1, :], ALU.subtract))
                for n, make in enumerate(steps):
                    make().then_inc(s.d, 1)
                    dve.wait_ge(s.d, n + 1)

                def one_hots(r, b, g):
                    dve.wait_ge(wide_in[b], 16 * (r + 1))
                    dve.wait_ge(q_ready[b], r)
                    nc.vector.tensor_scalar(hot[:, b, :], wide[:, b, 0, :], t.win_lane[:, bass.ds(g, 1)], None, ALU.is_equal)
                    nc.vector.tensor_scalar(hot_r[:, b, :], wide[0:RELS, b, 1, :], t.lane[0:RELS, 0:1], None, ALU.is_equal).then_inc(hot_made[b], 1)

                def addresses(r, b, g):
                    dve.wait_ge(key_in[b], 16 * TPG * r)
                    nc.vector.tensor_scalar(at[:, b, :], t.edge[:, bass.ds(g * TPG, TPG), 1], float(NPAD - 1), None, ALU.min).then_inc(at_set[b], 1)

                def multiply(r, b):
                    dve.wait_ge(key_in[b], 16 * TPG * (r + 1))
                    dve.wait_ge(q_ready[b], r + 1)
                    dve.wait_ge(reduced[(b - BANKS) % EL], r + (b >= BANKS))
                    for q in range(TPG):
                        ins = nc.vector.tensor_tensor(prod[:, b % BANKS, q, :].rearrange("p (h f) -> p h f", h=HEADS),
                                                      gathered(b, q)[:, 0:D].rearrange("p (h f) -> p h f", h=HEADS),
                                                      ps_r[b % 2][:, q * HD:(q + 1) * HD].unsqueeze(1).broadcast_to([P, HEADS, HD]), ALU.add)
                    ins.then_inc(with_rel[b], 1)
                    dve.wait_ge(with_rel[b], r + 1)
                    nc.vector.tensor_tensor(prod[:, b % BANKS, :, :], prod[:, b % BANKS, :, :], ps_q[b % BANKS][:, :, :], ALU.mult).then_inc(multiplied[b], 1)

                def body(r, last):
                    for b in range(EL):
                        if b < EL - 1:
                            one_hots(r, b + 1, EL * r + b + 1)
                        elif not last:
                            one_hots(r + 1, 0, EL * r + EL)
                        multiply(r, b)
                        if not last:
                            addresses(r + 1, b, EL * r + b + EL)

                for b in range(EL):
                    addresses(0, b, b)
                one_hots(0, 0, 0)
                body(0, False)
                with dve.Fori(1, NG // EL - 1) as r:
                    body(r, False)
                body(NG // EL - 1, True)

            @block.scalar
            def _(act):
                def turn(r):
                    for b in range(EL):
                        g = EL * r + b
                        act.wait_ge(multiplied[b], r + 1)
                        for q in range(TPG):
                            for h in range(HEADS):
                                terms = prod[:, b % BANKS, q, h * HD:(h + 1) * HD]
                                last = nc.scalar.activation(terms, terms, ACT.Copy,
                                                            accum_out=t.score[:, bass.ds(g * TPG + q, 1), h])
                        last.then_inc(reduced[b], 1)
                rounds(act, NG // EL, turn)


def segment_max(nc, i, t):
    TB = P // HEADS
    NB = -(-NT // TB)
    NTP = NB * TB
    with ExitStack() as ctx:
        sb, psum, sems, slot_sems = allocators(nc, ctx, "segment_max")
        hide = sb("hide", [P, NT], F32)
        masked = sb("masked", [P, NTP, HEADS], F32)
        keys = sb("keys", [P, NTP, HEADS], F32)
        key1 = sb("key1", [P, NT], F32)
        val = sb("val", [P, NB, P], F32)
        key = sb("key", [P, NB, P], F32)
        spare = t.acc[:, :, :].rearrange("p w f -> p (w f)")
        starts, ends, fwd = (spare[:, k * NB * P:(k + 1) * NB * P].rearrange("p (b e) -> p b e", e=P) for k in range(3))
        bwd = sb("bwd", [P, NB, P], F32)
        edge4 = sb("edge4", [P, NB, 4], F32)
        by_tile = sb("by_tile", [HEADS, NTP, 4], F32)
        whole = sb("whole", [HEADS, NTP], F32)
        joined = sb("joined", [HEADS, NTP + 1], F32)
        gate = sb("gate", [HEADS, NTP], F32)
        run = sb("run", [HEADS, NTP], F32)
        carry = sb("carry", [HEADS, NTP, 2], F32)
        carry_b = sb("carry_b", [P, NB, 2], F32)
        ps = [psum(f"ps{b}", [P, 4, P]) for b in range(2)]
        s = sems("pads d laid turned kept edge_out tile_in carry_out carry_in max_made back added weights")
        BLOCKS4 = [(b, min(4, NB - b)) for b in range(0, NB, 4)]

        with nc.Block() as block:
            @block.gpsimd
            def _(pool):
                pool.memset(masked[:, NT:NTP, :], -BIG).then_inc(s.pads, 1)
                pool.memset(keys[:, NT:NTP, :], -1.0).then_inc(s.pads, 1)

            @block.tensor
            def _(pe):
                pe.wait_ge(s.laid, 1)
                n = 0
                for what in (masked, keys):
                    flat = what[:, :, :].rearrange("p n h -> p (n h)")
                    for b0, m in BLOCKS4:
                        if n >= 2:
                            pe.wait_ge(s.kept, n - 1)
                        for q in range(m):
                            last = nc.tensor.transpose(ps[n % 2][:, q, :], flat[:, (b0 + q) * P:(b0 + q + 1) * P], t.ident[:, :])
                        last.then_inc(s.turned, 1)
                        n += 1
                pe.wait_ge(s.max_made, 1)
                for b0, m in BLOCKS4:
                    pe.wait_ge(s.kept, n - 1)
                    for q in range(m):
                        last = nc.tensor.transpose(ps[n % 2][:, q, :], fwd[:, b0 + q, :], t.ident[:, :])
                    last.then_inc(s.turned, 1)
                    n += 1

            @block.scalar
            def _(act):
                n = 0
                for to in (val, key):
                    for b0, m in BLOCKS4:
                        act.wait_ge(s.turned, n + 1)
                        nc.scalar.activation(to[:, b0:b0 + m, :], ps[n % 2][:, 0:m, :], ACT.Copy).then_inc(s.kept, 1)
                        n += 1
                flat = keys[:, :, :].rearrange("p n h -> p (n h)")
                for b0, m in BLOCKS4:
                    act.wait_ge(s.turned, n + 1)
                    nc.scalar.activation(flat[:, b0 * P:(b0 + m) * P], ps[n % 2][:, 0:m, :].rearrange("p a e -> p (a e)"), ACT.Copy).then_inc(s.kept, 1)
                    n += 1
                act.wait_ge(s.added, 1)
                nc.scalar.activation(t.score[:, :, :], t.score[:, :, :], ACT.Exp, scale=float(HD) ** -0.5).then_inc(s.weights, 1)

            @block.sync
            def _(sp):
                rows = t.edge_dram.rearrange("(b p c) -> p b c", p=P, c=4)
                tiles = t.edge_dram.rearrange("(n h c) -> h n c", h=HEADS, c=4)
                crows = t.carry_dram.rearrange("(b p c) -> p b c", p=P, c=2)
                ctiles = t.carry_dram.rearrange("(n h c) -> h n c", h=HEADS, c=2)
                sp.wait_ge(s.edge_out, 1)
                sp.dma_start(rows, edge4[:, :, :]).then_inc(s.edge_out, 16)
                sp.wait_ge(s.edge_out, 17)
                sp.dma_start(by_tile[:, :, :], tiles).then_inc(s.tile_in, 16)
                sp.wait_ge(s.carry_out, 1)
                sp.dma_start(ctiles, carry[:, :, :]).then_inc(s.carry_out, 16)
                sp.wait_ge(s.carry_out, 17)
                sp.dma_start(carry_b[:, :, :], crows).then_inc(s.carry_in, 16)

            @block.vector
            def _(dve):
                done = [0]

                def step_done(ins):
                    done[0] += 1
                    ins.then_inc(s.d, 1)
                    dve.wait_ge(s.d, done[0])

                v = nc.vector
                tt, ts, stt = v.tensor_tensor, v.tensor_scalar, v.scalar_tensor_tensor
                step_done(ts(hide[:, :], t.valid[:, :], 1.0, BIG, ALU.subtract, ALU.mult))
                step_done(tt(masked[:, 0:NT, :], t.score[:, :, :], t.valid[:, :].unsqueeze(2).broadcast_to([P, NT, HEADS]), ALU.mult))
                step_done(tt(masked[:, 0:NT, :], masked[:, 0:NT, :], hide[:, :].unsqueeze(2).broadcast_to([P, NT, HEADS]), ALU.add))
                step_done(stt(key1[:, :], t.edge[:, :, 0], 1.0, t.valid[:, :], ALU.add, ALU.mult))
                step_done(ts(key1[:, :], key1[:, :], -1.0, None, ALU.add))
                step_done(v.tensor_copy(keys[:, 0:NT, :], key1[:, :].unsqueeze(2).broadcast_to([P, NT, HEADS])))
                dve.wait_ge(s.pads, 2)
                dve.sem_inc(s.laid, 1)
                dve.wait_ge(s.kept, 2 * len(BLOCKS4))
                step_done(v.memset(starts[:, :, 0:1], -BIG))
                step_done(v.memset(ends[:, :, P - 1:P], -BIG))
                step_done(tt(starts[:, :, 1:P], key[:, :, 1:P], key[:, :, 0:P - 1], ALU.not_equal))
                step_done(ts(starts[:, :, 1:P], starts[:, :, 1:P], -BIG, None, ALU.mult))
                step_done(v.tensor_copy(ends[:, :, 0:P - 1], starts[:, :, 1:P]))
                flat = lambda a: a[:, :, :].rearrange("p b e -> p (b e)")
                step_done(v.tensor_tensor_scan(flat(fwd), flat(starts), flat(val), -BIG, ALU.add, ALU.max))
                step_done(v.tensor_tensor_scan(flat(bwd)[:, ::-1], flat(ends)[:, ::-1], flat(val)[:, ::-1], -BIG, ALU.add, ALU.max))
                step_done(tt(val[:, :, :], fwd[:, :, :], bwd[:, :, :], ALU.max))
                step_done(v.tensor_copy(edge4[:, :, 0:1], key[:, :, 0:1]))
                step_done(v.tensor_copy(edge4[:, :, 1:2], key[:, :, P - 1:P]))
                step_done(v.tensor_copy(edge4[:, :, 2:3], val[:, :, 0:1]))
                v.tensor_copy(edge4[:, :, 3:4], val[:, :, P - 1:P]).then_inc(s.edge_out, 1)
                dve.wait_ge(s.tile_in, 16)
                k0, k1, m0, m1 = (by_tile[:, :, c] for c in range(4))
                step_done(tt(whole[:, :], k0, k1, ALU.is_equal))
                step_done(v.memset(joined[:, :], 0.0))
                step_done(tt(joined[:, 1:NTP], k0[:, 1:NTP], k1[:, 0:NTP - 1], ALU.is_equal))
                step_done(tt(gate[:, :], whole[:, :], joined[:, 0:NTP], ALU.mult))
                step_done(ts(gate[:, :], gate[:, :], 1.0, BIG, ALU.subtract, ALU.mult))
                step_done(v.tensor_tensor_scan(run[:, :], gate[:, :], m1, -BIG, ALU.add, ALU.max))
                step_done(v.memset(carry[:, :, :], -BIG))
                step_done(ts(gate[:, :], joined[:, 0:NTP], 1.0, BIG, ALU.subtract, ALU.mult))
                step_done(tt(carry[:, 1:NTP, 0], run[:, 0:NTP - 1], gate[:, 1:NTP], ALU.add))
                step_done(tt(gate[:, :], whole[:, :], joined[:, 1:NTP + 1], ALU.mult))
                step_done(ts(gate[:, :], gate[:, :], 1.0, BIG, ALU.subtract, ALU.mult))
                step_done(v.tensor_tensor_scan(run[:, ::-1], gate[:, ::-1], m0[:, ::-1], -BIG, ALU.add, ALU.max))
                step_done(ts(gate[:, :], joined[:, 1:NTP + 1], 1.0, BIG, ALU.subtract, ALU.mult))
                step_done(tt(carry[:, 0:NTP - 1, 1], run[:, 1:NTP], gate[:, 0:NTP - 1], ALU.add))
                v.nop().then_inc(s.carry_out, 1)
                bc = lambda a: a.broadcast_to([P, NB, P])
                step_done(tt(starts[:, :, :], key[:, :, :], bc(key[:, :, 0:1]), ALU.is_equal))
                step_done(tt(ends[:, :, :], key[:, :, :], bc(key[:, :, P - 1:P]), ALU.is_equal))
                for a in (starts, ends):
                    step_done(ts(a[:, :, :], a[:, :, :], 1.0, BIG, ALU.subtract, ALU.mult))
                dve.wait_ge(s.carry_in, 16)
                for a, c in ((starts, 0), (ends, 1)):
                    step_done(tt(a[:, :, :], a[:, :, :], bc(carry_b[:, :, c:c + 1]), ALU.add))
                    step_done(tt(val[:, :, :], val[:, :, :], a[:, :, :], ALU.max))
                v.tensor_copy(fwd[:, :, :], val[:, :, :]).then_inc(s.max_made, 1)
                dve.wait_ge(s.kept, 3 * len(BLOCKS4))
                tt(t.score[:, :, :], masked[:, 0:NT, :], keys[:, 0:NT, :], ALU.subtract).then_inc(s.added, 1)
                dve.wait_ge(s.weights, 1)
                step_done(tt(t.score[:, :, :], t.score[:, :, :], t.valid[:, :].unsqueeze(2).broadcast_to([P, NT, HEADS]), ALU.mult))


def layer1_sum(nc, i, t):
    with ExitStack() as ctx:
        sb, psum, sems, slot_sems = allocators(nc, ctx, "layer1_sum")
        at = sb("at", [P, EL // 2, TPG], U32)
        vin = sb("vin", [P, EL, TPG, VROW], F32)
        hot = sb("hot", [P, EL, TPG, P], F32)
        rhs = sb("rhs", [P, EL, TPG, D + HEADS + 1], F32)
        ps = [psum(f"ps{b}", [P, 512]) for b in range(BANKS)]
        s = sems("acc_zero turn")
        at_set, hot_made, weighed, scaled_first, scaled_second, scaled_rest, summed, kept, loaded = slot_sems(
            "at_set hot_made weighed scaled_first scaled_second scaled_rest summed kept loaded")
        val_in = [t.val_in[b // 2] if b % 2 == 0 else loaded[b] for b in range(EL)]
        GATHERS_AHEAD = 4
        val_count = [16 * TPG if b % 2 == 0 else 16 for b in range(EL)]

        def by_weights(eng, b, q, h0, h1):
            return eng.tensor_tensor(rhs[:, b, q, h0 * HD:h1 * HD].rearrange("p (h f) -> p h f", h=h1 - h0),
                                     vin[:, b, q, h0 * HD:h1 * HD].rearrange("p (h f) -> p h f", h=h1 - h0),
                                     rhs[:, b, q, D + h0:D + h1].unsqueeze(2).broadcast_to([P, h1 - h0, HD]), ALU.mult)

        with nc.Block() as block:
            @block.sync
            def _(sp):
                def turn(r):
                    for b in range(1, EL, 2):
                        sp.wait_ge(scaled_first[b], r)
                        sp.wait_ge(scaled_second[b], r)
                        sp.wait_ge(scaled_rest[b], r)
                        sp.dma_start(vin[:, b, :, :], t.slot_val_dram[bass.ds((EL * r + b) * GE, GE), :]
                                     .rearrange("(q p) c -> p q c", p=P)).then_inc(loaded[b], 16)
                rounds(sp, NG // EL, turn)

            @block.gpsimd
            def _(pool):
                pool.memset(t.acc[:, :, :], 0.0).then_inc(s.acc_zero, 1)

                def gather(r, b):
                    pool.wait_ge(at_set[b], r + 1)
                    pool.wait_ge(scaled_first[b], r)
                    pool.wait_ge(scaled_second[b], r)
                    pool.sem_inc(s.turn, 1)
                    for q in range(TPG):
                        pool.indirect_dma_start(vin[:, b, q, :], None, t.val_dram,
                                                bass.IndirectOffsetOnAxis(ap=at[:, b // 2, q:q + 1], axis=0)).then_inc(val_in[b], 16)

                def scale(r, b):
                    pool.wait_ge(weighed[b], r + 1)
                    by_weights(nc.gpsimd, b, 1, HEADS // 2, HEADS).then_inc(scaled_rest[b], 1)

                def turn(r, last):
                    for b in range(0, EL, 2):
                        if b + GATHERS_AHEAD < EL:
                            gather(r, b + GATHERS_AHEAD)
                        elif not last:
                            gather(r + 1, b + GATHERS_AHEAD - EL)
                        scale(r, b + 1)
                for b in range(0, GATHERS_AHEAD, 2):
                    gather(0, b)
                turn(0, False)
                with pool.Fori(1, NG // EL - 1) as r:
                    turn(r, False)
                turn(NG // EL - 1, True)

            @block.scalar
            def _(act):
                def weights(r, b):
                    act.wait_ge(val_in[b], val_count[b] * (r + 1))
                    act.wait_ge(summed[b], r)
                    nc.scalar.activation(rhs[:, b, :, D:D + HEADS], t.score[:, bass.ds((EL * r + b) * TPG, TPG), :], ACT.Copy)
                    nc.scalar.activation(rhs[:, b, :, D + HEADS], vin[:, b, :, D], ACT.Copy).then_inc(weighed[b], 1)

                def scale(r, b):
                    act.wait_ge(weighed[b], r + 1)
                    for h in range(HEADS):
                        last = nc.scalar.activation(rhs[:, b, 0, h * HD:(h + 1) * HD], vin[:, b, 0, h * HD:(h + 1) * HD], ACT.Copy,
                                                    scale=rhs[:, b, 0, D + h:D + h + 1])
                    last.then_inc(scaled_first[b], 1)
                with_ahead(act, EL, 1, weights, scale)

            @block.tensor
            def _(pe):
                def turn(r):
                    for b in range(EL):
                        pe.wait_ge(hot_made[b], r + 1)
                        pe.wait_ge(scaled_first[b], r + 1)
                        pe.wait_ge(scaled_second[b], r + 1)
                        if b % 2 == 1:
                            pe.wait_ge(scaled_rest[b], r + 1)
                        pe.wait_ge(kept[(b - BANKS) % EL], r + (b >= BANKS))
                        for q in range(TPG):
                            last = nc.tensor.matmul(ps[b % BANKS][:, 0:D + HEADS + 1], hot[:, b, q, :], rhs[:, b, q, :],
                                                    start=q == 0, stop=q == TPG - 1)
                        last.then_inc(summed[b], 1)
                rounds(pe, NG // EL, turn)

            @block.vector
            def _(dve):
                dve.wait_ge(s.acc_zero, 1)

                def addresses(r, b):
                    dve.wait_ge(val_in[b], 16 * TPG * r)
                    nc.vector.tensor_scalar(at[:, b // 2, :], t.edge[:, bass.ds((EL * r + b) * TPG, TPG), 1], float(NPAD - 1), None,
                                            ALU.min).then_inc(at_set[b], 1)

                def one_hots(r, b):
                    dve.wait_ge(summed[b], r)
                    for q in range(TPG):
                        last = nc.vector.tensor_scalar(hot[:, b, q, :], t.cols[:, :], t.local[:, bass.ds((EL * r + b) * TPG + q, 1)], None,
                                                       ALU.is_equal)
                    last.then_inc(hot_made[b], 1)

                def scale(r, b):
                    dve.wait_ge(weighed[b], r + 1)
                    by_weights(nc.vector, b, 1, 0, HEADS if b % 2 == 0 else HEADS // 2).then_inc(scaled_second[b], 1)

                def prepare_group(r, b):
                    one_hots(r, b)
                    scale(r, b)

                pair = []

                def add_group(r, b):
                    if b % 2 == 0:
                        pair[:] = [dve.value_load(t.dst_pair[0:1, bass.ds(EL // 2 * r + b // 2, 1)], min_val=0, max_val=NW * NW - 1)]
                    win = pair[0] // NW if b % 2 == 0 else pair[0] % NW
                    sums = t.acc[:, bass.ds(win, 1), 0:D + HEADS + 1].rearrange("p a f -> p (a f)")
                    dve.wait_ge(summed[b], r + 1)
                    dve.wait_ge(kept[(b - 1) % EL], r + (b > 0))
                    nc.vector.tensor_tensor(sums, sums, ps[b % BANKS][:, 0:D + HEADS + 1], ALU.add).then_inc(kept[b], 1)

                def turn(r, last):
                    for b in range(EL):
                        if b < EL - 2:
                            prepare_group(r, b + 2)
                        elif not last:
                            prepare_group(r + 1, b + 2 - EL)
                        if b % 2 == 0 and not last:
                            addresses(r + 1, b)
                        add_group(r, b)

                for b in range(0, EL, 2):
                    addresses(0, b)
                prepare_group(0, 0)
                prepare_group(0, 1)
                turn(0, False)
                with dve.Fori(1, NG // EL - 1) as r:
                    turn(r, False)
                turn(NG // EL - 1, True)


def layer1_nodes(nc, i, t):
    with ExitStack() as ctx:
        sb, psum, sems, slot_sems = allocators(nc, ctx, "layer1_nodes")
        wo = sb("wo", [P, 2, D], F32)
        bo = sb("bo", [1, D], F32)
        gamma = sb("gamma", [P, D], F32)
        beta = sb("beta", [P, D], F32)
        alone = sb("alone", [P, NW, HEADS], F32)
        den = sb("den", [P, NW, HEADS], F32)
        msg = sb("msg", [P, CW, D], F32)
        own = sb("own", [P, CW, D], F32)
        msg_t = sb("msg_t", [P, 2, CW * P], F32)
        shifted = sb("shifted", [P, NW, D], F32)
        v = sb("v", [P, CW, D], F32)
        result = sb("result", [P, CW, D], F32)
        stats = sb("stats", [P, CW, 6], F32)
        mean_var = sb("mean_var", [P, CW, 2], F32)
        var_eps = sb("var_eps", [P, CW], F32)
        rstd = sb("rstd", [P, CW], F32)
        inverse = sb("inverse", [P, NW], F32)
        fine = sb("fine", [P, NW], F32)
        ps_x = [psum(f"ps_x{b}", [P, 512]) for b in range(3)]
        ps_o = [psum(f"ps_o{b}", [P, 512]) for b in range(CW)]
        s = sems("w_in d p carried msg_made shifted_made combined turned msg_t_made projected added var_made rooted normed out_done")
        with nc.Block() as block:
            @block.sync
            def _(sp):
                sp.dma_start(wo[:, :, :], i.L1_gnn_Wo.rearrange("(k p) m -> p k m", p=P)).then_inc(s.w_in, 16)
                sp.dma_start(bo[:, :], i.L1_gnn_bo.rearrange("(a m) -> a m", a=1)).then_inc(s.w_in, 16)
                sp.dma_start(gamma[:, :], i.L1_gnn_gamma.partition_broadcast(P)).then_inc(s.w_in, 16)
                sp.dma_start(beta[:, :], i.L1_gnn_beta.partition_broadcast(P)).then_inc(s.w_in, 16)
                def turn(c):
                    sp.wait_ge(s.normed, (c + 1) * CW)
                    sp.dma_start(i.out[bass.ds(c * CW * P, CW * P), :].rearrange("(w p) m -> p w m", p=P), result[:, :, :]).then_inc(s.out_done, 16)
                rounds(sp, CH - 1, turn)
                first = (CH - 1) * CW * P
                sp.wait_ge(s.normed, CH * CW)
                sp.dma_start(i.out[first:(NW - 1) * P, :].rearrange("(w p) m -> p w m", p=P), result[:, 0:CW - 1, :]).then_inc(s.out_done, 16)
                sp.dma_start(i.out[(NW - 1) * P:N, :], result[0:TAIL_NODES, CW - 1, :]).then_inc(s.out_done, 16)
                sp.wait_ge(s.out_done, 16 * (CH + 1))

            @block.tensor
            def _(pe):
                pe.wait_ge(s.w_in, 16 * 4)
                def turn(c):
                    for w in range(CW):
                        pe.wait_ge(s.msg_made, c * CW + w + 1)
                        if w < 3:
                            pe.wait_ge(s.msg_t_made, c * CW)
                        else:
                            pe.wait_ge(s.msg_t_made, c * CW + w - 2)
                        for half in range(2):
                            last = nc.tensor.transpose(ps_x[w % 3][:, half * P:(half + 1) * P], msg[:, w, half * P:(half + 1) * P], t.ident[:, :])
                        last.then_inc(s.turned, 1)
                    for w in range(CW):
                        pe.wait_ge(s.msg_t_made, c * CW + w + 1)
                        pe.wait_ge(s.added, c * CW)
                        for k in range(2):
                            nc.tensor.matmul(ps_o[w][:, 0:D], msg_t[:, k, w * P:(w + 1) * P], wo[:, k, :], start=k == 0, stop=False)
                        nc.tensor.matmul(ps_o[w][:, 0:D], t.ones[0:1, 0:P], bo[0:1, :], start=False, stop=True).then_inc(s.projected, 1)
                rounds(pe, CH, turn)

            @block.scalar
            def _(act):
                def turned_kept(c):
                    for w in range(CW):
                        act.wait_ge(s.turned, c * CW + w + 1)
                        nc.scalar.activation(msg_t[:, :, w * P:(w + 1) * P], ps_x[w % 3][:, 0:2 * P].rearrange("p (k n) -> p k n", k=2),
                                             ACT.Copy).then_inc(s.msg_t_made, 1)

                def root(c, norm):
                    act.wait_ge(s.var_made, c * 2 + norm + 1)
                    nc.scalar.activation(rstd[:, :], var_eps[:, :], ACT.Sqrt).then_inc(s.rooted, 1)

                turned_kept(0)
                turned_kept(1)
                root(0, 0)
                root(0, 1)
                with act.Fori(1, CH - 1) as c:
                    turned_kept(c + 1)
                    root(c, 0)
                    root(c, 1)
                root(CH - 1, 0)
                root(CH - 1, 1)

            @block.gpsimd
            def _(pool):
                pool.wait_ge(s.d, 7)
                PSTEPS = 2 * CW

                def turn(c):
                    n = c * PSTEPS
                    tt = nc.gpsimd.tensor_tensor
                    heads = lambda a: a.rearrange("p a (h f) -> p (a h) f", h=HEADS)
                    pool.wait_ge(s.turned, c * CW)
                    for w in range(CW):
                        by_head = lambda a: a[:, w, :].rearrange("p (h f) -> p h f", h=HEADS)
                        over = lambda a: a[:, bass.ds(c * CW + w, 1), :].rearrange("p a h -> p (a h)").unsqueeze(2).broadcast_to([P, HEADS, HD])
                        tt(by_head(msg), heads(t.acc[:, bass.ds(c * CW + w, 1), 0:D]), over(den), ALU.mult).then_inc(s.p, 1)
                        tt(by_head(own), heads(t.val[:, bass.ds(c * CW + w, 1), 0:D]), over(alone), ALU.mult).then_inc(s.p, 1)
                        pool.wait_ge(s.p, n + 2 * (w + 1))
                        tt(msg[:, w, :], msg[:, w, :], own[:, w, :], ALU.add).then_inc(s.msg_made, 1)
                    pool.wait_ge(s.w_in, 16 * 4)
                    tt(shifted[:, bass.ds(c * CW, CW), :], t.x[:, bass.ds(c * CW, CW), :], beta[:, :].unsqueeze(1).broadcast_to([P, CW, D]), ALU.add).then_inc(s.shifted_made, 1)
                rounds(pool, CH, turn)

            @block.vector
            def _(dve):
                tt, ts, stt = nc.vector.tensor_tensor, nc.vector.tensor_scalar, nc.vector.scalar_tensor_tensor
                weights = t.acc[:, :, D:D + HEADS]
                ts(alone[:, :, :], weights, 0.0, None, ALU.is_equal).then_inc(s.d, 1)
                tt(fine[:, :], t.acc[:, :, D + HEADS], t.val[:, :, D], ALU.add).then_inc(s.d, 1)
                dve.wait_ge(s.d, 2)
                tt(den[:, :, :], weights, alone[:, :, :], ALU.add).then_inc(s.d, 1)
                ts(fine[:, :], fine[:, :], 0.0, None, ALU.is_equal).then_inc(s.d, 1)
                dve.wait_ge(s.d, 4)
                nc.vector.reciprocal(den[:, :, :], den[:, :, :]).then_inc(s.d, 1)
                nc.vector.reciprocal(inverse[:, :], fine[:, :]).then_inc(s.d, 1)
                dve.wait_ge(s.d, 6)
                tt(fine[:, :], fine[:, :], inverse[:, :], ALU.mult).then_inc(s.d, 1)
                dve.wait_ge(s.d, 7)
                FIRST_STEPS = 7
                DSTEPS = 2 * MOMENT_STEPS + CW + 3
                dve.wait_ge(s.w_in, 16 * 4)

                def turn(c):
                    n = c * DSTEPS + FIRST_STEPS
                    dve.wait_ge(s.normed, c * CW)
                    for w in range(CW):
                        dve.wait_ge(s.projected, c * CW + w + 1)
                        tt(v[:, w, :], ps_o[w][:, 0:D], t.x[:, bass.ds(c * CW + w, 1), :].rearrange("p a m -> p (a m)"), ALU.add).then_inc(s.added, 1)
                    dve.wait_ge(s.added, (c + 1) * CW)
                    moments(nc, dve, s.d, n, s.carried, v, stats, mean_var, var_eps, s.var_made)
                    n += MOMENT_STEPS
                    for w in range(CW):
                        stt(v[:, w, :], v[:, w, :], mean_var[:, w, 0:1], gamma[:, :], ALU.subtract, ALU.mult).then_inc(s.d, 1)
                    dve.wait_ge(s.rooted, c * 2 + 1)
                    nc.vector.reciprocal(rstd[:, :], rstd[:, :]).then_inc(s.d, 1)
                    dve.wait_ge(s.d, n + CW + 1)
                    tt(rstd[:, :], rstd[:, :], fine[:, bass.ds(c * CW, CW)], ALU.mult).then_inc(s.d, 1)
                    dve.wait_ge(s.d, n + CW + 2)
                    dve.wait_ge(s.shifted_made, c + 1)
                    for w in range(CW):
                        stt(v[:, w, :], v[:, w, :], rstd[:, w:w + 1], shifted[:, bass.ds(c * CW + w, 1), :].rearrange("p a m -> p (a m)"), ALU.mult, ALU.add).then_inc(s.combined, 1)
                    dve.wait_ge(s.combined, (c + 1) * CW)
                    moments(nc, dve, s.d, n + CW + 2, s.carried, v, stats, mean_var, var_eps, s.var_made)
                    n += CW + 2 + MOMENT_STEPS
                    dve.wait_ge(s.rooted, c * 2 + 2)
                    nc.vector.reciprocal(rstd[:, :], rstd[:, :]).then_inc(s.d, 1)
                    dve.wait_ge(s.d, n + 1)
                    dve.wait_ge(s.out_done, 16 * c)
                    for w in range(CW):
                        ts(result[:, w, :], v[:, w, :], mean_var[:, w, 0:1], rstd[:, w:w + 1], ALU.subtract, ALU.mult).then_inc(s.normed, 1)
                rounds(dve, CH, turn)


def build(nc, i):
    with ExitStack() as ctx:
        t = named()
        ring = lambda name, slots: [ctx.enter_context(nc.semaphore(f"{name}_{b}")) for b in range(slots)]
        t.row_out, t.key_in, t.val_in = ring("row_out", EL), ring("key_in", EL), ring("val_in", EL // 2)
        sb = allocators(nc, ctx, "all")[0]
        t.x = sb("x", [P, NW, D], F32)
        t.table3 = sb("table3", [P, NW, 3 * ROWW], BF16)
        t.ident = sb("ident", [P, P], F32)
        t.lane = sb("lane", [P, 1], F32)
        t.trash = sb("trash", [P, 1], F32)
        t.cols = sb("cols", [P, P], F32)
        t.win_of_col = sb("win_of_col", [P, NW * HEADS], F32)
        t.ones = sb("ones", [P, P], F32)
        t.elem_w = sb("elem_w", [P, HEADS], F32)
        t.fill_at = sb("fill_at", [P, 2 * NW], I32)
        t.src_pair = sb("src_pair", [P, NG // 2], I32)
        t.dst_pair = sb("dst_pair", [P, NG // 2], I32)
        t.dst_win = sb("dst_win", [P, NG], I32)
        t.first_edge = sb("first_edge", [P, NG], I32)
        t.win_base = sb("win_base", [P, NG], F32)
        t.win_lane = sb("win_lane", [P, NG], F32)

        def dram(name, shape, dt):
            return nc.dram_tensor(name, shape, dt, kind="Internal").ap()

        t.rec_dram = dram("edge_records", [EPAD + GE, 8], F32)
        t.row_dram = dram("edge_rows16", [3, EPAD + GE], I16)
        t.rows_dram = dram("rows_by_src", [SCRAP + 2 * NW * GE, ROWW], F32)
        t.key_dram = dram("keys", [NPAD, D], F32)
        t.val_dram = dram("values", [NPAD, VROW], F32)
        t.both_dram = dram("keys_and_values", [NPAD, D + VROW], F32)
        t.slot_val_dram = dram("values_by_slot", [NROWS, VROW], F32)
        tiles = -(-NT // (P // HEADS)) * P
        t.edge_dram = dram("tile_ends", [tiles * 4], F32)
        t.carry_dram = dram("tile_carries", [tiles * 2], F32)

        prepare(nc, i, t)
        t.edge = sb("edge", [P, NT, 8], F32)
        t.local = sb("local", [P, NT], F32)
        t.valid = sb("valid", [P, NT], F32)
        t.score = sb("score", [P, NT, HEADS], F32)
        t.acc = sb("acc", [P, NW, ROWW], F32)
        layer0_edges(nc, i, t)
        layer0_sum(nc, i, t)
        t.val = sb("val", [P, NW, VROW], F32)
        layer0_nodes(nc, i, t)
        layer1_scores(nc, i, t)
        segment_max(nc, i, t)
        layer1_sum(nc, i, t)
        layer1_nodes(nc, i, t)


INPUTS = ["x", "src", "dst", "edge_type_64", "edge_weight", "L0_gnn_W1", "L0_gnn_b1", "L0_gnn_W2", "L0_gnn_b2",
          "L0_gnn_attn_w", "L0_gnn_attn_b", "L1_gnn_query_emb", "L1_gnn_Wq", "L1_gnn_bq", "L1_gnn_Wk", "L1_gnn_bk",
          "L1_gnn_Wv", "L1_gnn_bv", "L1_gnn_rel_w", "L1_gnn_Wo", "L1_gnn_bo", "L1_gnn_gamma", "L1_gnn_beta"]


def kernel(**inputs):
    import numpy as np
    from concourse import bacc
    from concourse.bass_utils import run_bass_kernel_spmd

    nc = bacc.Bacc("TRN2", target_bir_lowering=False, num_devices=1)
    arrays, args = {}, {}
    for name in INPUTS:
        a = np.ascontiguousarray(inputs[name])
        arrays[f"in_{name}"] = a
        args[name] = nc.dram_tensor(f"in_{name}", a.shape, mybir.dt.from_np(a.dtype), kind="ExternalInput").ap()
    args["out"] = nc.dram_tensor("out_0", (N, D), F32, kind="ExternalOutput").ap()
    build(nc, named(**args))
    result = run_bass_kernel_spmd(nc, [arrays], core_ids=[0])
    return result.results[0]["out_0"]
```
